# Optimizing a Trainium2 kernel written in Bass

```python
import numpy as np
import jax
import jax.numpy as jnp

def _softmax(x, axis=-1):
    return jax.nn.softmax(x, axis=axis)

def _gelu(x):
    return jax.nn.gelu(x, approximate=True)

def _silu(x):
    return jax.nn.silu(x)

def _sigmoid(x):
    return jax.nn.sigmoid(x)

def _layernorm(x, axis=-1, eps=1e-05):
    m = jnp.mean(x, axis=axis, keepdims=True)
    v = jnp.var(x, axis=axis, keepdims=True)
    return (x - m) / jnp.sqrt(v + eps)

def _scatter_add(tgt, idx, src, axis=0):
    return tgt.at[idx].add(src)

def _segment_sum(src, seg, n):
    return jax.ops.segment_sum(src, seg, n)
kernel_name = 'mk_flamingo_gated_d4_seqx_r8_4550b6'

def setup_inputs(seed: int=0):
    np.random.seed(seed)
    _w = jnp.asarray

    def _rec_inputs():
        import jax
        import jax.numpy as jnp
        _rk = jax.random.key(seed)
        x = 7.22e-05 + 1 * jax.random.normal(jax.random.fold_in(_rk, 1), (64, 64, 128), jnp.float32)
        _lenS = 64 - jax.random.randint(jax.random.fold_in(_rk, 7), (64,), 0, max(1, 64 // 4) + 1, jnp.int32)
        _lenS2 = 64 - jax.random.randint(jax.random.fold_in(_rk, 8), (64,), 0, max(1, 64 // 4) + 1, jnp.int32)
        _ctx_1024P = jax.random.normal(jax.random.fold_in(_rk, 11), (64, 16, 128), jnp.float32)
        _ctx_1024c = jax.random.dirichlet(jax.random.fold_in(_rk, 511), 0.3 * jnp.ones((16,), jnp.float32), (64, 64))
        _ctx_1024t = jnp.einsum('bsk,bkd->bsd', _ctx_1024c, _ctx_1024P)
        _ctx_1024t = _ctx_1024t * jax.lax.rsqrt(jnp.mean(jnp.square(_ctx_1024t)) + 1e-12) * 0.953939
        ctx_1024 = 4.13588e-05 + 0.999923 * (_ctx_1024t + 0.3 * jax.random.normal(jax.random.fold_in(_rk, 611), (64, 64, 128), jnp.float32))
        fside_Bx16xSxS2_0 = 9.80324e-06 + 0.100009 * jax.random.normal(jax.random.fold_in(_rk, 13), (64, 16, 64, 64), jnp.float32)
        fside_SxS2_0 = -2.64403e-05 + 0.100002 * jax.random.normal(jax.random.fold_in(_rk, 15), (64, 64), jnp.float32)
        _validS = jnp.arange(64)[None, :] < _lenS[:, None]
        _validS2 = jnp.arange(64)[None, :] < _lenS2[:, None]
        _causal = jnp.tril(jnp.ones((64, 64), dtype=bool))
        mask_Bx1xSxS2_ik1 = jnp.where(jnp.broadcast_to(_validS2[:, None, None, :], (64, 1, 64, 64)), 1, 0).astype(jnp.int32)
        mask_BxS2_bf0 = jnp.logical_not(jnp.ones((64, 64), dtype=bool))
        _g = jax.random.normal(jax.random.fold_in(_rk, 9001), (2, 4), jnp.float32)
        _g = jnp.sign(_g) * jnp.maximum(jnp.abs(_g), 1.0) + (_g == 0) * 1.0
        g_xattn = _g[0]
        g_ffn = _g[1]
        return (x, ctx_1024, fside_Bx16xSxS2_0, fside_SxS2_0, mask_Bx1xSxS2_ik1, mask_BxS2_bf0, g_xattn, g_ffn)
    x, ctx_1024, fside_Bx16xSxS2_0, fside_SxS2_0, mask_Bx1xSxS2_ik1, mask_BxS2_bf0, g_xattn, g_ffn = _rec_inputs()

    def _L0_xattn_setup():
        import jax, jax.numpy as jnp
        import numpy as np
        D_MODEL = 128
        N_HEAD = 16
        B, S = (4, 256)

        def _split_heads(x):
            b, l, d = x.shape
            return x.reshape(b, l, N_HEAD, d // N_HEAD).transpose(0, 2, 1, 3)
        key = jax.random.key(seed)
        ks = jax.random.split(key, 13)
        s = 1.0 / np.sqrt(D_MODEL)
        inp = {'query': jax.random.normal(ks[0], (B, S, D_MODEL), jnp.float32), 'key_': jax.random.normal(ks[1], (B, S, D_MODEL), jnp.float32), 'value': jax.random.normal(ks[2], (B, S, D_MODEL), jnp.float32), 'mask': jax.random.randint(ks[3], (B, 1, S, S), 0, 2, jnp.int32), 'Wq': jax.random.normal(ks[4], (D_MODEL, D_MODEL), jnp.float32) * s, 'bq': jax.random.normal(ks[5], (D_MODEL,), jnp.float32) * 0.02, 'Wk': jax.random.normal(ks[6], (D_MODEL, D_MODEL), jnp.float32) * s, 'bk': jax.random.normal(ks[7], (D_MODEL,), jnp.float32) * 0.02, 'Wv': jax.random.normal(ks[8], (D_MODEL, D_MODEL), jnp.float32) * s, 'bv': jax.random.normal(ks[9], (D_MODEL,), jnp.float32) * 0.02, 'Wo': jax.random.normal(ks[10], (D_MODEL, D_MODEL), jnp.float32) * s, 'bo': jax.random.normal(ks[11], (D_MODEL,), jnp.float32) * 0.02}
        return inp
    _L0_xattn_all = _L0_xattn_setup()
    _L0_xattn_in = {k: v for k, v in _L0_xattn_all.items() if k in ('Wq', 'bq', 'Wk', 'bk', 'Wv', 'bv', 'Wo', 'bo')}
    del _L0_xattn_all

    def _L0_ffn_setup():
        import jax, jax.numpy as jnp
        import numpy as np
        key = jax.random.key(seed)
        k1, k2, k3, k4 = jax.random.split(key, 4)
        B, T, M = (4, 256, 128)
        E, F = (16, 512)
        x = jax.random.normal(k1, (B, T, M), dtype=jnp.float32) * 0.02
        Wg = jax.random.normal(k2, (M, E), dtype=jnp.float32) * 0.02
        w1 = jax.random.normal(k3, (E, M, F), dtype=jnp.float32) * 0.02
        w2 = jax.random.normal(k4, (E, F, M), dtype=jnp.float32) * 0.02
        return {'x': x, 'Wg': Wg, 'w1': w1, 'w2': w2}
    _L0_ffn_all = _L0_ffn_setup()
    _L0_ffn_in = {k: v for k, v in _L0_ffn_all.items() if k in ('Wg', 'w1', 'w2')}
    del _L0_ffn_all

    def _L1_xattn_setup():
        import jax, jax.numpy as jnp
        import numpy as np
        E = 128
        H = 16
        D = E // H
        key = jax.random.key(seed)
        ks = jax.random.split(key, 12)
        B, T, S = (2, 256, 256)
        inp = {'query': jax.random.normal(ks[0], (B, T, E), jnp.float32), 'key': jax.random.normal(ks[1], (B, S, E), jnp.float32), 'value': jax.random.normal(ks[2], (B, S, E), jnp.float32), 'spatial_bias': jax.random.normal(ks[3], (B, H, T, S), jnp.float32) * 0.1, 'directional_bias': jax.random.normal(ks[4], (B, H, T, S), jnp.float32) * 0.1, 'key_padding_mask': jnp.zeros((B, S), dtype=bool), 'attn_mask': jax.random.normal(ks[5], (T, S), jnp.float32) * 0.1, 'Wq': jax.random.normal(ks[6], (E, E), jnp.float32) / np.sqrt(E), 'bq': jnp.zeros((E,), jnp.float32), 'Wk': jax.random.normal(ks[7], (E, E), jnp.float32) / np.sqrt(E), 'bk': jnp.zeros((E,), jnp.float32), 'Wv': jax.random.normal(ks[8], (E, E), jnp.float32) / np.sqrt(E), 'bv': jnp.zeros((E,), jnp.float32), 'Wo': jax.random.normal(ks[9], (E, E), jnp.float32) / np.sqrt(E), 'bo': jnp.zeros((E,), jnp.float32)}
        return inp
    _L1_xattn_all = _L1_xattn_setup()
    _L1_xattn_in = {k: v for k, v in _L1_xattn_all.items() if k in ('Wq', 'bq', 'Wk', 'bk', 'Wv', 'bv', 'Wo', 'bo')}
    del _L1_xattn_all

    def _L1_ffn_setup():
        import jax, jax.numpy as jnp
        import numpy as np
        EPS = 1e-06
        LN_EPS = 1e-05

        def _absmean_core(W):
            gamma = jnp.mean(jnp.abs(W)) + EPS
            Ws = W / gamma
            Wq = jnp.sign(Ws) * jnp.minimum(jnp.round(jnp.abs(Ws)), 1.0)
            return (Wq, gamma)

        @jax.custom_vjp
        def absmean(W):
            return _absmean_core(W)[0]

        def _absmean_fwd(W):
            Wq, gamma = _absmean_core(W)
            return (Wq, gamma)

        def _absmean_bwd(gamma, g):
            return (g / gamma,)
        absmean.defvjp(_absmean_fwd, _absmean_bwd)

        def layernorm(x, w, b, eps=LN_EPS):
            mu = jnp.mean(x, axis=-1, keepdims=True)
            var = jnp.mean((x - mu) ** 2, axis=-1, keepdims=True)
            return (x - mu) * jax.lax.rsqrt(var + eps) * w + b
        key = jax.random.key(seed)
        k1, k2, k3 = jax.random.split(key, 3)
        d, h = (128, 512)
        B, T = (8, 256)
        return {'x': jax.random.normal(k1, (B, T, d), jnp.float32), 'W_fc': jax.random.normal(k2, (h, d), jnp.float32), 'ln_w': jnp.ones((h,), jnp.float32), 'ln_b': jnp.zeros((h,), jnp.float32), 'W_proj': jax.random.normal(k3, (d, h), jnp.float32)}
    _L1_ffn_all = _L1_ffn_setup()
    _L1_ffn_in = {k: v for k, v in _L1_ffn_all.items() if k in ('W_fc', 'ln_w', 'ln_b', 'W_proj')}
    del _L1_ffn_all

    def _L2_xattn_setup():
        import jax, jax.numpy as jnp
        import numpy as np
        B, LX, LY, D = (32, 128, 128, 128)
        key = jax.random.key(seed)
        k1, k2, k3, k4 = jax.random.split(key, 4)
        x = jax.random.normal(k1, (B, LX, D), dtype=jnp.float32)
        y = jax.random.normal(k2, (B, LY, D), dtype=jnp.float32)
        y_mask = jnp.zeros((B, LY), dtype=bool)
        W = jax.random.normal(k3, (D, D), dtype=jnp.float32) * (1.0 / np.sqrt(D))
        b = jax.random.normal(k4, (D,), dtype=jnp.float32) * 0.01
        return {'x': x, 'y': y, 'y_mask': y_mask, 'W': W, 'b': b}
    _L2_xattn_all = _L2_xattn_setup()
    _L2_xattn_in = {k: v for k, v in _L2_xattn_all.items() if k in ('W', 'b')}
    del _L2_xattn_all

    def _L2_ffn_setup():
        import jax, jax.numpy as jnp
        import numpy as np
        TOP_K = 2
        TEMP = 0.9
        EPS = 1e-05
        B, S, D, F, E = (2, 256, 128, 512, 8)

        def _moe_forward(x, gate_w, gate_b, w1, b1, w2, b2, ln_g, ln_b):
            logits = (x @ gate_w + gate_b) / TEMP
            topk_vals, topk_idx = jax.lax.top_k(logits, TOP_K)
            keep = jax.nn.one_hot(topk_idx, E, dtype=jnp.bool_).any(-2)
            masked = jnp.where(keep, logits, -jnp.inf)
            gate_probs = jax.nn.softmax(masked, axis=-1)
            h = jnp.einsum('bsd,edf->bsef', x, w1) + b1
            h = jax.nn.gelu(h, approximate=False)
            expert_out = jnp.einsum('bsef,efd->bsed', h, w2) + b2
            out = jnp.einsum('bse,bsed->bsd', gate_probs, expert_out)
            mu = out.mean(-1, keepdims=True)
            var = out.var(-1, keepdims=True)
            out = (out - mu) / jnp.sqrt(var + EPS) * ln_g + ln_b
            return out
        key = jax.random.key(seed)
        ks = jax.random.split(key, 4)
        scale_in = 1.0 / np.sqrt(D)
        scale_ff = 1.0 / np.sqrt(F)
        return {'x': jax.random.normal(ks[0], (B, S, D), jnp.float32), 'gate_w': jax.random.normal(ks[1], (D, E), jnp.float32) * scale_in, 'gate_b': jnp.zeros((E,), jnp.float32), 'w1': jax.random.normal(ks[2], (E, D, F), jnp.float32) * scale_in, 'b1': jnp.zeros((E, F), jnp.float32), 'w2': jax.random.normal(ks[3], (E, F, D), jnp.float32) * scale_ff, 'b2': jnp.zeros((E, D), jnp.float32), 'ln_g': jnp.ones((D,), jnp.float32), 'ln_b': jnp.zeros((D,), jnp.float32)}
    _L2_ffn_all = _L2_ffn_setup()
    _L2_ffn_in = {k: v for k, v in _L2_ffn_all.items() if k in ('gate_w', 'gate_b', 'w1', 'b1', 'w2', 'b2', 'ln_g', 'ln_b')}
    del _L2_ffn_all

    def _L3_xattn_setup():
        import jax, jax.numpy as jnp
        import numpy as np
        HEADS = 8
        DIM_HEAD = 64
        SCALE = 8.0
        EPS = 1e-05

        def layer_norm(x, g, b):
            mu = jnp.mean(x, axis=-1, keepdims=True)
            var = jnp.mean((x - mu) ** 2, axis=-1, keepdims=True)
            return (x - mu) * jax.lax.rsqrt(var + EPS) * g + b
        key = jax.random.key(seed)
        ks = jax.random.split(key, 6)
        b, n, dim = (4, 512, 128)
        inner = HEADS * DIM_HEAD
        return {'x': jax.random.normal(ks[0], (b, n, dim), jnp.float32), 'context': jax.random.normal(ks[1], (b, n, dim), jnp.float32), 'Wq': jax.random.normal(ks[2], (dim, inner), jnp.float32) * 0.03, 'Wkv': jax.random.normal(ks[3], (dim, 2 * inner), jnp.float32) * 0.03, 'null_kv': jax.random.normal(ks[4], (2, DIM_HEAD), jnp.float32), 'ln_q_g': jnp.ones((inner,), jnp.float32), 'ln_q_b': jnp.zeros((inner,), jnp.float32), 'ln_out_g': jnp.ones((inner,), jnp.float32), 'ln_out_b': jnp.zeros((inner,), jnp.float32), 'Wout': jax.random.normal(ks[5], (inner, dim), jnp.float32) * 0.03}
    _L3_xattn_all = _L3_xattn_setup()
    _L3_xattn_in = {k: v for k, v in _L3_xattn_all.items() if k in ('Wq', 'Wkv', 'null_kv', 'ln_q_g', 'ln_q_b', 'ln_out_g', 'ln_out_b', 'Wout')}
    del _L3_xattn_all

    def _L3_ffn_setup():
        import math
        import jax, jax.numpy as jnp
        import numpy as np
        TOP_K = 2
        CAP_FACTOR = 1.25
        CLAMP = 10000.0
        key = jax.random.key(seed)
        k1, k2, k3, k4, k5 = jax.random.split(key, 5)
        B, S, D, F, E = (4, 256, 128, 512, 8)
        std = 0.02
        return {'x': jax.random.normal(k1, (B, S, D), dtype=jnp.float32), 'Wr': jax.random.normal(k2, (D, E), dtype=jnp.float32) * std, 'W1': jax.random.normal(k3, (E, D, F), dtype=jnp.float32) * std, 'W3': jax.random.normal(k4, (E, D, F), dtype=jnp.float32) * std, 'W2': jax.random.normal(k5, (E, F, D), dtype=jnp.float32) * std}
    _L3_ffn_all = _L3_ffn_setup()
    _L3_ffn_in = {k: v for k, v in _L3_ffn_all.items() if k in ('Wr', 'W1', 'W3', 'W2')}
    del _L3_ffn_all
    return {'x': x, 'ctx_1024': ctx_1024, 'fside_Bx16xSxS2_0': fside_Bx16xSxS2_0, 'fside_SxS2_0': fside_SxS2_0, 'mask_Bx1xSxS2_ik1': mask_Bx1xSxS2_ik1, 'mask_BxS2_bf0': mask_BxS2_bf0, 'g_xattn': g_xattn, 'g_ffn': g_ffn, 'L0_xattn_Wq': _L0_xattn_in['Wq'], 'L0_xattn_bq': _L0_xattn_in['bq'], 'L0_xattn_Wk': _L0_xattn_in['Wk'], 'L0_xattn_bk': _L0_xattn_in['bk'], 'L0_xattn_Wv': _L0_xattn_in['Wv'], 'L0_xattn_bv': _L0_xattn_in['bv'], 'L0_xattn_Wo': _L0_xattn_in['Wo'], 'L0_xattn_bo': _L0_xattn_in['bo'], 'L0_ffn_Wg': _L0_ffn_in['Wg'], 'L0_ffn_w1': _L0_ffn_in['w1'], 'L0_ffn_w2': _L0_ffn_in['w2'], 'L1_xattn_Wq': _L1_xattn_in['Wq'], 'L1_xattn_bq': _L1_xattn_in['bq'], 'L1_xattn_Wk': _L1_xattn_in['Wk'], 'L1_xattn_bk': _L1_xattn_in['bk'], 'L1_xattn_Wv': _L1_xattn_in['Wv'], 'L1_xattn_bv': _L1_xattn_in['bv'], 'L1_xattn_Wo': _L1_xattn_in['Wo'], 'L1_xattn_bo': _L1_xattn_in['bo'], 'L1_ffn_W_fc': _L1_ffn_in['W_fc'], 'L1_ffn_ln_w': _L1_ffn_in['ln_w'], 'L1_ffn_ln_b': _L1_ffn_in['ln_b'], 'L1_ffn_W_proj': _L1_ffn_in['W_proj'], 'L2_xattn_W': _L2_xattn_in['W'], 'L2_xattn_b': _L2_xattn_in['b'], 'L2_ffn_gate_w': _L2_ffn_in['gate_w'], 'L2_ffn_gate_b': _L2_ffn_in['gate_b'], 'L2_ffn_w1': _L2_ffn_in['w1'], 'L2_ffn_b1': _L2_ffn_in['b1'], 'L2_ffn_w2': _L2_ffn_in['w2'], 'L2_ffn_b2': _L2_ffn_in['b2'], 'L2_ffn_ln_g': _L2_ffn_in['ln_g'], 'L2_ffn_ln_b': _L2_ffn_in['ln_b'], 'L3_xattn_Wq': _L3_xattn_in['Wq'], 'L3_xattn_Wkv': _L3_xattn_in['Wkv'], 'L3_xattn_null_kv': _L3_xattn_in['null_kv'], 'L3_xattn_ln_q_g': _L3_xattn_in['ln_q_g'], 'L3_xattn_ln_q_b': _L3_xattn_in['ln_q_b'], 'L3_xattn_ln_out_g': _L3_xattn_in['ln_out_g'], 'L3_xattn_ln_out_b': _L3_xattn_in['ln_out_b'], 'L3_xattn_Wout': _L3_xattn_in['Wout'], 'L3_ffn_Wr': _L3_ffn_in['Wr'], 'L3_ffn_W1': _L3_ffn_in['W1'], 'L3_ffn_W3': _L3_ffn_in['W3'], 'L3_ffn_W2': _L3_ffn_in['W2']}

def reference(x, ctx_1024, fside_Bx16xSxS2_0, fside_SxS2_0, mask_Bx1xSxS2_ik1, mask_BxS2_bf0, g_xattn, g_ffn, L0_xattn_Wq, L0_xattn_bq, L0_xattn_Wk, L0_xattn_bk, L0_xattn_Wv, L0_xattn_bv, L0_xattn_Wo, L0_xattn_bo, L0_ffn_Wg, L0_ffn_w1, L0_ffn_w2, L1_xattn_Wq, L1_xattn_bq, L1_xattn_Wk, L1_xattn_bk, L1_xattn_Wv, L1_xattn_bv, L1_xattn_Wo, L1_xattn_bo, L1_ffn_W_fc, L1_ffn_ln_w, L1_ffn_ln_b, L1_ffn_W_proj, L2_xattn_W, L2_xattn_b, L2_ffn_gate_w, L2_ffn_gate_b, L2_ffn_w1, L2_ffn_b1, L2_ffn_w2, L2_ffn_b2, L2_ffn_ln_g, L2_ffn_ln_b, L3_xattn_Wq, L3_xattn_Wkv, L3_xattn_null_kv, L3_xattn_ln_q_g, L3_xattn_ln_q_b, L3_xattn_ln_out_g, L3_xattn_ln_out_b, L3_xattn_Wout, L3_ffn_Wr, L3_ffn_W1, L3_ffn_W3, L3_ffn_W2):
    import jax
    import jax.numpy as jnp

    def _L0_xattn_ref(query, key_, value, mask, Wq, bq, Wk, bk, Wv, bv, Wo, bo):
        import jax, jax.numpy as jnp
        import numpy as np
        D_MODEL = 128
        N_HEAD = 16
        B, S = (4, 256)

        def _split_heads(x):
            b, l, d = x.shape
            return x.reshape(b, l, N_HEAD, d // N_HEAD).transpose(0, 2, 1, 3)
        q = _split_heads(query @ Wq + bq)
        k = _split_heads(key_ @ Wk + bk)
        v = _split_heads(value @ Wv + bv)
        dh = q.shape[-1]
        score = jnp.einsum('bhqd,bhkd->bhqk', q, k) / jnp.sqrt(jnp.float32(dh))
        score = jnp.where(mask == 0, jnp.float32(-1000000000.0), score)
        attn = jax.nn.softmax(score, axis=-1)
        out = jnp.einsum('bhqk,bhkd->bhqd', attn, v)
        b, h, l, d = out.shape
        out = out.transpose(0, 2, 1, 3).reshape(b, l, h * d)
        return out @ Wo + bo

    def _L0_ffn_ref(x, Wg, w1, w2):
        import jax, jax.numpy as jnp
        import numpy as np
        d = x.shape[-1]
        xr = x.reshape(-1, d)
        S = xr.shape[0]
        E = Wg.shape[1]
        C = (S + E - 1) // E
        gate = jax.nn.softmax(xr @ Wg, axis=-1)
        idx = jnp.argmax(gate, axis=1)
        gates_s = jnp.take_along_axis(gate, idx[:, None], axis=1)[:, 0]
        onehot = jax.nn.one_hot(idx, E, dtype=jnp.int32)
        loc = jnp.sum((jnp.cumsum(onehot, axis=0) - 1) * onehot, axis=1)
        valid = loc < C
        loc_pad = jnp.minimum(loc, C)
        dispatched = jnp.zeros((E, C + 1, d), dtype=x.dtype).at[idx, loc_pad].set(xr)
        dispatched = dispatched[:, :C]
        h = jax.nn.relu(jnp.einsum('ecm,emf->ecf', dispatched, w1))
        expert_out = jnp.einsum('ecf,efm->ecm', h, w2)
        gathered = expert_out[idx, jnp.minimum(loc, C - 1)]
        combined = gathered * (gates_s * valid.astype(x.dtype))[:, None]
        return combined.reshape(x.shape)

    def _L1_xattn_ref(query, key, value, spatial_bias, directional_bias, key_padding_mask, attn_mask, Wq, bq, Wk, bk, Wv, bv, Wo, bo):
        import jax, jax.numpy as jnp
        import numpy as np
        E = 128
        H = 16
        D = E // H
        B, T, _ = query.shape
        S = key.shape[1]
        scale = D ** (-0.5)
        q = (query @ Wq.T + bq).reshape(B, T, H, D).transpose(0, 2, 1, 3)
        k = (key @ Wk.T + bk).reshape(B, S, H, D).transpose(0, 2, 1, 3)
        v = (value @ Wv.T + bv).reshape(B, S, H, D).transpose(0, 2, 1, 3)
        scores = jnp.einsum('bhtd,bhsd->bhts', q, k) * scale
        scores = scores + attn_mask[None, None, :, :]
        pad = key_padding_mask[:, None, None, :]
        scores = jnp.where(pad, -jnp.inf, scores)
        if T == S:
            scores = scores + spatial_bias + directional_bias
        probs = jax.nn.softmax(scores, axis=-1)
        out = jnp.einsum('bhts,bhsd->bhtd', probs, v)
        out = out.transpose(0, 2, 1, 3).reshape(B, T, E)
        return out @ Wo.T + bo

    def _L1_ffn_ref(x, W_fc, ln_w, ln_b, W_proj):
        import jax, jax.numpy as jnp
        import numpy as np
        EPS = 1e-06
        LN_EPS = 1e-05

        def _absmean_core(W):
            gamma = jnp.mean(jnp.abs(W)) + EPS
            Ws = W / gamma
            Wq = jnp.sign(Ws) * jnp.minimum(jnp.round(jnp.abs(Ws)), 1.0)
            return (Wq, gamma)

        @jax.custom_vjp
        def absmean(W):
            return _absmean_core(W)[0]

        def _absmean_fwd(W):
            Wq, gamma = _absmean_core(W)
            return (Wq, gamma)

        def _absmean_bwd(gamma, g):
            return (g / gamma,)
        absmean.defvjp(_absmean_fwd, _absmean_bwd)

        def layernorm(x, w, b, eps=LN_EPS):
            mu = jnp.mean(x, axis=-1, keepdims=True)
            var = jnp.mean((x - mu) ** 2, axis=-1, keepdims=True)
            return (x - mu) * jax.lax.rsqrt(var + eps) * w + b
        h = jnp.einsum('btd,hd->bth', x, absmean(W_fc))
        h = jax.nn.gelu(h, approximate=False)
        h = layernorm(h, ln_w, ln_b)
        return jnp.einsum('bth,dh->btd', h, absmean(W_proj))

    def _L2_xattn_ref(x, y, y_mask, W, b):
        import jax, jax.numpy as jnp
        import numpy as np
        B, LX, LY, D = (32, 128, 128, 128)
        x_proj = jax.nn.relu(jnp.einsum('bxd,ed->bxe', x, W) + b)
        y_proj = jax.nn.relu(jnp.einsum('byd,ed->bye', y, W) + b)
        scores = jnp.einsum('bxd,byd->bxy', x_proj, y_proj)
        scores = jnp.where(y_mask[:, None, :], -jnp.inf, scores)
        att = jax.nn.softmax(scores, axis=-1)
        return jnp.einsum('bxy,byd->bxd', att, y)

    def _L2_ffn_ref(x, gate_w, gate_b, w1, b1, w2, b2, ln_g, ln_b):
        import jax, jax.numpy as jnp
        import numpy as np
        TOP_K = 2
        TEMP = 0.9
        EPS = 1e-05
        B, S, D, F, E = (2, 256, 128, 512, 8)

        def _moe_forward(x, gate_w, gate_b, w1, b1, w2, b2, ln_g, ln_b):
            logits = (x @ gate_w + gate_b) / TEMP
            topk_vals, topk_idx = jax.lax.top_k(logits, TOP_K)
            keep = jax.nn.one_hot(topk_idx, E, dtype=jnp.bool_).any(-2)
            masked = jnp.where(keep, logits, -jnp.inf)
            gate_probs = jax.nn.softmax(masked, axis=-1)
            h = jnp.einsum('bsd,edf->bsef', x, w1) + b1
            h = jax.nn.gelu(h, approximate=False)
            expert_out = jnp.einsum('bsef,efd->bsed', h, w2) + b2
            out = jnp.einsum('bse,bsed->bsd', gate_probs, expert_out)
            mu = out.mean(-1, keepdims=True)
            var = out.var(-1, keepdims=True)
            out = (out - mu) / jnp.sqrt(var + EPS) * ln_g + ln_b
            return out
        return _moe_forward(x, gate_w, gate_b, w1, b1, w2, b2, ln_g, ln_b)

    def _L3_xattn_ref(x, context, Wq, Wkv, null_kv, ln_q_g, ln_q_b, ln_out_g, ln_out_b, Wout):
        import jax, jax.numpy as jnp
        import numpy as np
        HEADS = 8
        DIM_HEAD = 64
        SCALE = 8.0
        EPS = 1e-05

        def layer_norm(x, g, b):
            mu = jnp.mean(x, axis=-1, keepdims=True)
            var = jnp.mean((x - mu) ** 2, axis=-1, keepdims=True)
            return (x - mu) * jax.lax.rsqrt(var + EPS) * g + b
        b, n, _ = x.shape
        m = context.shape[1]
        h, d = (HEADS, DIM_HEAD)
        q = x @ Wq
        kv = context @ Wkv
        k, v = jnp.split(kv, 2, axis=-1)
        q = layer_norm(q, ln_q_g, ln_q_b)
        split = lambda t: t.reshape(t.shape[0], t.shape[1], h, d).transpose(0, 2, 1, 3)
        q, k, v = (split(q), split(k), split(v))
        nk = jnp.broadcast_to(null_kv[0], (b, h, 1, d))
        nv = jnp.broadcast_to(null_kv[1], (b, h, 1, d))
        k = jnp.concatenate([nk, k], axis=2)
        v = jnp.concatenate([nv, v], axis=2)
        q = jax.nn.softmax(q, axis=-1) * SCALE
        k = jax.nn.softmax(k, axis=2)
        ctx = jnp.einsum('bhnd,bhne->bhde', k, v)
        out = jnp.einsum('bhnd,bhde->bhne', q, ctx)
        out = out.transpose(0, 2, 1, 3).reshape(b, n, h * d)
        out = layer_norm(out, ln_out_g, ln_out_b)
        return out @ Wout

    def _L3_ffn_ref(x, Wr, W1, W3, W2):
        import math
        import jax, jax.numpy as jnp
        import numpy as np
        TOP_K = 2
        CAP_FACTOR = 1.25
        CLAMP = 10000.0
        B, S, D = x.shape
        E = Wr.shape[1]
        K = TOP_K
        T = B * S
        cap = max(1, math.ceil(T * K * CAP_FACTOR / E))
        xf = x.reshape(T, D)
        logits = jnp.clip(xf @ Wr, -CLAMP, CLAMP)
        top_v, top_i = jax.lax.top_k(logits, K)
        m = jnp.max(top_v, axis=-1, keepdims=True)
        expv = jnp.exp(top_v - m)
        top_p = expv / (jnp.sum(expv, axis=-1, keepdims=True) + 1e-12)
        Sp = T * K
        experts = top_i.reshape(Sp)
        weights = top_p.reshape(Sp)
        tokens = jnp.repeat(jnp.arange(T), K)
        oh = experts[:, None] == jnp.arange(E)[None, :]
        pos = jnp.sum(jnp.cumsum(oh.astype(jnp.int32), axis=0) * oh, axis=-1) - 1
        kept = pos < cap
        pos_safe = jnp.where(kept, pos, cap)
        xe = jnp.zeros((E, cap + 1, D), x.dtype).at[experts, pos_safe].set(xf[tokens])[:, :cap]
        h = jax.nn.silu(jnp.einsum('ecd,edf->ecf', xe, W1)) * jnp.einsum('ecd,edf->ecf', xe, W3)
        ye = jnp.einsum('ecf,efd->ecd', h, W2)
        yp = ye[experts, jnp.minimum(pos_safe, cap - 1)]
        wk = weights * kept.astype(weights.dtype)
        out = jnp.zeros((T, D), x.dtype).at[tokens].add(wk[:, None] * yp)
        return out.reshape(B, S, D)
    x = x + jnp.tanh(g_xattn[0]) * _L0_xattn_ref(_layernorm(x, axis=-1), ctx_1024, ctx_1024, mask_Bx1xSxS2_ik1, L0_xattn_Wq, L0_xattn_bq, L0_xattn_Wk, L0_xattn_bk, L0_xattn_Wv, L0_xattn_bv, L0_xattn_Wo, L0_xattn_bo)
    x = x + jnp.tanh(g_ffn[0]) * _L0_ffn_ref(_layernorm(x, axis=-1), L0_ffn_Wg, L0_ffn_w1, L0_ffn_w2)
    x = x + jnp.tanh(g_xattn[1]) * _L1_xattn_ref(_layernorm(x, axis=-1), ctx_1024, ctx_1024, fside_Bx16xSxS2_0, fside_Bx16xSxS2_0, mask_BxS2_bf0, fside_SxS2_0, L1_xattn_Wq, L1_xattn_bq, L1_xattn_Wk, L1_xattn_bk, L1_xattn_Wv, L1_xattn_bv, L1_xattn_Wo, L1_xattn_bo)
    x = x + jnp.tanh(g_ffn[1]) * _L1_ffn_ref(_layernorm(x, axis=-1), L1_ffn_W_fc, L1_ffn_ln_w, L1_ffn_ln_b, L1_ffn_W_proj)
    x = x + jnp.tanh(g_xattn[2]) * _L2_xattn_ref(_layernorm(x, axis=-1), ctx_1024, mask_BxS2_bf0, L2_xattn_W, L2_xattn_b)
    x = x + jnp.tanh(g_ffn[2]) * _L2_ffn_ref(_layernorm(x, axis=-1), L2_ffn_gate_w, L2_ffn_gate_b, L2_ffn_w1, L2_ffn_b1, L2_ffn_w2, L2_ffn_b2, L2_ffn_ln_g, L2_ffn_ln_b)
    x = x + jnp.tanh(g_xattn[3]) * _L3_xattn_ref(_layernorm(x, axis=-1), ctx_1024, L3_xattn_Wq, L3_xattn_Wkv, L3_xattn_null_kv, L3_xattn_ln_q_g, L3_xattn_ln_q_b, L3_xattn_ln_out_g, L3_xattn_ln_out_b, L3_xattn_Wout)
    x = x + jnp.tanh(g_ffn[3]) * _L3_ffn_ref(_layernorm(x, axis=-1), L3_ffn_Wr, L3_ffn_W1, L3_ffn_W3, L3_ffn_W2)
    return x

_drawn_inputs = setup_inputs


def setup_inputs(seed=0):
    import zlib

    import numpy as np

    out = dict(_drawn_inputs(seed))
    spreads = {'L1_xattn_bq': (0.0, 0.352),
     'L1_xattn_bk': (0.0, 2.0),
     'L1_xattn_bv': (0.0, 0.1),
     'L1_xattn_bo': (0.0, 0.1),
     'L1_ffn_ln_w': (1.0, 0.2),
     'L1_ffn_ln_b': (0.0, 0.1),
     'L2_ffn_gate_b': (0.0, 0.587),
     'L2_ffn_b1': (0.0, 0.8),
     'L2_ffn_b2': (0.0, 0.8),
     'L2_ffn_ln_g': (1.0, 0.6),
     'L2_ffn_ln_b': (0.0, 0.8),
     'L3_xattn_ln_q_g': (1.0, 0.6),
     'L3_xattn_ln_q_b': (0.0, 2.0),
     'L3_xattn_ln_out_g': (1.0, 0.6),
     'L3_xattn_ln_out_b': (0.0, 0.8)}
    factors = {'fside_SxS2_0': 3.812,
     'L0_xattn_bq': 8.0,
     'L0_xattn_bk': 64.0,
     'L0_xattn_bv': 2.933,
     'L0_xattn_bo': 3.182,
     'L0_ffn_Wg': 8.0,
     'L0_ffn_w1': 8.0,
     'L0_ffn_w2': 8.0,
     'L2_xattn_b': 32.941,
     'L3_xattn_Wq': 8.0,
     'L3_xattn_null_kv': 8.0,
     'L3_ffn_Wr': 8.0,
     'L3_ffn_W1': 8.0,
     'L3_ffn_W3': 8.0,
     'L3_ffn_W2': 8.0,
     'L3_xattn_Wkv': 7.838}
    for name, (base, spread) in spreads.items():
        noise = np.random.default_rng([zlib.crc32(name.encode()), seed]).standard_normal(out[name].shape)
        drawn = base * np.exp(spread * noise) if base else spread * noise
        out[name] = jnp.asarray(drawn.astype(out[name].dtype))
    for name, factor in factors.items():
        out[name] = (out[name] * factor).astype(out[name].dtype)
    return out
```

```python
from contextlib import ExitStack

import concourse.bass as bass
from concourse import mybir

F32 = mybir.dt.float32
BF16 = mybir.dt.bfloat16
I32 = mybir.dt.int32
U32 = mybir.dt.uint32
U8 = mybir.dt.uint8
ALU = mybir.AluOpType
ACT = mybir.ActivationFunctionType
AX = mybir.AxisListType

P = 128
B, S, D = 64, 64, 128
T = B * S
NT = T // P
H16, DH = 16, 8
HALF = H16 // 2
LN_EPS = 1e-5
CHUNK = 256
MAX_SLOTS = 40 * CHUNK
NOWHERE = 2.0 ** 20
MASKED = -(2.0 ** 100)


class Core:

    def __init__(self, nc, ctx):
        self.nc, self.ctx = nc, ctx
        sb = self.sb
        self.x = sb("x", [P, NT, D])
        self.bn = sb("bn", [P, NT, 6])
        self.mean = sb("mean", [P, NT])
        self.rstd = sb("rstd", [P, NT])
        self.ctxT = sb("ctxT", [P, T])
        self.ident = sb("ident", [P, P])
        self.ones = sb("ones", [1, P])
        self.gates = sb("gates", [P, 8])
        self.rows_in = nc.dram_tensor("rows_in", (MAX_SLOTS, D), F32).ap()
        self.rows_out = nc.dram_tensor("rows_out", (MAX_SLOTS, D), F32).ap()

    def sb(self, name, shape, dt=F32):
        return self.ctx.enter_context(self.nc.sbuf_tensor(name, shape, dt))


class Phase:

    def __init__(self, nc, name):
        self.nc, self.name, self.ctx, self.sems = nc, name, ExitStack(), []

    def __enter__(self):
        return self

    def __exit__(self, *e):
        self.ctx.__exit__(*e)
        if self.sems:
            self.nc.clear_and_free_semaphores(self.sems)
            self.nc.all_engine_barrier()

    def sb(self, name, shape, dt=F32):
        return self.ctx.enter_context(self.nc.sbuf_tensor(f"{self.name}_{name}", shape, dt))

    def ps(self, name, shape, dt=F32):
        return self.ctx.enter_context(self.nc.psum_tensor(f"{self.name}_{name}", shape, dt))

    def sem(self, name):
        self.sems.append(self.nc.alloc_semaphore(f"{self.name}_{name}"))
        return self.sems[-1]


def reused(eng, sem, value):
    if not isinstance(value, int) or value > 0:
        eng.wait_ge(sem, value)


def flat(ap):
    return ap.rearrange("b s d -> (b s) d")


def setup(nc, core, x_dram, ctx_dram, g_xattn, g_ffn):
    G = 4
    with Phase(nc, "setup") as ph:
        g_raw = ph.sb("g_raw", [P, 8])
        zeros = ph.sb("zeros", [P, 8 * D])
        zeroed = ph.sem("zeroed")
        raw = ph.sb("raw", [P, 2, G, D])
        turned = [ph.ps(f"turned{k}", [P, G * P]) for k in range(2)]
        x_in, g_in, ctx_in = ph.sem("x_in"), ph.sem("g_in"), [ph.sem("ctx_in0"), ph.sem("ctx_in1")]
        filled, ident_done = ph.sem("filled"), ph.sem("ident_done")
        turned_ready, ctxT_done = ph.sem("turned_ready"), ph.sem("ctxT_done")
        summed, gates_done = ph.sem("summed"), ph.sem("gates_done")
        x_tiles = flat(x_dram).rearrange("(n p) d -> p n d", p=P)
        ctx_tiles = flat(ctx_dram).rearrange("(n p) d -> p n d", p=P)
        block = ph.ctx.enter_context(nc.Block())

        @block.sync
        def _(sp):
            sp.dma_start(raw[:, 0, :, :], ctx_tiles[:, 0:G, :]).then_inc(ctx_in[0], 16)
            sp.dma_start(core.x[:, :, :], x_tiles).then_inc(x_in, 16)
            sp.dma_start(g_raw[:, 0:4], g_xattn.rearrange("(a n) -> a n", a=1).broadcast_to([P, 4])).then_inc(g_in, 16)
            sp.dma_start(g_raw[:, 4:8], g_ffn.rearrange("(a n) -> a n", a=1).broadcast_to([P, 4])).then_inc(g_in, 16)
            for c in range(1, NT // G):
                if c >= 2:
                    sp.wait_ge(turned_ready, c - 1)
                sp.dma_start(raw[:, c % 2, :, :], ctx_tiles[:, c * G:(c + 1) * G, :]).then_inc(ctx_in[c % 2], 16)
            sp.wait_ge(filled, 3)
            tables = core.rows_in.rearrange("(n p a) d -> n p (a d)", p=P, a=8)
            for n in range(MAX_SLOTS // P // 8):
                sp.dma_start(tables[n, :, :], zeros[:, :]).then_inc(zeroed, 16)
            sp.wait_ge(zeroed, 16 * (MAX_SLOTS // P // 8))

        @block.gpsimd
        def _(pool):
            pool.memset(core.ident[:, :], 0.0).then_inc(filled, 1)
            pool.memset(core.ones[:, :], 1.0).then_inc(filled, 1)
            pool.memset(zeros[:, :], 0.0).then_inc(filled, 1)
            pool.wait_ge(filled, 3)
            pool.affine_select(out=core.ident[:, :], in_=core.ident[:, :], compare_op=ALU.not_equal, fill=1.0,
                               base=0, pattern=[[-1, P]], channel_multiplier=1).then_inc(ident_done, 1)

        @block.tensor
        def _(pe):
            pe.wait_ge(ident_done, 1)
            for c in range(NT // G):
                pe.wait_ge(ctx_in[c % 2], 16 * (c // 2 + 1))
                if c >= 2:
                    pe.wait_ge(ctxT_done, c - 1)
                for k in range(G):
                    last = nc.tensor.transpose(turned[c % 2][:, k * P:(k + 1) * P], raw[:, c % 2, k, :], core.ident[:, :])
                last.then_inc(turned_ready, 1)

        @block.scalar
        def _(act):
            act.wait_ge(g_in, 32)
            nc.scalar.activation(core.gates[:, :], g_raw[:, :], ACT.Tanh).then_inc(gates_done, 1)
            for c in range(NT // G):
                act.wait_ge(turned_ready, c + 1)
                nc.scalar.copy(core.ctxT[:, c * G * P:(c + 1) * G * P], turned[c % 2][:, :]).then_inc(ctxT_done, 1)

        @block.vector
        def _(dve):
            dve.wait_ge(x_in, 16)
            with dve.Fori(0, NT) as t:
                nc.vector.bn_stats(core.bn[:, t, :], core.x[:, t, :]).then_inc(summed, 1)


def row_statistics(nc, ph, core):
    root = ph.sb("root", [P, NT])
    y = ph.sb("y", [P, NT])
    yy = ph.sb("yy", [P, NT])
    veps = ph.sb("veps", [P, NT])
    ready, rooted, stepped = ph.sem("veps_ready"), ph.sem("rooted"), ph.sem("stepped")

    def on_scalar(act):
        act.wait_ge(ready, 1)
        nc.scalar.activation(root[:, :], veps[:, :], ACT.Sqrt).then_inc(rooted, 1)

    def on_vector(dve):
        def step(k, ins):
            ins.then_inc(stepped, 1)
            dve.wait_ge(stepped, k)
        even, odd = core.bn[:, :, 1], core.bn[:, :, 4]
        step(1, nc.vector.tensor_tensor(y[:, :], even, odd, ALU.subtract))
        step(2, nc.vector.tensor_tensor(yy[:, :], core.bn[:, :, 2], core.bn[:, :, 5], ALU.add))
        step(3, nc.vector.tensor_tensor(core.mean[:, :], even, odd, ALU.add))
        step(4, nc.vector.tensor_scalar(core.mean[:, :], core.mean[:, :], 0.5, None, ALU.mult))
        step(5, nc.vector.scalar_tensor_tensor(out=y[:, :], in0=y[:, :], scalar=0.25, in1=y[:, :], op0=ALU.mult, op1=ALU.mult))
        step(6, nc.vector.tensor_scalar(yy[:, :], yy[:, :], 1.0 / D, LN_EPS, ALU.mult, ALU.add))
        nc.vector.tensor_tensor(veps[:, :], yy[:, :], y[:, :], ALU.add).then_inc(ready, 1)
        dve.wait_ge(rooted, 1)
        step(7, nc.vector.reciprocal(y[:, :], root[:, :]))
        step(8, nc.vector.tensor_tensor(yy[:, :], y[:, :], y[:, :], ALU.mult))
        step(9, nc.vector.tensor_tensor(yy[:, :], yy[:, :], veps[:, :], ALU.mult))
        step(10, nc.vector.tensor_scalar(yy[:, :], yy[:, :], -0.5, 1.5, ALU.mult, ALU.add))
        step(11, nc.vector.tensor_tensor(core.rstd[:, :], y[:, :], yy[:, :], ALU.mult))

    return on_scalar, on_vector


def attention16(nc, core, name, gate, w_dram, b_dram, transposed, neg_steps, side=None, neg_extra=None):
    with Phase(nc, name) as ph:
        w_raw = ph.sb("w_raw", [P, 4, D])
        w = ph.sb("w", [P, 4, D])
        bq = ph.sb("bq", [P, 2])
        bk = ph.sb("bk", [P, 2])
        bv = ph.sb("bv", [P, 1])
        bo = ph.sb("bo", [1, D])
        bvo = ph.sb("bvo", [1, D])
        own = ph.sb("own", [P, HALF])
        xn = ph.sb("xn", [P, D])
        xnT = ph.sb("xnT", [P, P])
        cdup = ph.sb("cdup", [P, 2, 2, S])
        qbd = ph.sb("qbd", [P, 2, P])
        kT = ph.sb("kT", [P, 2, S])
        kbd = ph.sb("kbd", [P, 2, HALF, S])
        vbd = ph.sb("vbd", [P, 2, HALF, 2, DH + 1])
        s1 = ph.sb("s1", [P, H16, S])
        s2 = ph.sb("s2", [P, H16, S])
        p = ph.sb("p", [P, H16, S])
        pT = ph.sb("pT", [P, HALF, P])
        mx = ph.sb("mx", [P, H16])
        rden = ph.sb("rden", [P, H16])
        o = ph.sb("o", [P, D])
        oT = ph.sb("oT", [P, P])
        neg = ph.sb("neg", [P, NT, S])
        ps_x = ph.ps("ps_x", [P, P])
        ps_qk = ph.ps("ps_qk", [P, 4 * S])
        ps_v = ph.ps("ps_v", [P, 2, D])
        ps_s = ph.ps("ps_s", [P, H16, S])
        ps_t = ph.ps("ps_t", [P, HALF, P])
        ps_o = ph.ps("ps_o", [P, 512])
        side_in_buf = ph.sb("side", [P, 2, H16, S]) if side is not None else None

        names = ("w_in b_in w_ready w_turned neg_ready filled own_ready bvo_ready qk_scaled "
                 "xn_ready xnT_ps xnT_ready cdup_ready qk_ps v_ps q_ready k_ready kbd_ready vbd_ready "
                 "s_ps s1_ready max_ready s2_ready p_ready pT_ps pT_ready o_ps rden_ready o_ready oT_ps oT_ready "
                 "y_ps x_ready summed aggregated").split()
        if side is not None:
            names += ["side_in0", "side_in1", "side_ready"]
        s = {n: ph.sem(n) for n in names}
        root_on_scalar, root_on_vector = row_statistics(nc, ph, core)
        neg_dma, neg_vector = neg_steps(ph, neg, s["neg_ready"])
        block = ph.ctx.enter_context(nc.Block())

        if side is not None:
            side_tiles = side.rearrange("(n b) h q k -> n b q h k", b=2)

        @block.sync
        def _(sp):
            for k in range(4):
                dst = (w_raw if transposed else w)[:, k, :]
                sp.dma_start(dst, w_dram[k]).then_inc(s["w_in"], 16)
            neg_dma(sp)
            for half in range(2):
                rows = slice(64 * half, 64 * half + 64)
                sp.dma_start(bq[rows, :], b_dram[0].rearrange("(h r) -> r h", h=2), allow_slow_non_contiguous=True).then_inc(s["b_in"], 16)
                sp.dma_start(bk[rows, :], b_dram[1].rearrange("(h r) -> r h", h=2), allow_slow_non_contiguous=True).then_inc(s["b_in"], 16)
            sp.dma_start(bv[:, :], b_dram[2].rearrange("(r a) -> r a", a=1)).then_inc(s["b_in"], 16)
            sp.dma_start(bo[:, :], b_dram[3].rearrange("(a r) -> a r", a=1)).then_inc(s["b_in"], 16)
            if side is not None:
                def load_side(t, k):
                    for b in range(2):
                        sp.dma_start(side_in_buf[64 * b:64 * b + 64, k, :, :], side_tiles[t, b, :, :, :]
                                     ).then_inc(s[f"side_in{k}"], 16)
                load_side(0, 0)
                load_side(1, 1)
                with sp.Fori(1, NT // 2) as u:
                    for k in range(2):
                        sp.wait_ge(s["s1_ready"], u * 2 + (k - 1))
                        load_side(u * 2 + k, k)

        @block.gpsimd
        def _(pool):
            pool.memset(own[:, :], 1.0).then_inc(s["filled"], 1)
            pool.memset(qbd[:, :, :], 0.0).then_inc(s["filled"], 1)
            pool.memset(vbd[:, :, :, :, :], 0.0).then_inc(s["filled"], 1)
            pool.wait_ge(s["filled"], 3)
            for h in range(2):
                rows = slice(64 * h, 64 * h + 64)
                pool.memset(vbd[rows, :, :, h, DH:DH + 1], 1.0).then_inc(s["filled"], 1)
            for h in range(2):
                part = own[64 * h:64 * h + 64, :]
                pool.affine_select(out=part, in_=part, compare_op=ALU.is_ge, fill=0.0, base=0,
                                   pattern=[[-DH, HALF]], channel_multiplier=1).then_inc(s["own_ready"], 1)
            pool.wait_ge(s["own_ready"], 2)
            for h in range(2):
                part = own[64 * h:64 * h + 64, :]
                pool.affine_select(out=part, in_=part, compare_op=ALU.is_ge, fill=0.0, base=DH - 1,
                                   pattern=[[DH, HALF]], channel_multiplier=-1).then_inc(s["own_ready"], 1)
            pool.wait_ge(s["own_ready"], 4)

            def context(t):
                reused(pool, s["v_ps"], t)
                src = core.ctxT[:, bass.ts(t, P)].rearrange("p (b k) -> p b k", b=2)
                pool.tensor_copy(cdup[:, :, :, :], src.unsqueeze(2).broadcast_to([P, 2, 2, S])).then_inc(s["cdup_ready"], 1)

            def spread(t):
                pool.wait_ge(s["k_ready"], t + 1)
                reused(pool, s["s_ps"], t)
                for hh in range(2):
                    pool.tensor_tensor(kbd[:, hh, :, :], kT[:, hh, :].unsqueeze(1).broadcast_to([P, HALF, S]),
                                       own[:, :].unsqueeze(2).broadcast_to([P, HALF, S]), ALU.mult
                                       ).then_inc(s["kbd_ready"], 1)

            def side_add(t, k):
                pool.wait_ge(s[f"side_in{k}"], t * 16 + (32 if k == 0 else 16))
                buf = side_in_buf[:, k, :, :]
                pool.tensor_tensor(buf, buf, neg[:, t, :].unsqueeze(1).broadcast_to([P, H16, S]), ALU.add
                                   ).then_inc(s["side_ready"], 1)

            if side is None:
                context(0)
                spread(0)
                with pool.Fori(1, NT) as i:
                    context(i)
                    spread(i)
            else:
                pool.wait_ge(s["neg_ready"], 1)

                def pair(i):
                    for k in range(2):
                        context(i + k)
                        spread(i + k)
                        side_add(i + k, k)
                pair(0)
                with pool.Fori(1, NT // 2) as u:
                    pair(u * 2)

        @block.tensor
        def _(pe):
            pe.wait_ge(s["w_in"], 64)
            if transposed:
                for k in range(4):
                    last = nc.tensor.transpose(ps_t[:, k, :], w_raw[:, k, :], core.ident[:, :])
                last.then_inc(s["w_turned"], 1)
            pe.wait_ge(s["w_ready"], 1)
            pe.wait_ge(s["b_in"], 96)
            nc.tensor.matmul(ps_o[0:1, 0:D], bv[:, :], w[:, 3, :], start=True, stop=True).then_inc(s["w_turned"], 1)
            pe.wait_ge(s["bvo_ready"], 1)

            def turn_x(t):
                pe.wait_ge(s["xn_ready"], t + 1)
                reused(pe, s["xnT_ready"], t)
                nc.tensor.transpose(ps_x[:, :], xn[:, :], core.ident[:, :]).then_inc(s["xnT_ps"], 1)

            def project(t):
                pe.wait_ge(s["cdup_ready"], t + 1)
                reused(pe, s["k_ready"], t)
                for hh in range(2):
                    for b in range(2):
                        nc.tensor.matmul(ps_qk[64 * b:64 * b + 64, (2 + hh) * S:(3 + hh) * S], w[:, 1, 64 * hh:64 * hh + 64],
                                         cdup[:, b, 0, :], start=True, stop=True)
                reused(pe, s["vbd_ready"], 2 * t)
                for b in range(2):
                    last = nc.tensor.matmul(ps_v[:, b, :], cdup[:, b, :, :].rearrange("p a k -> p (a k)"), w[:, 2, :],
                                            start=True, stop=True)
                last.then_inc(s["v_ps"], 1)
                pe.wait_ge(s["xnT_ready"], t + 1)
                for hh in range(2):
                    for b in range(2):
                        last = nc.tensor.matmul(ps_qk[64 * b:64 * b + 64, hh * S:(hh + 1) * S], w[:, 0, 64 * hh:64 * hh + 64],
                                                xnT[:, 64 * b:64 * b + 64], start=True, stop=True)
                last.then_inc(s["qk_ps"], 1)

            def scores(t):
                pe.wait_ge(s["q_ready"], 2 * t + 2)
                pe.wait_ge(s["kbd_ready"], 2 * t + 2)
                reused(pe, s["s1_ready"], t)
                for hh in range(2):
                    last = nc.tensor.matmul(ps_s[:, hh * HALF:(hh + 1) * HALF, :], qbd[:, hh, :], kbd[:, hh, :, :],
                                            start=True, stop=True)
                last.then_inc(s["s_ps"], 1)

            def values(t):
                pe.wait_ge(s["p_ready"], t + 1)
                reused(pe, s["pT_ready"], 2 * t)
                for j in range(HALF):
                    last = nc.tensor.transpose(ps_t[:, j, :], p[:, 2 * j:2 * j + 2, :].rearrange("q a k -> q (a k)"), core.ident[:, :])
                    if j % 4 == 3:
                        last.then_inc(s["pT_ps"], 1)
                pe.wait_ge(s["vbd_ready"], 2 * t + 2)
                reused(pe, s["x_ready"], t)
                for j in range(HALF):
                    if j % 4 == 0:
                        pe.wait_ge(s["pT_ready"], 2 * t + j // 4 + 1)
                    for b in range(2):
                        last = nc.tensor.matmul(ps_o[64 * b:64 * b + 64, 18 * j:18 * j + 18], pT[:, j, 64 * b:64 * b + 64],
                                                vbd[:, b, j, :, :], start=True, stop=True)
                last.then_inc(s["o_ps"], 1)
                pe.wait_ge(s["o_ready"], t + 1)
                nc.tensor.transpose(ps_o[:, 256:256 + P], o[:, :], core.ident[:, :]).then_inc(s["oT_ps"], 1)
                pe.wait_ge(s["oT_ready"], t + 1)
                nc.tensor.matmul(ps_o[:, 384:384 + D], oT[:, :], w[:, 3, :], start=True, stop=False)
                nc.tensor.matmul(ps_o[:, 384:384 + D], core.ones[:, :], bvo[:, :], start=False, stop=True).then_inc(s["y_ps"], 1)

            turn_x(0)
            project(0)
            scores(0)
            def step(i):
                turn_x(i + 1)
                project(i + 1)
                values(i)
                scores(i + 1)

            step(0)
            with pe.Fori(1, NT - 1) as i:
                step(i)
            values(NT - 1)

        @block.scalar
        def _(act):
            if transposed:
                act.wait_ge(s["w_turned"], 1)
                nc.scalar.copy(w[:, :, :], ps_t[:, 0:4, :]).then_inc(s["w_ready"], 1)
            root_on_scalar(act)
            act.wait_ge(s["w_in"], 64)
            act.wait_ge(s["b_in"], 96)

            def queries(t):
                act.wait_ge(s["xnT_ps"], t + 1)
                reused(act, s["qk_ps"], t)
                nc.scalar.copy(xnT[:, :], ps_x[:, :]).then_inc(s["xnT_ready"], 1)

            def values(t):
                act.wait_ge(s["v_ps"], t + 1)
                reused(act, s["o_ps"], t)
                for h in range(2):
                    rows = slice(64 * h, 64 * h + 64)
                    src = ps_v[rows, :, :].rearrange("p b (j a d) -> p b j a d", a=2, d=DH)[:, :, :, h, :]
                    nc.scalar.copy(vbd[rows, :, :, h, 0:DH], src).then_inc(s["vbd_ready"], 1)

            def exponent(t):
                act.wait_ge(s["s2_ready"], t + 1)
                reused(act, s["pT_ps"], 2 * t)
                nc.scalar.activation(p[:, :, :], s2[:, :, :], ACT.Exp).then_inc(s["p_ready"], 1)

            def turned(t):
                for k in range(2):
                    act.wait_ge(s["pT_ps"], 2 * t + k + 1)
                    if k == 0:
                        reused(act, s["o_ps"], t)
                    nc.scalar.copy(pT[:, 4 * k:4 * k + 4, :], ps_t[:, 4 * k:4 * k + 4, :]).then_inc(s["pT_ready"], 1)

            def outputs(t):
                act.wait_ge(s["oT_ps"], t + 1)
                reused(act, s["y_ps"], t)
                nc.scalar.copy(oT[:, :], ps_o[:, 256:256 + P]).then_inc(s["oT_ready"], 1)

            queries(0)
            values(0)
            def step(i):
                exponent(i)
                queries(i + 1)
                turned(i)
                outputs(i)
                values(i + 1)

            step(0)
            nc.scalar.preload_act_table(ACT.Exp)
            with act.Fori(1, NT - 1) as i:
                step(i)
            exponent(NT - 1)
            turned(NT - 1)
            outputs(NT - 1)

        @block.vector
        def _(dve):
            neg_vector(dve)
            if not transposed:
                dve.wait_ge(s["w_in"], 64)
                nc.vector.memset(s2[0:1, 0, 0:1], 0.0).then_inc(s["w_ready"], 1)
            dve.wait_ge(s["w_ready"], 1)
            dve.wait_ge(s["b_in"], 96)
            nc.vector.tensor_scalar(w[:, 0, :], w[:, 0, :], DH ** -0.5, None, ALU.mult).then_inc(s["qk_scaled"], 1)
            nc.vector.tensor_scalar(bq[:, :], bq[:, :], DH ** -0.5, None, ALU.mult).then_inc(s["qk_scaled"], 1)
            dve.wait_ge(s["w_turned"], 2 if transposed else 1)
            nc.vector.tensor_tensor(bvo[:, :], ps_o[0:1, 0:D], bo[:, :], ALU.add).then_inc(s["bvo_ready"], 1)
            dve.wait_ge(s["filled"], 5)
            dve.wait_ge(s["qk_scaled"], 2)
            dve.wait_ge(s["bvo_ready"], 1)
            root_on_vector(dve)

            def normalise(t):
                reused(dve, s["xnT_ps"], t)
                nc.vector.tensor_scalar(xn[:, :], core.x[:, t, :], core.mean[:, bass.ts(t, 1)], core.rstd[:, bass.ts(t, 1)],
                                        ALU.subtract, ALU.mult).then_inc(s["xn_ready"], 1)

            def queries_keys(t):
                dve.wait_ge(s["qk_ps"], t + 1)
                reused(dve, s["s_ps"], t)
                for b in range(2):
                    rows = slice(64 * b, 64 * b + 64)
                    nc.vector.tensor_tensor(qbd[rows, :, 64 * b:64 * b + 64], ps_qk[rows, 0:2 * S].rearrange("p (h q) -> p h q", h=2),
                                            bq[rows, :].unsqueeze(2).broadcast_to([64, 2, S]), ALU.add).then_inc(s["q_ready"], 1)
                reused(dve, s["kbd_ready"], 2 * t)
                nc.vector.tensor_tensor(kT[:, :, :], ps_qk[:, 2 * S:4 * S].rearrange("p (h q) -> p h q", h=2),
                                        bk[:, :].unsqueeze(2).broadcast_to([P, 2, S]), ALU.add).then_inc(s["k_ready"], 1)

            def softmax(t, k):
                dve.wait_ge(s["s_ps"], t + 1)
                if side is None:
                    nc.vector.tensor_tensor(s1[:, :, :], ps_s[:, :, :], neg[:, t, :].unsqueeze(1).broadcast_to([P, H16, S]),
                                            ALU.add).then_inc(s["s1_ready"], 1)
                else:
                    dve.wait_ge(s["side_ready"], t + 1)
                    nc.vector.scalar_tensor_tensor(out=s1[:, :, :], in0=side_in_buf[:, k, :, :], scalar=2.0, in1=ps_s[:, :, :],
                                                   op0=ALU.mult, op1=ALU.add).then_inc(s["s1_ready"], 1)
                dve.wait_ge(s["s1_ready"], t + 1)
                nc.vector.tensor_reduce(mx[:, :], s1[:, :, :], AX.X, ALU.max).then_inc(s["max_ready"], 1)
                dve.wait_ge(s["max_ready"], t + 1)
                reused(dve, s["p_ready"], t)
                nc.vector.tensor_tensor(s2[:, :, :], s1[:, :, :], mx[:, :].unsqueeze(2).broadcast_to([P, H16, S]),
                                        ALU.subtract).then_inc(s["s2_ready"], 1)

            def outputs(t):
                dve.wait_ge(s["o_ps"], t + 1)
                o_ps = ps_o[:, 0:18 * HALF].rearrange("p (h d) -> p h d", d=DH + 1)
                nc.vector.reciprocal(rden[:, :], o_ps[:, :, DH]).then_inc(s["rden_ready"], 1)
                dve.wait_ge(s["rden_ready"], t + 1)
                nc.vector.tensor_tensor(o[:, :].rearrange("p (h d) -> p h d", d=DH), o_ps[:, :, 0:DH],
                                        rden[:, :].unsqueeze(2).broadcast_to([P, H16, DH]), ALU.mult).then_inc(s["o_ready"], 1)

            def residual(t):
                dve.wait_ge(s["y_ps"], t + 1)
                nc.vector.scalar_tensor_tensor(out=core.x[:, t, :], in0=ps_o[:, 384:384 + D], scalar=core.gates[:, gate:gate + 1],
                                               in1=core.x[:, t, :], op0=ALU.mult, op1=ALU.add).then_inc(s["x_ready"], 1)
                dve.wait_ge(s["x_ready"], t + 1)
                dve.wait_ge(s["bvo_ready"], 1)
                nc.vector.bn_stats(core.bn[:, t, :], core.x[:, t, :]).then_inc(s["summed"], 1)

            def step(i, k, last=False):
                softmax(i, k)
                if not last:
                    normalise(i + 1)
                outputs(i)
                if not last:
                    queries_keys(i + 1)
                residual(i)

            normalise(0)
            queries_keys(0)
            if side is None:
                step(0, 0)
                with dve.Fori(1, NT - 1) as i:
                    step(i, 0)
                step(NT - 1, 0, last=True)
            else:
                step(0, 0)
                step(1, 1)
                with dve.Fori(1, NT // 2 - 1) as u:
                    step(u * 2, 0)
                    step(u * 2 + 1, 1)
                step(NT - 2, 0)
                step(NT - 1, 1, last=True)


def store_x(nc, core, out):
    with Phase(nc, "store") as ph:
        stored = ph.sem("stored")
        block = ph.ctx.enter_context(nc.Block())

        @block.sync
        def _(sp):
            sp.dma_start(flat(out).rearrange("(n p) d -> p n d", p=P), core.x[:, :, :]).then_inc(stored, 16)
            sp.wait_ge(stored, 16)


def build(nc, a, out, stop):
    with ExitStack() as ctx:
        core = Core(nc, ctx)
        setup(nc, core, a["x"], a["ctx_1024"], a["g_xattn"], a["g_ffn"])

        def neg_of_mask(ph, neg, ready):
            raw = ph.sb("mask_raw", [P, NT, S], I32)
            mask_in = ph.sem("mask_in")

            def dma(sp):
                sp.dma_start(raw[:, :, :], a["mask_Bx1xSxS2_ik1"].rearrange("b a q k -> (b a q) k").rearrange(
                    "(n p) k -> p n k", p=P)).then_inc(mask_in, 16)

            def vector(dve):
                dve.wait_ge(mask_in, 16)
                nc.vector.tensor_scalar(neg[:, :, :], raw[:, :, :], 0.0, MASKED, ALU.is_equal, ALU.mult).then_inc(ready, 1)
                dve.wait_ge(ready, 1)
            return dma, vector

        attention16(nc, core, "l0a", 0, [a[f"L0_xattn_W{c}"] for c in "qkvo"], [a[f"L0_xattn_b{c}"] for c in "qkvo"],
                    False, neg_of_mask)
        if stop > 1:
            build_rest(nc, core, a, stop)
        store_x(nc, core, out)



class Routing:

    def __init__(self, ph, top, experts, rows):
        self.top, self.experts = top, experts
        self.rows = rows
        self.slot = ph.sb("slot", [P, top, NT], U32)
        self.weight = ph.sb("weight", [P, top, NT])
        self.chunk_expert = ph.sb("chunk_expert", [1, MAX_SLOTS // CHUNK], I32)


def route(nc, core, name, r, gate, wg_dram, cap, bg_dram=None, temp=1.0, sum_eps=0.0, clamp=None):
    E, top = r.experts, r.top
    G = 4
    with Phase(nc, name) as ph:
        wg = ph.sb("wg", [P, E])
        bg = ph.sb("bg", [P, E])
        xs = ph.sb("xs", [P, 2, G, D])
        xT = ph.sb("xT", [P, G * P])
        xn_all = ph.sb("xn_all", [P, NT, D])
        lg = ph.sb("lg", [P, NT, E])
        tmp = ph.sb("tmp", [P, NT, E])
        picks = [ph.sb(f"pick{k}", [P, NT, E]) for k in range(top)]
        member = ph.sb("member", [P, NT, E])
        pos = ph.sb("pos", [P, NT, E])
        scan = [ph.sb(f"scan{k}", [P, NT, E]) for k in range(2)]
        best = ph.sb("best", [P, top, NT])
        index = ph.sb("index", [P, NT])
        choice_pos = ph.sb("choice_pos", [P, NT])
        choice_slot = ph.sb("choice_slot", [P, NT])
        iota_i = ph.sb("iota_i", [P, E], I32)
        iota = ph.sb("iota", [P, E])
        before = ph.sb("before", [P, P])
        ones = ph.sb("ones", [P, P])
        total = ph.sb("total", [P, NT])
        ps_x = ph.ps("ps_x", [P, G * P])
        ps_l = ph.ps("ps_l", [P, 512])
        ps_before = ph.ps("ps_before", [P, 512])
        ps_total = ph.ps("ps_total", [P, 512])
        NC = MAX_SLOTS // CHUNK
        if cap is None:
            starts_i = ph.sb("starts_i", [P, NC], I32)
            starts = ph.sb("starts", [P, NC])
            more = ph.sb("more", [P, E, NC])
            ends = [ph.sb(f"ends{k}", [P, E]) for k in range(2)]
            chunks = ph.sb("chunks", [P, E])
            ce = ph.sb("ce", [P, NC])
        sems = {n: ph.sem(n) for n in "wg_in xs_ready xn_ready xT_ps xT_ready l_ps lg_ready member_ready filled consts prefix_ps exp_in exp_out slots_ready scattered".split()}
        step_sem = ph.sem("step")
        root_on_scalar, root_on_vector = row_statistics(nc, ph, core)
        block = ph.ctx.enter_context(nc.Block())

        @block.sync
        def _(sp):
            sp.dma_start(wg[:, :], wg_dram).then_inc(sems["wg_in"], 16)
            if bg_dram is not None:
                sp.dma_start(bg[:, :], bg_dram.rearrange("(a n) -> a n", a=1).broadcast_to([P, E])).then_inc(sems["wg_in"], 16)

        @block.gpsimd
        def _(pool):
            pool.memset(ones[:, :], 1.0).then_inc(sems["filled"], 1)
            pool.iota(iota_i[:, :], [[1, E]], base=0, channel_multiplier=0).then_inc(sems["filled"], 1)
            if cap is None:
                pool.iota(starts_i[:, :], [[CHUNK, NC]], base=0, channel_multiplier=0).then_inc(sems["filled"], 1)
            pool.wait_ge(sems["filled"], 3 if cap is None else 2)
            pool.affine_select(out=before[:, :], in_=ones[:, :], compare_op=ALU.is_ge, fill=0.0, base=-1,
                               pattern=[[1, P]], channel_multiplier=-1).then_inc(sems["consts"], 1)
            pool.tensor_copy(iota[:, :], iota_i[:, :]).then_inc(sems["consts"], 1)
            if cap is None:
                pool.tensor_copy(starts[:, :], starts_i[:, :]).then_inc(sems["consts"], 1)
            pool.wait_ge(sems["slots_ready"], top)
            for t in range(NT):
                for k in range(top):
                    pool.indirect_dma_start(
                        out=core.rows_in[0:r.rows, :], out_offset=bass.IndirectOffsetOnAxis(ap=r.slot[:, k, t:t + 1], axis=0),
                        in_=xn_all[:, t, :], in_offset=None, bounds_check=r.rows - 1, oob_is_err=False
                    ).then_inc(sems["scattered"], 16)
            pool.wait_ge(sems["scattered"], 16 * NT * top)

        @block.tensor
        def _(pe):
            def chunk(c, k):
                pe.wait_ge(sems["xs_ready"], c + 1)
                reused(pe, sems["xT_ready"], c)
                for g in range(G):
                    last = nc.tensor.transpose(ps_x[:, g * P:(g + 1) * P], xs[:, k, g, :], core.ident[:, :])
                last.then_inc(sems["xT_ps"], 1)
                pe.wait_ge(sems["xT_ready"], c + 1)
                reused(pe, sems["lg_ready"], c)
                for g in range(G):
                    last = nc.tensor.matmul(ps_l[:, g * E:(g + 1) * E], xT[:, g * P:(g + 1) * P], wg[:, :], start=True, stop=True)
                last.then_inc(sems["l_ps"], 1)
            pe.wait_ge(sems["wg_in"], 16 if bg_dram is None else 32)
            chunk(0, 0)
            chunk(1, 1)
            with pe.Fori(1, NT // G // 2) as u:
                chunk(u * 2, 0)
                chunk(u * 2 + 1, 1)
            pe.wait_ge(sems["consts"], 2)
            pe.wait_ge(sems["member_ready"], 1)
            flat_member = member[:, :, :].rearrange("p t e -> p (t e)")
            nc.tensor.matmul(ps_before[:, 0:NT * E], before[:, :], flat_member, start=True, stop=True).then_inc(sems["prefix_ps"], 1)
            nc.tensor.matmul(ps_total[:, 0:NT * E], ones[:, :], flat_member, start=True, stop=True).then_inc(sems["prefix_ps"], 1)

        @block.scalar
        def _(act):
            root_on_scalar(act)

            def chunk(c):
                act.wait_ge(sems["xT_ps"], c + 1)
                reused(act, sems["l_ps"], c)
                nc.scalar.copy(xT[:, :], ps_x[:, :]).then_inc(sems["xT_ready"], 1)
            chunk(0)
            with act.Fori(1, NT // G) as c:
                chunk(c)
            act.wait_ge(sems["exp_in"], 1)
            if top == 1:
                nc.scalar.activation(tmp[:, :, :], tmp[:, :, :], ACT.Exp).then_inc(sems["exp_out"], 1)
            else:
                nc.scalar.activation(total[:, :], total[:, :], ACT.Exp, scale=1.0 / temp).then_inc(sems["exp_out"], 1)

        @block.vector
        def _(dve):
            root_on_vector(dve)
            dve.wait_ge(sems["wg_in"], 16 if bg_dram is None else 32)

            def rows(c, k):
                reused(dve, sems["xT_ps"], c - 1)
                for g in range(G):
                    last = nc.vector.tensor_scalar(xs[:, k, g, :], core.x[:, c * G + g, :], core.mean[:, bass.ts(c * G + g, 1)],
                                                   core.rstd[:, bass.ts(c * G + g, 1)], ALU.subtract, ALU.mult)
                last.then_inc(sems["xs_ready"], 1)
                for g in range(G):
                    nc.vector.tensor_scalar(xn_all[:, c * G + g, :], core.x[:, c * G + g, :], core.mean[:, bass.ts(c * G + g, 1)],
                                            core.rstd[:, bass.ts(c * G + g, 1)], ALU.subtract, ALU.mult).then_inc(sems["xn_ready"], 1)

            def logits(c):
                dve.wait_ge(sems["l_ps"], c + 1)
                src = ps_l[:, 0:G * E].rearrange("p (g e) -> p g e", g=G)
                if bg_dram is not None:
                    nc.vector.tensor_tensor(lg[:, bass.ts(c, G), :], src, bg[:, :].unsqueeze(1).broadcast_to([P, G, E]), ALU.add
                                            ).then_inc(sems["lg_ready"], 1)
                else:
                    lim = clamp or 3e38
                    nc.vector.tensor_scalar(lg[:, bass.ts(c, G), :], src, lim, -lim, ALU.min, ALU.max).then_inc(sems["lg_ready"], 1)
            rows(0, 0)
            rows(1, 1)
            logits(0)
            with dve.Fori(1, NT // G // 2) as u:
                rows(u * 2, 0)
                logits(u * 2 - 1)
                rows(u * 2 + 1, 1)
                logits(u * 2)
            logits(NT // G - 1)
            dve.wait_ge(sems["lg_ready"], NT // G)
            dve.wait_ge(sems["xn_ready"], NT)
            dve.wait_ge(sems["consts"], 3 if cap is None else 2)

            steps = [0]

            def step(ins):
                steps[0] += 1
                ins.then_inc(step_sem, 1)
                dve.wait_ge(step_sem, steps[0])

            def over_experts(ap):
                return ap.unsqueeze(2).broadcast_to([P, NT, E])

            def over_tokens(ap):
                return ap.unsqueeze(1).broadcast_to([P, NT, E])
            V = nc.vector
            for k in range(top):
                step(V.tensor_reduce(best[:, k, :], lg[:, :, :], AX.X, ALU.max))
                if k == 0 and top == 1:
                    step(V.tensor_tensor(tmp[:, :, :], lg[:, :, :], over_experts(best[:, 0, :]), ALU.subtract))
                    nc.vector.memset(total[:, 0:1], 0.0).then_inc(sems["exp_in"], 1)
                    dve.wait_ge(sems["exp_out"], 1)
                    step(V.tensor_reduce(total[:, :], tmp[:, :, :], AX.X, ALU.add))
                    step(V.reciprocal(total[:, :], total[:, :]))
                step(V.tensor_tensor(tmp[:, :, :], lg[:, :, :], over_experts(best[:, k, :]), ALU.is_equal))
                step(V.scalar_tensor_tensor(out=tmp[:, :, :], in0=tmp[:, :, :], scalar=-float(E), in1=over_tokens(iota[:, :]),
                                            op0=ALU.mult, op1=ALU.add))
                step(V.tensor_reduce(index[:, :], tmp[:, :, :], AX.X, ALU.min))
                step(V.tensor_scalar(index[:, :], index[:, :], float(E), None, ALU.add))
                step(V.tensor_tensor(picks[k][:, :, :], over_tokens(iota[:, :]), over_experts(index[:, :]), ALU.is_equal))
                if k + 1 < top:
                    step(V.scalar_tensor_tensor(out=lg[:, :, :], in0=picks[k][:, :, :], scalar=MASKED, in1=lg[:, :, :],
                                                op0=ALU.mult, op1=ALU.add))
            if top == 1:
                V.tensor_copy(member[:, :, :], picks[0][:, :, :]).then_inc(sems["member_ready"], 1)
                step(V.tensor_scalar(r.weight[:, 0, :], total[:, :], core.gates[:, gate:gate + 1], None, ALU.mult))
            else:
                V.tensor_tensor(member[:, :, :], picks[0][:, :, :], picks[1][:, :, :], ALU.add).then_inc(sems["member_ready"], 1)
                V.tensor_tensor(total[:, :], best[:, 1, :], best[:, 0, :], ALU.subtract).then_inc(sems["exp_in"], 1)
                dve.wait_ge(sems["exp_out"], 1)
                step(V.tensor_scalar(index[:, :], total[:, :], 1.0, sum_eps, ALU.add, ALU.add))
                step(V.reciprocal(index[:, :], index[:, :]))
                if gate is not None:
                    step(V.tensor_scalar(index[:, :], index[:, :], core.gates[:, gate:gate + 1], None, ALU.mult))
                step(V.tensor_copy(r.weight[:, 0, :], index[:, :]))
                step(V.tensor_tensor(r.weight[:, 1, :], total[:, :], index[:, :], ALU.mult))
            dve.wait_ge(sems["prefix_ps"], 2)
            tot = ps_total[:, 0:NT * E].rearrange("p (t e) -> p t e", e=E)
            step(V.tensor_copy(tmp[:, :, :], tot))
            src, k, width = tmp, 0, 1
            while width < NT:
                dst = scan[k]
                step(V.tensor_copy(dst[:, 0:width, :], src[:, 0:width, :]))
                step(V.tensor_tensor(dst[:, width:NT, :], src[:, width:NT, :], src[:, 0:NT - width, :], ALU.add))
                src, k, width = dst, 1 - k, 2 * width
            counts = src
            step(V.tensor_tensor(pos[:, :, :], counts[:, :, :], tmp[:, :, :], ALU.subtract))
            step(V.tensor_tensor(pos[:, :, :], pos[:, :, :], ps_before[:, 0:NT * E].rearrange("p (t e) -> p t e", e=E), ALU.add))
            slot_of = scan[k]
            if cap is not None:
                step(V.tensor_scalar(iota[:, :], iota[:, :], float(cap), None, ALU.mult))
                base = iota
            else:
                n = counts[:, NT - 1, :]
                step(V.tensor_tensor(more[:, :, :], n.unsqueeze(2).broadcast_to([P, E, NC]),
                                     starts[:, :].unsqueeze(1).broadcast_to([P, E, NC]), ALU.is_gt))
                step(V.tensor_reduce(chunks[:, :], more[:, :, :], AX.X, ALU.add))
                step(V.tensor_scalar(chunks[:, :], chunks[:, :], float(CHUNK), None, ALU.mult))
                e_src, ke, width = chunks, 0, 1
                while width < E:
                    step(V.tensor_copy(ends[ke][:, 0:width], e_src[:, 0:width]))
                    step(V.tensor_tensor(ends[ke][:, width:E], e_src[:, width:E], e_src[:, 0:E - width], ALU.add))
                    e_src, ke, width = ends[ke], 1 - ke, 2 * width
                step(V.tensor_tensor(more[:, :, :], starts[:, :].unsqueeze(1).broadcast_to([P, E, NC]),
                                     e_src[:, :].unsqueeze(2).broadcast_to([P, E, NC]), ALU.is_ge))
                step(V.tensor_reduce(ce[:, :], more[:, :, :].rearrange("p e c -> p c e"), AX.X, ALU.add))
                step(V.tensor_scalar(ce[:, :], ce[:, :], float(E - 1), None, ALU.min))
                step(V.tensor_copy(r.chunk_expert[:, :], ce[0:1, :]))
                step(V.tensor_tensor(chunks[:, :], e_src[:, :], chunks[:, :], ALU.subtract))
                base = chunks
            step(V.tensor_tensor(slot_of[:, :, :], pos[:, :, :], over_tokens(base[:, :]), ALU.add))
            for k in range(top):
                step(V.tensor_tensor(tmp[:, :, :], slot_of[:, :, :], picks[k][:, :, :], ALU.mult))
                step(V.tensor_reduce(choice_slot[:, :], tmp[:, :, :], AX.X, ALU.add))
                if cap is not None:
                    step(V.tensor_tensor(tmp[:, :, :], pos[:, :, :], picks[k][:, :, :], ALU.mult))
                    step(V.tensor_reduce(choice_pos[:, :], tmp[:, :, :], AX.X, ALU.add))
                    step(V.tensor_scalar(choice_pos[:, :], choice_pos[:, :], float(cap), None, ALU.is_ge))
                    step(V.scalar_tensor_tensor(out=choice_slot[:, :], in0=choice_pos[:, :], scalar=NOWHERE, in1=choice_slot[:, :],
                                                op0=ALU.mult, op1=ALU.add))
                    step(V.tensor_scalar(choice_pos[:, :], choice_pos[:, :], -1.0, 1.0, ALU.mult, ALU.add))
                    step(V.tensor_tensor(r.weight[:, k, :], r.weight[:, k, :], choice_pos[:, :], ALU.mult))
                V.tensor_copy(r.slot[:, k, :], choice_slot[:, :]).then_inc(sems["slots_ready"], 1)
                dve.wait_ge(sems["slots_ready"], k + 1)

def experts(nc, core, name, r, sets, inner, w1_dram, w2_dram, act_func, w3_dram=None, b1_dram=None, b2_dram=None, dynamic=False):
    F = w1_dram.shape[2]
    FC = F // P
    A = CHUNK // P
    PAIR = 2 * inner
    with Phase(nc, name) as ph:
        w1 = ph.sb("w1", [P, 2, F])
        w3 = ph.sb("w3", [P, 2, F]) if w3_dram is not None else None
        w2 = ph.sb("w2", [P, 2, FC, D])
        b1 = ph.sb("b1", [P, 2, FC]) if b1_dram is not None else None
        b2 = ph.sb("b2", [P, 2, D]) if b2_dram is not None else None
        rows = ph.sb("rows", [P, 2, A, D])
        xT = ph.sb("xT", [P, 2, CHUNK])
        hT = ph.sb("hT", [P, 2, FC, CHUNK])
        sT = ph.sb("sT", [P, 2, CHUNK]) if w3_dram is not None else None
        y = ph.sb("y", [P, 2, A, D])
        ps_x = ph.ps("ps_x", [P, CHUNK])
        ps_h = [ph.ps(f"ps_h{k}", [P, 512]) for k in range(4)]
        ps_y = [ph.ps(f"ps_y{k}", [P, 512]) for k in range(A)]
        w_in = [ph.sem("w_in0"), ph.sem("w_in1")]
        rows_in = [ph.sem("rows_in0"), ph.sem("rows_in1")]
        stored = [ph.sem("stored0"), ph.sem("stored1")]
        xT_ps, xT_ready, h_ps, h_ready = ph.sem("xT_ps"), ph.sem("xT_ready"), ph.sem("h_ps"), ph.sem("h_ready")
        s_ready, y_ps, y_ready = ph.sem("s_ready"), ph.sem("y_ps"), ph.sem("y_ready")
        set_dmas = 2 + (w3 is not None) + (b1 is not None) + (b2 is not None)
        in_tiles = core.rows_in.rearrange("(n a p) d -> n p a d", p=P, a=A)
        out_tiles = core.rows_out.rearrange("(n a p) d -> n p a d", p=P, a=A)
        w2_tiles = w2_dram.rearrange("e (f p) d -> e p f d", p=P)
        block = ph.ctx.enter_context(nc.Block())

        def run(eng, one):
            for c in range(PAIR):
                one(0, c)
            with eng.Fori(1, sets // 2 - 1) as u:
                for c in range(PAIR):
                    one(u, c)
            for c in range(PAIR):
                one(sets // 2 - 1, c)

        def set_arrived(eng, u, c):
            if c % inner == 0:
                eng.wait_ge(w_in[c // inner], (u + 1) * (16 * set_dmas))

        def is_last(u, c):
            return isinstance(u, int) and u == sets // 2 - 1 and c == PAIR - 1

        @block.sync
        def _(sp):
            def load_set(u, k):
                if not isinstance(u, int) or u > 0:
                    sp.wait_ge(y_ready, u * PAIR + (k - 1) * inner)
                e = u * 2 + k
                if dynamic:
                    at = r.chunk_expert[0:1, e:e + 1] if isinstance(e, int) else r.chunk_expert[0:1, bass.ts(e, 1)]
                    e = sp.value_load(at, min_val=0, max_val=r.experts - 1)
                sp.dma_start(w1[:, k, :], w1_dram[e, :, :]).then_inc(w_in[k], 16)
                if w3 is not None:
                    sp.dma_start(w3[:, k, :], w3_dram[e, :, :]).then_inc(w_in[k], 16)
                if b1 is not None:
                    sp.dma_start(b1[:, k, :], b1_dram[e, :, :]).then_inc(w_in[k], 16)
                if b2 is not None:
                    sp.dma_start(b2[:, k, :], b2_dram[e, :, :].broadcast_to([P, D])).then_inc(w_in[k], 16)
                sp.dma_start(w2[:, k, :, :], w2_tiles[e, :, :, :]).then_inc(w_in[k], 16)

            def one(u, c):
                if c % inner == 0:
                    load_set(u, c // inner)
                q = u * PAIR + c
                reused(sp, xT_ps, q - 1)
                sp.dma_start(rows[:, c % 2, :, :], in_tiles[q, :, :, :]).then_inc(rows_in[c % 2], 16)
            run(sp, one)

        @block.tensor
        def _(pe):
            def turn(u, c):
                pe.wait_ge(rows_in[c % 2], u * (16 * inner) + 16 * (c // 2 + 1))
                reused(pe, xT_ready, u * PAIR + c)
                for a in range(A):
                    last = nc.tensor.transpose(ps_x[:, a * P:(a + 1) * P], rows[:, c % 2, a, :], core.ident[:, :])
                last.then_inc(xT_ps, 1)

            def one(u, c):
                q, k, b = u * PAIR + c, c // inner, c % 2
                set_arrived(pe, u, c)
                pe.wait_ge(xT_ready, q + 1)
                for f in range(FC):
                    if w3 is None:
                        reused(pe, h_ready, (q - 1) * FC + (f + 1))
                        nc.tensor.matmul(ps_h[f][:, 0:CHUNK], w1[:, k, f * P:(f + 1) * P], xT[:, b, :], start=True, stop=True
                                         ).then_inc(h_ps, 1)
                    else:
                        reused(pe, h_ready, q * FC + (f - 1))
                        nc.tensor.matmul(ps_h[f % 2][:, 0:CHUNK], w1[:, k, f * P:(f + 1) * P], xT[:, b, :], start=True, stop=True)
                        nc.tensor.matmul(ps_h[2 + f % 2][:, 0:CHUNK], w3[:, k, f * P:(f + 1) * P], xT[:, b, :], start=True, stop=True
                                         ).then_inc(h_ps, 1)
                if not is_last(u, c):
                    turn(*((u, c + 1) if c + 1 < PAIR else (u + 1, 0)))
                for f in range(FC):
                    pe.wait_ge(h_ready, q * FC + (f + 1))
                    if f == 0:
                        reused(pe, y_ready, q)
                    for a in range(A):
                        last = nc.tensor.matmul(ps_y[a][:, 0:D], hT[:, b, f, a * P:(a + 1) * P], w2[:, k, f, :],
                                                start=(f == 0), stop=(f == FC - 1))
                last.then_inc(y_ps, 1)
            turn(0, 0)
            run(pe, one)

        @block.scalar
        def _(act):
            def one(u, c):
                q, k, b = u * PAIR + c, c // inner, c % 2
                if b1 is not None:
                    set_arrived(act, u, c)
                for f in range(FC):
                    act.wait_ge(h_ps, q * FC + (f + 1))
                    if w3 is None:
                        if f == 0:
                            reused(act, y_ps, q - 1)
                        bias = {"bias": b1[:, k, f:f + 1]} if b1 is not None else {}
                        nc.scalar.activation(hT[:, b, f, :], ps_h[f][:, 0:CHUNK], act_func, **bias).then_inc(h_ready, 1)
                    else:
                        reused(act, h_ready, q * FC + (f - 1))
                        nc.scalar.activation(sT[:, f % 2, :], ps_h[f % 2][:, 0:CHUNK], act_func).then_inc(s_ready, 1)
            nc.scalar.preload_act_table(act_func)
            run(act, one)

        @block.vector
        def _(dve):
            def copy_x(u, c):
                q = u * PAIR + c
                dve.wait_ge(xT_ps, q + 1)
                reused(dve, h_ps, (q - 1) * FC)
                nc.vector.tensor_copy(xT[:, c % 2, :], ps_x[:, :]).then_inc(xT_ready, 1)

            def one(u, c):
                q, k, b = u * PAIR + c, c // inner, c % 2
                if w3 is not None:
                    for f in range(FC):
                        dve.wait_ge(s_ready, q * FC + (f + 1))
                        if f == 0:
                            reused(dve, y_ps, q - 1)
                        nc.vector.tensor_tensor(hT[:, b, f, :], sT[:, f % 2, :], ps_h[2 + f % 2][:, 0:CHUNK], ALU.mult
                                                ).then_inc(h_ready, 1)
                if not is_last(u, c):
                    copy_x(*((u, c + 1) if c + 1 < PAIR else (u + 1, 0)))
                if b2 is not None:
                    set_arrived(dve, u, c)
                dve.wait_ge(y_ps, q + 1)
                reused(dve, stored[b], u * (16 * inner) + 16 * (c // 2))
                for a in range(A):
                    if b2 is not None:
                        last = nc.vector.tensor_tensor(y[:, b, a, :], ps_y[a][:, 0:D], b2[:, k, :], ALU.add)
                    else:
                        last = nc.vector.tensor_copy(y[:, b, a, :], ps_y[a][:, 0:D])
                last.then_inc(y_ready, 1)
            copy_x(0, 0)
            run(dve, one)

        @block.gpsimd
        def _(pool):
            def one(u, c):
                q = u * PAIR + c
                pool.wait_ge(y_ready, q + 1)
                pool.dma_start(out_tiles[q, :, :, :], y[:, c % 2, :, :]).then_inc(stored[c % 2], 16)
            run(pool, one)
            for b in range(2):
                pool.wait_ge(stored[b], 16 * (sets * inner // 2))


def combine(nc, core, name, r, norm=None, gate=None):
    top = r.top
    GROUP = 8
    NG = NT // GROUP
    with Phase(nc, name) as ph:
        got = ph.sb("got", [P, top, NT, D])
        z = ph.sb("z", [P, 2, D])
        lnp = ph.sb("lnp", [P, 2, D])
        lnp_in, scaled, normed, zeroed = ph.sem("lnp_in"), ph.sem("scaled"), ph.sem("normed"), ph.sem("zeroed")
        gathered = [ph.sem(f"gathered{g}") for g in range(NG)]
        added, summed = ph.sem("added"), ph.sem("summed")
        root_on_scalar, root_on_vector = row_statistics(nc, ph, core)
        block = ph.ctx.enter_context(nc.Block())

        @block.sync
        def _(sp):
            if norm is not None:
                for k in range(2):
                    sp.dma_start(lnp[:, k, :], norm[k].rearrange("(a n) -> a n", a=1).broadcast_to([P, D])).then_inc(lnp_in, 16)

        @block.gpsimd
        def _(pool):
            pool.wait_ge(zeroed, 1)
            for t in range(NT):
                for k in range(top):
                    pool.indirect_dma_start(
                        out=got[:, k, t, :], out_offset=None, in_=core.rows_out[0:r.rows, :],
                        in_offset=bass.IndirectOffsetOnAxis(ap=r.slot[:, k, t:t + 1], axis=0),
                        bounds_check=r.rows - 1, oob_is_err=False).then_inc(gathered[t // GROUP], 16)

        @block.scalar
        def _(act):
            if norm is not None:
                root_on_scalar(act)

        @block.vector
        def _(dve):
            nc.vector.memset(got[:, :, :, :], 0.0).then_inc(zeroed, 1)
            dest = core.x if norm is None else got[:, 0, :, :]
            for g in range(NG):
                dve.wait_ge(gathered[g], 16 * GROUP * top)
                with dve.Fori(g * GROUP, (g + 1) * GROUP) as t:
                    if norm is None:
                        nc.vector.scalar_tensor_tensor(out=core.x[:, t, :], in0=got[:, 0, t, :], scalar=r.weight[:, 0, bass.ts(t, 1)],
                                                       in1=core.x[:, t, :], op0=ALU.mult, op1=ALU.add).then_inc(added, 1)
                    else:
                        nc.vector.tensor_scalar(got[:, 0, t, :], got[:, 0, t, :], r.weight[:, 0, bass.ts(t, 1)], None, ALU.mult
                                                ).then_inc(added, 1)
                n = (g + 1) * GROUP + g * GROUP * (top - 1)
                dve.wait_ge(added, n)
                if top == 2:
                    with dve.Fori(g * GROUP, (g + 1) * GROUP) as t:
                        out = core.x[:, t, :] if norm is None else got[:, 0, t, :]
                        nc.vector.scalar_tensor_tensor(out=out, in0=got[:, 1, t, :], scalar=r.weight[:, 1, bass.ts(t, 1)],
                                                       in1=out, op0=ALU.mult, op1=ALU.add).then_inc(added, 1)
                    dve.wait_ge(added, n + GROUP)
                with dve.Fori(g * GROUP, (g + 1) * GROUP) as t:
                    src = core.x[:, t, :] if norm is None else got[:, 0, t, :]
                    nc.vector.bn_stats(core.bn[:, t, :], src).then_inc(summed, 1)
            if norm is not None:
                dve.wait_ge(summed, NT)
                root_on_vector(dve)
                dve.wait_ge(lnp_in, 32)
                for k in range(2):
                    nc.vector.tensor_scalar(lnp[:, k, :], lnp[:, k, :], core.gates[:, gate:gate + 1], None, ALU.mult).then_inc(scaled, 1)
                dve.wait_ge(scaled, 2)

                def one(t):
                    nc.vector.tensor_scalar(z[:, 0, :], got[:, 0, t, :], core.mean[:, bass.ts(t, 1)], core.rstd[:, bass.ts(t, 1)],
                                            ALU.subtract, ALU.mult).then_inc(normed, 1)
                    dve.wait_ge(normed, t * 4 + 1)
                    nc.vector.tensor_tensor(z[:, 0, :], z[:, 0, :], lnp[:, 0, :], ALU.mult).then_inc(normed, 1)
                    dve.wait_ge(normed, t * 4 + 2)
                    nc.vector.tensor_tensor(z[:, 1, :], z[:, 0, :], lnp[:, 1, :], ALU.add).then_inc(normed, 1)
                    dve.wait_ge(normed, t * 4 + 3)
                    nc.vector.tensor_tensor(core.x[:, t, :], z[:, 1, :], core.x[:, t, :], ALU.add).then_inc(normed, 1)
                one(0)
                with dve.Fori(1, NT) as t:
                    one(t)
                dve.wait_ge(normed, 4 * NT)
                with dve.Fori(0, NT) as t:
                    nc.vector.bn_stats(core.bn[:, t, :], core.x[:, t, :]).then_inc(summed, 1)


def ternary_ffn(nc, core, name, gate, wfcT_dram, wprojT_dram, ln_w, ln_b):
    F = wfcT_dram.shape[1]
    FC = F // P
    with Phase(nc, name) as ph:
        wfc = ph.sb("wfc", [P, F])
        wproj = ph.sb("wproj", [P, FC, D])
        pos = ph.sb("pos", [P, F])
        neg = ph.sb("neg", [P, F])
        q_fc = ph.sb("q_fc", [P, F])
        q_proj = ph.sb("q_proj", [P, FC, D])
        w_out = ph.sb("w_out", [P, FC, D])
        lnw = ph.sb("lnw", [P, FC])
        lnb = ph.sb("lnb", [P, FC])
        shift = ph.sb("shift", [1, D])
        sums = ph.sb("sums", [P, 2])
        thr = ph.sb("thr", [P, 4])
        ones = ph.sb("ones", [P, P])
        half = ph.sb("half", [P, 1])
        xn = ph.sb("xn", [P, 2, D])
        xnT = ph.sb("xnT", [P, 2, P])
        h = ph.sb("h", [P, 2, F])
        hn = ph.sb("hn", [P, 2, F])
        hT = ph.sb("hT", [P, 2, F])
        bn = ph.sb("bn", [P, 2, 6])
        mv = ph.sb("mv", [P, 2, 2])
        ve = ph.sb("ve", [P, 2, 1])
        rs = ph.sb("rs", [P, 2, 1])
        ps_x = [ph.ps(f"ps_x{k}", [P, P]) for k in range(2)]
        ps_h = [ph.ps(f"ps_h{k}", [P, F]) for k in range(2)]
        ps_t = [ph.ps(f"ps_t{k}", [P, F]) for k in range(2)]
        ps_y = [ph.ps(f"ps_y{k}", [P, D]) for k in range(2)]
        s = {n: ph.sem(n) for n in ("w_in filled summed0 sums_ps signs quantised shift_ps shift_ready xn_ready xnT_ps xnT_ready h_ps "
                                    "h_ready bn_ready mv_ready ve_ready rs_ready hn_ready hT_ps hT_ready y_ps x_ready summed").split()}
        root_on_scalar, root_on_vector = row_statistics(nc, ph, core)
        block = ph.ctx.enter_context(nc.Block())

        def pairs(eng, step, first=0, last=NT):
            step(first, 0)
            step(first + 1, 1)
            with eng.Fori(first // 2 + 1, last // 2) as u:
                step(u * 2, 0)
                step(u * 2 + 1, 1)

        @block.sync
        def _(sp):
            sp.dma_start(wfc[:, :], wfcT_dram).then_inc(s["w_in"], 16)
            sp.dma_start(wproj[:, :, :], wprojT_dram.rearrange("(f p) d -> p f d", p=P)).then_inc(s["w_in"], 16)
            sp.dma_start(lnw[:, :], ln_w).then_inc(s["w_in"], 16)
            sp.dma_start(lnb[:, :], ln_b).then_inc(s["w_in"], 16)

        @block.gpsimd
        def _(pool):
            pool.memset(ones[:, :], 1.0).then_inc(s["filled"], 1)
            pool.memset(half[:, :], -0.5).then_inc(s["filled"], 1)
            pool.wait_ge(s["filled"], 2)

            def one(t, k):
                pool.wait_ge(s["ve_ready"], t + 1)
                if not isinstance(t, int) or t >= 2:
                    pool.wait_ge(s["hn_ready"], t - 1)
                pool.tensor_tensor(rs[:, k, :], ve[:, k, :], half[:, :], ALU.pow).then_inc(s["rs_ready"], 1)
            pairs(pool, one)

        @block.tensor
        def _(pe):
            pe.wait_ge(s["filled"], 2)
            pe.wait_ge(s["summed0"], 2)
            nc.tensor.matmul(ps_y[0][:, 0:2], ones[:, :], sums[:, :], start=True, stop=True).then_inc(s["sums_ps"], 1)
            pe.wait_ge(s["quantised"], 3)
            for f in range(FC):
                last = nc.tensor.matmul(ps_y[0][0:1, 0:D], lnb[:, f:f + 1], q_proj[:, f, :], start=(f == 0), stop=(f == FC - 1))
            last.then_inc(s["shift_ps"], 1)
            pe.wait_ge(s["shift_ready"], 1)

            def front(t, k):
                pe.wait_ge(s["xn_ready"], t + 1)
                reused(pe, s["xnT_ready"], t - 1)
                nc.tensor.transpose(ps_x[k][:, :], xn[:, k, :], core.ident[:, :]).then_inc(s["xnT_ps"], 1)
                pe.wait_ge(s["xnT_ready"], t + 1)
                reused(pe, s["h_ready"], t - 1)
                nc.tensor.matmul(ps_h[k][:, :], xnT[:, k, :], q_fc[:, :], start=True, stop=True).then_inc(s["h_ps"], 1)

            def back(t, k):
                pe.wait_ge(s["hn_ready"], t + 1)
                reused(pe, s["hT_ready"], t - 1)
                for f in range(FC):
                    last = nc.tensor.transpose(ps_t[k][:, f * P:(f + 1) * P], hn[:, k, f * P:(f + 1) * P], core.ident[:, :])
                last.then_inc(s["hT_ps"], 1)
                pe.wait_ge(s["hT_ready"], t + 1)
                reused(pe, s["x_ready"], t - 1)
                for f in range(FC):
                    nc.tensor.matmul(ps_y[k][:, :], hT[:, k, f * P:(f + 1) * P], w_out[:, f, :], start=(f == 0), stop=False)
                nc.tensor.matmul(ps_y[k][:, :], core.ones[:, :], shift[:, :], start=False, stop=True).then_inc(s["y_ps"], 1)

            front(0, 0)
            front(1, 1)
            back(0, 0)
            with pe.Fori(1, NT // 2) as u:
                front(u * 2, 0)
                back(u * 2 - 1, 1)
                front(u * 2 + 1, 1)
                back(u * 2, 0)
            back(NT - 1, 1)

        @block.scalar
        def _(act):
            root_on_scalar(act)

            def front(t, k):
                act.wait_ge(s["xnT_ps"], t + 1)
                reused(act, s["h_ps"], t - 1)
                nc.scalar.copy(xnT[:, k, :], ps_x[k][:, :]).then_inc(s["xnT_ready"], 1)
                act.wait_ge(s["h_ps"], t + 1)
                reused(act, s["hn_ready"], t - 1)
                nc.scalar.activation(h[:, k, :], ps_h[k][:, :], ACT.Gelu).then_inc(s["h_ready"], 1)

            def back(t, k):
                act.wait_ge(s["hT_ps"], t + 1)
                reused(act, s["y_ps"], t - 1)
                nc.scalar.copy(hT[:, k, :], ps_t[k][:, :]).then_inc(s["hT_ready"], 1)
            nc.scalar.preload_act_table(ACT.Gelu)
            front(0, 0)
            front(1, 1)
            back(0, 0)
            with act.Fori(1, NT // 2) as u:
                front(u * 2, 0)
                back(u * 2 - 1, 1)
                front(u * 2 + 1, 1)
                back(u * 2, 0)
            back(NT - 1, 1)

        @block.vector
        def _(dve):
            V = nc.vector
            root_on_vector(dve)
            dve.wait_ge(s["w_in"], 64)
            for k, w in enumerate((wfc[:, :], wproj[:, :, :].rearrange("p f d -> p (f d)"))):
                V.tensor_reduce(sums[:, k:k + 1], w, AX.X, ALU.add, apply_absolute_value=True).then_inc(s["summed0"], 1)
            dve.wait_ge(s["sums_ps"], 1)
            V.tensor_scalar(thr[:, 0:2], ps_y[0][:, 0:2], 1.0 / (P * F), 1e-6, ALU.mult, ALU.add).then_inc(s["signs"], 1)
            dve.wait_ge(s["signs"], 1)
            V.tensor_scalar(thr[:, 2:4], thr[:, 0:2], -0.5, None, ALU.mult).then_inc(s["signs"], 1)
            dve.wait_ge(s["signs"], 2)
            V.tensor_scalar(thr[:, 0:2], thr[:, 0:2], 0.5, None, ALU.mult).then_inc(s["signs"], 1)
            dve.wait_ge(s["signs"], 3)
            for k, (w, q) in enumerate(((wfc[:, :], q_fc[:, :]), (wproj[:, :, :].rearrange("p f d -> p (f d)"), q_proj[:, :, :].rearrange("p f d -> p (f d)")))):
                n = 3 + 2 * k
                reused(dve, s["quantised"], k)
                V.tensor_scalar(pos[:, :], w, thr[:, k:k + 1], None, ALU.is_gt).then_inc(s["signs"], 1)
                V.tensor_scalar(neg[:, :], w, thr[:, 2 + k:3 + k], None, ALU.is_lt).then_inc(s["signs"], 1)
                dve.wait_ge(s["signs"], n + 2)
                V.tensor_tensor(q, pos[:, :], neg[:, :], ALU.subtract).then_inc(s["quantised"], 1)
            dve.wait_ge(s["quantised"], 2)
            V.tensor_tensor(w_out[:, :, :], q_proj[:, :, :], lnw[:, :].unsqueeze(2).broadcast_to([P, FC, D]), ALU.mult).then_inc(s["quantised"], 1)
            dve.wait_ge(s["shift_ps"], 1)
            V.tensor_copy(shift[:, :], ps_y[0][0:1, 0:D]).then_inc(s["shift_ready"], 1)

            def normalise(t, k):
                reused(dve, s["xnT_ps"], t - 1)
                V.tensor_scalar(xn[:, k, :], core.x[:, t, :], core.mean[:, bass.ts(t, 1)], core.rstd[:, bass.ts(t, 1)],
                                ALU.subtract, ALU.mult).then_inc(s["xn_ready"], 1)

            def variance(t, k):
                dve.wait_ge(s["h_ready"], t + 1)
                V.bn_stats(bn[:, k, :], h[:, k, :]).then_inc(s["bn_ready"], 1)
                dve.wait_ge(s["w_in"], 64)
                dve.wait_ge(s["bn_ready"], t + 1)
                V.bn_aggr(mv[:, k, :], bn[:, k, :]).then_inc(s["mv_ready"], 1)
                dve.wait_ge(s["mv_ready"], t + 1)
                V.tensor_scalar(ve[:, k, :], mv[:, k, 1:2], LN_EPS, None, ALU.add).then_inc(s["ve_ready"], 1)

            def inner(t, k):
                dve.wait_ge(s["rs_ready"], t + 1)
                reused(dve, s["hT_ps"], t - 1)
                V.tensor_scalar(hn[:, k, :], h[:, k, :], mv[:, k, 0:1], rs[:, k, :], ALU.subtract, ALU.mult).then_inc(s["hn_ready"], 1)

            def residual(t, k):
                dve.wait_ge(s["y_ps"], t + 1)
                V.scalar_tensor_tensor(out=core.x[:, t, :], in0=ps_y[k][:, :], scalar=core.gates[:, gate:gate + 1],
                                       in1=core.x[:, t, :], op0=ALU.mult, op1=ALU.add).then_inc(s["x_ready"], 1)
                dve.wait_ge(s["x_ready"], t + 1)
                dve.wait_ge(s["w_in"], 64)
                V.bn_stats(core.bn[:, t, :], core.x[:, t, :]).then_inc(s["summed"], 1)

            normalise(0, 0)
            normalise(1, 1)
            variance(0, 0)
            inner(0, 0)
            normalise(2, 0)
            variance(1, 1)
            inner(1, 1)
            residual(0, 0)
            with dve.Fori(1, NT // 2 - 1) as u:
                normalise(u * 2 + 1, 1)
                variance(u * 2, 0)
                inner(u * 2, 0)
                residual(u * 2 - 1, 1)
                normalise(u * 2 + 2, 0)
                variance(u * 2 + 1, 1)
                inner(u * 2 + 1, 1)
                residual(u * 2, 0)
            normalise(NT - 1, 1)
            variance(NT - 2, 0)
            inner(NT - 2, 0)
            residual(NT - 3, 1)
            variance(NT - 1, 1)
            inner(NT - 1, 1)
            residual(NT - 2, 0)
            residual(NT - 1, 1)


def attention1(nc, core, name, gate, wT_dram, b_dram, ctx_dram, pad_dram):
    G = 4
    NSTEP = NT // G
    with Phase(nc, name) as ph:
        wT = ph.sb("wT", [P, D])
        b = ph.sb("b", [P, 1])
        pad = ph.sb("pad", [P, NT, P], U8)
        neg = ph.sb("neg", [P, NT, P])
        across = ph.sb("across", [P, P])
        yp = ph.sb("yp", [P, T])
        cx = ph.sb("cx", [P, NT, D])
        xn = ph.sb("xn", [P, G, D])
        xnT = ph.sb("xnT", [P, G * P])
        xp = ph.sb("xp", [P, G * P])
        s1 = ph.sb("s1", [P, G, P])
        nmx = ph.sb("nmx", [P, G])
        p = ph.sb("p", [P, G, P])
        den = ph.sb("den", [P, G])
        rg = ph.sb("rg", [P, G])
        rgate = ph.sb("rgate", [P, G])
        pT = ph.sb("pT", [P, G * P])
        ps_x, ps_p, ps_s, ps_t, ps_o = (ph.ps(n, [P, G * P]) for n in ("ps_x", "ps_p", "ps_s", "ps_t", "ps_o"))
        ps_c = [ph.ps(f"ps_c{k}", [P, 512]) for k in range(2)]
        s = {n: ph.sem(n) for n in ("w_in pad_in cx_in filled across_ready neg_ready c_ps yp_ready xn_ready xnT_ps xnT_ready p_ps "
                                    "xp_ready s_ps s1_ready max_ready p_ready pT_ps pT_ready o_ps den_ready rg_ready x_ready summed").split()}
        root_on_scalar, root_on_vector = row_statistics(nc, ph, core)
        block = ph.ctx.enter_context(nc.Block())

        @block.sync
        def _(sp):
            sp.dma_start(wT[:, :], wT_dram).then_inc(s["w_in"], 16)
            sp.dma_start(b[:, :], b_dram.rearrange("(r a) -> r a", a=1)).then_inc(s["w_in"], 16)
            src = pad_dram.rearrange("(n b) k -> n (b k)", b=2).rearrange("(a n) k -> a n k", a=1)
            sp.dma_start(pad[:, :, :], src.broadcast_to([P, NT, P])).then_inc(s["pad_in"], 16)
            sp.dma_start(cx[:, :, :], flat(ctx_dram).rearrange("(n p) d -> p n d", p=P)).then_inc(s["cx_in"], 16)

        @block.gpsimd
        def _(pool):
            pool.memset(across[:, :], 0.0).then_inc(s["filled"], 1)
            pool.wait_ge(s["filled"], 1)
            for k in range(2):
                pool.memset(across[64 * k:64 * k + 64, 64 * (1 - k):64 * (1 - k) + 64], MASKED).then_inc(s["across_ready"], 1)

        @block.tensor
        def _(pe):
            pe.wait_ge(s["w_in"], 32)
            for c in range(T // 512):
                reused(pe, s["yp_ready"], c - 1)
                nc.tensor.matmul(ps_c[c % 2][:, :], wT[:, :], core.ctxT[:, c * 512:(c + 1) * 512], start=True, stop=True).then_inc(s["c_ps"], 1)

            def front(t):
                pe.wait_ge(s["xn_ready"], t * G + G)
                reused(pe, s["xnT_ready"], t)
                for g in range(G):
                    last = nc.tensor.transpose(ps_x[:, g * P:(g + 1) * P], xn[:, g, :], core.ident[:, :])
                last.then_inc(s["xnT_ps"], 1)
                pe.wait_ge(s["xnT_ready"], t + 1)
                reused(pe, s["xp_ready"], t)
                nc.tensor.matmul(ps_p[:, :], wT[:, :], xnT[:, :], start=True, stop=True).then_inc(s["p_ps"], 1)

            def scores(t):
                pe.wait_ge(s["xp_ready"], t + 1)
                reused(pe, s["s1_ready"], t)
                for g in range(G):
                    last = nc.tensor.matmul(ps_s[:, g * P:(g + 1) * P], xp[:, g * P:(g + 1) * P], yp[:, bass.ts(t * G + g, P)], start=True, stop=True)
                last.then_inc(s["s_ps"], 1)

            def values(t):
                pe.wait_ge(s["p_ready"], t * G + G)
                reused(pe, s["pT_ready"], t)
                for g in range(G):
                    last = nc.tensor.transpose(ps_t[:, g * P:(g + 1) * P], p[:, g, :], core.ident[:, :])
                last.then_inc(s["pT_ps"], 1)
                pe.wait_ge(s["pT_ready"], t + 1)
                reused(pe, s["x_ready"], t * G)
                for g in range(G):
                    last = nc.tensor.matmul(ps_o[:, g * P:(g + 1) * P], pT[:, g * P:(g + 1) * P], cx[:, t * G + g, :], start=True, stop=True)
                last.then_inc(s["o_ps"], 1)
            pe.wait_ge(s["yp_ready"], T // 512)
            pe.wait_ge(s["cx_in"], 16)
            front(0)
            scores(0)
            front(1)
            values(0)
            with pe.Fori(1, NSTEP - 1) as t:
                scores(t)
                front(t + 1)
                values(t)
            scores(NSTEP - 1)
            values(NSTEP - 1)

        @block.scalar
        def _(act):
            root_on_scalar(act)
            act.wait_ge(s["w_in"], 32)
            for c in range(T // 512):
                act.wait_ge(s["c_ps"], c + 1)
                nc.scalar.activation(yp[:, c * 512:(c + 1) * 512], ps_c[c % 2][:, :], ACT.Relu, bias=b[:, :]).then_inc(s["yp_ready"], 1)
            nc.scalar.preload_act_table(ACT.Exp)

            def front(t):
                act.wait_ge(s["xnT_ps"], t + 1)
                reused(act, s["p_ps"], t)
                nc.scalar.copy(xnT[:, :], ps_x[:, :]).then_inc(s["xnT_ready"], 1)
                act.wait_ge(s["p_ps"], t + 1)
                reused(act, s["s_ps"], t)
                nc.scalar.activation(xp[:, :], ps_p[:, :], ACT.Relu, bias=b[:, :]).then_inc(s["xp_ready"], 1)

            def exponent(t):
                act.wait_ge(s["max_ready"], t + 1)
                reused(act, s["pT_ps"], t)
                reused(act, s["rg_ready"], t)
                for g in range(G):
                    nc.scalar.activation(p[:, g, :], s1[:, g, :], ACT.Exp, bias=nmx[:, g:g + 1], accum_out=den[:, g:g + 1]).then_inc(s["p_ready"], 1)

            def turned(t):
                act.wait_ge(s["pT_ps"], t + 1)
                reused(act, s["o_ps"], t)
                nc.scalar.copy(pT[:, :], ps_t[:, :]).then_inc(s["pT_ready"], 1)
            front(0)
            exponent(0)
            front(1)
            turned(0)
            with act.Fori(1, NSTEP - 1) as t:
                exponent(t)
                front(t + 1)
                turned(t)
            exponent(NSTEP - 1)
            turned(NSTEP - 1)

        @block.vector
        def _(dve):
            V = nc.vector
            root_on_vector(dve)
            dve.wait_ge(s["pad_in"], 16)
            dve.wait_ge(s["across_ready"], 2)
            V.scalar_tensor_tensor(out=neg[:, :, :], in0=pad[:, :, :], scalar=MASKED, in1=across[:, :].unsqueeze(1).broadcast_to([P, NT, P]),
                                   op0=ALU.mult, op1=ALU.add).then_inc(s["neg_ready"], 1)
            dve.wait_ge(s["neg_ready"], 1)

            def normalise(t):
                reused(dve, s["xnT_ps"], t)
                for g in range(G):
                    at = bass.ts(t * G + g, 1)
                    V.tensor_scalar(xn[:, g, :], core.x[:, t * G + g, :], core.mean[:, at], core.rstd[:, at],
                                    ALU.subtract, ALU.mult).then_inc(s["xn_ready"], 1)

            def softmax(t):
                dve.wait_ge(s["s_ps"], t + 1)
                reused(dve, s["p_ready"], t * G)
                V.tensor_tensor(s1[:, :, :], ps_s[:, :].rearrange("p (g k) -> p g k", g=G), neg[:, bass.ts(t, G), :], ALU.add).then_inc(s["s1_ready"], 1)
                dve.wait_ge(s["s1_ready"], t + 1)
                V.tensor_reduce(nmx[:, :], s1[:, :, :], AX.X, ALU.max, negate=True).then_inc(s["max_ready"], 1)

            def residual(t):
                dve.wait_ge(s["p_ready"], t * G + G)
                reused(dve, s["rg_ready"], t)
                V.reciprocal(rg[:, :], den[:, :]).then_inc(s["den_ready"], 1)
                dve.wait_ge(s["den_ready"], t + 1)
                reused(dve, s["x_ready"], t * G)
                V.tensor_scalar(rgate[:, :], rg[:, :], core.gates[:, gate:gate + 1], None, ALU.mult).then_inc(s["rg_ready"], 1)
                dve.wait_ge(s["rg_ready"], t + 1)
                dve.wait_ge(s["o_ps"], t + 1)
                for g in range(G):
                    V.scalar_tensor_tensor(out=core.x[:, t * G + g, :], in0=ps_o[:, g * P:(g + 1) * P], scalar=rgate[:, g:g + 1],
                                           in1=core.x[:, t * G + g, :], op0=ALU.mult, op1=ALU.add).then_inc(s["x_ready"], 1)
                dve.wait_ge(s["x_ready"], t * G + G)
                for g in range(G):
                    dve.wait_ge(s["pad_in"], 16)
                    V.bn_stats(core.bn[:, t * G + g, :], core.x[:, t * G + g, :]).then_inc(s["summed"], 1)
            normalise(0)
            softmax(0)
            normalise(1)
            residual(0)
            with dve.Fori(1, NSTEP - 1) as t:
                softmax(t)
                normalise(t + 1)
                residual(t)
            softmax(NSTEP - 1)
            residual(NSTEP - 1)


def linear_attention(nc, core, name, gate, wq_dram, wkv_dram, null_kv, lnq_g, lnq_b, lno_g, lno_b, wout_dram):
    HD = 64
    H = 8
    I = H * HD
    J = I // P
    with Phase(nc, name) as ph:
        wq = ph.sb("wq", [P, I])
        wkv = ph.sb("wkv", [P, 2 * I])
        wout = ph.sb("wout", [P, J, D])
        w_out = ph.sb("w_out", [P, J, D])
        lq = ph.sb("lq", [P, 2, I])
        log = ph.sb("log", [P, J])
        lob = ph.sb("lob", [P, J])
        shift = ph.sb("shift", [1, D])
        nk = ph.sb("nk", [P, 1])
        nv = ph.sb("nv", [P, HD])
        half = ph.sb("half", [P, 1])
        xn = ph.sb("xn", [P, D])
        xnT = ph.sb("xnT", [P, P])
        cT = ph.sb("cT", [P, P])
        bn = ph.sb("bn", [P, 6])
        mv = ph.sb("mv", [P, 2])
        ve = ph.sb("ve", [P, 1])
        rs = ph.sb("rs", [P, 1])
        qn = ph.sb("qn", [P, I])
        qg = ph.sb("qg", [P, I])
        qb = ph.sb("qb", [P, H, HD])
        mq = ph.sb("mq", [P, H])
        qs = ph.sb("qs", [P, H, HD])
        pq = ph.sb("pq", [P, H, HD])
        sq = ph.sb("sq", [P, H])
        rq = ph.sb("rq", [P, H])
        mk0 = ph.sb("mk0", [P, J, 2])
        mk = ph.sb("mk", [P, J, 2])
        kc = ph.sb("kc", [P, J, 2, S])
        ek = ph.sb("ek", [P, J, 2, S])
        dn = ph.sb("dn", [P, J, 2])
        en = ph.sb("en", [P, J, 2])
        sk = ph.sb("sk", [P, J, 2])
        sk2 = ph.sb("sk2", [P, J, 2])
        rk = ph.sb("rk", [P, J, 2])
        kS = ph.sb("kS", [P, I])
        v = ph.sb("v", [P, I])
        nvt = ph.sb("nvt", [P, 2, J, HD])
        cmb = ph.sb("cmb", [P, 2, J, P])
        qT = ph.sb("qT", [P, J, 2, S])
        o1 = ph.sb("o1", [P, H, HD])
        bo = ph.sb("bo", [P, 6])
        mo = ph.sb("mo", [P, 2])
        vo = ph.sb("vo", [P, 1])
        ro = ph.sb("ro", [P, 1])
        on = ph.sb("on", [P, I])
        oT = ph.sb("oT", [P, I])
        ps_q, ps_k, ps_v, ps_o = (ph.ps(n, [P, I]) for n in ("ps_q", "ps_k", "ps_v", "ps_o"))
        ps_cm = [ph.ps(f"ps_cm{b}", [P, J, P]) for b in range(2)]
        ps_x, ps_y = ph.ps("ps_x", [P, P]), ph.ps("ps_y", [P, D])
        s = {n: ph.sem(n) for n in (
            "w_in filled folded shift_ps shift_ready xn_ready xnT_ps xnT_ready cT_ready q_ps k_ps v_ps bn_ready mv_ready ve_ready "
            "rs_ready qn_ready qg_ready qb_ready mq_ready qs_ready pq_ready sq_ready rq_ready qT_ps qT_ready mk0_ready mk_ready "
            "kc_ready dn_ready en_ready ek_ready sk_ready sk2_ready rk_ready kS_ps kS_ready v_ready nvt_ready cm_ps cmb_ready "
            "o_ps o1_ready bo_ready mo_ready vo_ready ro_ready on_ready oT_ps oT_ready y_ps x_ready summed").split()}
        root_on_scalar, root_on_vector = row_statistics(nc, ph, core)
        block = ph.ctx.enter_context(nc.Block())
        W_DMAS = 11

        def tiles(eng, step):
            step(0)
            with eng.Fori(1, NT - 1) as t:
                step(t)
            step(NT - 1)

        def is_last(t):
            return isinstance(t, int) and t == NT - 1

        @block.sync
        def _(sp):
            def load(dst, src):
                sp.dma_start(dst, src).then_inc(s["w_in"], 16)
            load(wq[:, :], wq_dram)
            load(wkv[:, :], wkv_dram)
            load(wout[:, :, :], wout_dram.rearrange("(j p) d -> p j d", p=P))
            load(lq[:, 0, :], lnq_g.rearrange("(a n) -> a n", a=1).broadcast_to([P, I]))
            load(lq[:, 1, :], lnq_b.rearrange("(a n) -> a n", a=1).broadcast_to([P, I]))
            load(log[:, :], lno_g)
            load(lob[:, :], lno_b)
            for b in range(2):
                load(nk[64 * b:64 * b + 64, :], null_kv[0:1, :].rearrange("a d -> d a"))
                load(nv[64 * b:64 * b + 64, :], null_kv[1:2, :].broadcast_to([64, HD]))

        @block.gpsimd
        def _(pool):
            pool.memset(half[:, :], -0.5).then_inc(s["filled"], 1)
            pool.memset(cmb[:, :, :, :], 0.0).then_inc(s["filled"], 1)
            pool.wait_ge(s["filled"], 2)
            pool.wait_ge(s["w_in"], 16 * W_DMAS)

            def context(t):
                reused(pool, s["v_ps"], t)
                pool.tensor_copy(cT[:, :], core.ctxT[:, bass.ts(t, P)]).then_inc(s["cT_ready"], 1)

            def step(t):
                pool.wait_ge(s["ve_ready"], t + 1)
                pool.tensor_tensor(rs[:, :], ve[:, :], half[:, :], ALU.pow).then_inc(s["rs_ready"], 1)
                pool.wait_ge(s["qn_ready"], t + 1)
                pool.tensor_tensor(qg[:, :], qn[:, :], lq[:, 0, :], ALU.mult).then_inc(s["qg_ready"], 1)
                pool.wait_ge(s["qg_ready"], t + 1)
                reused(pool, s["qs_ready"], t)
                pool.tensor_tensor(qb[:, :, :].rearrange("p h d -> p (h d)"), qg[:, :], lq[:, 1, :], ALU.add).then_inc(s["qb_ready"], 1)
                pool.wait_ge(s["en_ready"], t + 1)
                reused(pool, s["cmb_ready"], 2 * t)
                pool.tensor_tensor(nvt[:, :, :, :], en[:, :, :].rearrange("p j b -> p b j").unsqueeze(3).broadcast_to([P, 2, J, HD]),
                                   nv[:, :].unsqueeze(1).unsqueeze(1).broadcast_to([P, 2, J, HD]), ALU.mult).then_inc(s["nvt_ready"], 1)
                if not is_last(t):
                    context(t + 1)
                pool.wait_ge(s["vo_ready"], t + 1)
                pool.tensor_tensor(ro[:, :], vo[:, :], half[:, :], ALU.pow).then_inc(s["ro_ready"], 1)
            context(0)
            tiles(pool, step)

        @block.tensor
        def _(pe):
            pe.wait_ge(s["w_in"], 16 * W_DMAS)
            for j in range(J):
                last = nc.tensor.matmul(ps_y[0:1, :], lob[:, j:j + 1], wout[:, j, :], start=(j == 0), stop=(j == J - 1))
            last.then_inc(s["shift_ps"], 1)
            pe.wait_ge(s["shift_ready"], 1)
            pe.wait_ge(s["folded"], 1)

            def front(t):
                pe.wait_ge(s["xn_ready"], t + 1)
                reused(pe, s["xnT_ready"], t)
                nc.tensor.transpose(ps_x[:, :], xn[:, :], core.ident[:, :]).then_inc(s["xnT_ps"], 1)
                pe.wait_ge(s["cT_ready"], t + 1)
                reused(pe, s["kS_ready"], t)
                for j in range(J):
                    last = nc.tensor.matmul(ps_k[:, j * P:(j + 1) * P], wkv[:, j * P:(j + 1) * P], cT[:, :], start=True, stop=True)
                last.then_inc(s["k_ps"], 1)
                pe.wait_ge(s["xnT_ready"], t + 1)
                reused(pe, s["qT_ready"], t)
                nc.tensor.matmul(ps_q[:, :], xnT[:, :], wq[:, :], start=True, stop=True).then_inc(s["q_ps"], 1)
                reused(pe, s["v_ready"], t)
                nc.tensor.matmul(ps_v[:, :], cT[:, :], wkv[:, I:2 * I], start=True, stop=True).then_inc(s["v_ps"], 1)

            def step(t):
                pe.wait_ge(s["ek_ready"], t + 1)
                for j in range(J):
                    last = nc.tensor.transpose(ps_k[:, j * P:(j + 1) * P], ek[:, j, :, :].rearrange("p b k -> p (b k)"), core.ident[:, :])
                last.then_inc(s["kS_ps"], 1)
                pe.wait_ge(s["kS_ready"], t + 1)
                pe.wait_ge(s["v_ready"], t + 1)
                reused(pe, s["cmb_ready"], 2 * t)
                for b in range(2):
                    rows = slice(64 * b, 64 * b + 64)
                    for j in range(J):
                        last = nc.tensor.matmul(ps_cm[b][:, j, :], kS[rows, j * P:(j + 1) * P], v[rows, j * P:(j + 1) * P], start=True, stop=True)
                last.then_inc(s["cm_ps"], 1)
                pe.wait_ge(s["pq_ready"], t + 1)
                for j in range(J):
                    last = nc.tensor.transpose(ps_q[:, j * P:(j + 1) * P], pq[:, 2 * j:2 * j + 2, :].rearrange("p h d -> p (h d)"), core.ident[:, :])
                last.then_inc(s["qT_ps"], 1)
                pe.wait_ge(s["qT_ready"], t + 1)
                pe.wait_ge(s["cmb_ready"], 2 * t + 2)
                reused(pe, s["oT_ready"], t)
                for j in range(J):
                    for b in range(2):
                        last = nc.tensor.matmul(ps_o[64 * b:64 * b + 64, j * P:(j + 1) * P], qT[:, j, b, :], cmb[:, b, j, :], start=True, stop=True)
                last.then_inc(s["o_ps"], 1)
                if not is_last(t):
                    front(t + 1)
                pe.wait_ge(s["on_ready"], t + 1)
                for j in range(J):
                    last = nc.tensor.transpose(ps_o[:, j * P:(j + 1) * P], on[:, j * P:(j + 1) * P], core.ident[:, :])
                last.then_inc(s["oT_ps"], 1)
                pe.wait_ge(s["oT_ready"], t + 1)
                reused(pe, s["x_ready"], t)
                for j in range(J):
                    nc.tensor.matmul(ps_y[:, :], oT[:, j * P:(j + 1) * P], w_out[:, j, :], start=(j == 0), stop=False)
                nc.tensor.matmul(ps_y[:, :], core.ones[:, :], shift[:, :], start=False, stop=True).then_inc(s["y_ps"], 1)
            front(0)
            tiles(pe, step)

        @block.scalar
        def _(act):
            root_on_scalar(act)
            nc.scalar.preload_act_table(ACT.Exp)

            def turn_x(t):
                act.wait_ge(s["xnT_ps"], t + 1)
                reused(act, s["q_ps"], t)
                nc.scalar.copy(xnT[:, :], ps_x[:, :]).then_inc(s["xnT_ready"], 1)

            def step(t):
                act.wait_ge(s["v_ps"], t + 1)
                reused(act, s["cm_ps"], t)
                nc.scalar.copy(v[:, :], ps_v[:, :]).then_inc(s["v_ready"], 1)
                act.wait_ge(s["dn_ready"], t + 1)
                reused(act, s["nvt_ready"], t)
                nc.scalar.activation(en[:, :, :], dn[:, :, :], ACT.Exp).then_inc(s["en_ready"], 1)
                act.wait_ge(s["kc_ready"], t + 1)
                nc.scalar.activation(ek[:, :, :, :], kc[:, :, :, :], ACT.Exp).then_inc(s["ek_ready"], 1)
                act.wait_ge(s["kS_ps"], t + 1)
                nc.scalar.copy(kS[:, :], ps_k[:, :]).then_inc(s["kS_ready"], 1)
                act.wait_ge(s["qs_ready"], t + 1)
                nc.scalar.activation(pq[:, :, :], qs[:, :, :], ACT.Exp).then_inc(s["pq_ready"], 1)
                if not is_last(t):
                    turn_x(t + 1)
                act.wait_ge(s["oT_ps"], t + 1)
                reused(act, s["y_ps"], t)
                nc.scalar.copy(oT[:, :], ps_o[:, :]).then_inc(s["oT_ready"], 1)
            turn_x(0)
            tiles(act, step)

        @block.vector
        def _(dve):
            V = nc.vector
            root_on_vector(dve)
            dve.wait_ge(s["w_in"], 16 * W_DMAS)
            V.tensor_tensor(w_out[:, :, :], wout[:, :, :], log[:, :].unsqueeze(2).broadcast_to([P, J, D]), ALU.mult).then_inc(s["folded"], 1)
            dve.wait_ge(s["shift_ps"], 1)
            V.tensor_copy(shift[:, :], ps_y[0:1, :]).then_inc(s["shift_ready"], 1)
            dve.wait_ge(s["filled"], 2)

            def normalise(t):
                reused(dve, s["xnT_ps"], t)
                V.tensor_scalar(xn[:, :], core.x[:, t, :], core.mean[:, bass.ts(t, 1)], core.rstd[:, bass.ts(t, 1)],
                                ALU.subtract, ALU.mult).then_inc(s["xn_ready"], 1)

            def step(t):
                k4 = ps_k[:, :].rearrange("p (j b k) -> p j b k", j=J, b=2)
                dve.wait_ge(s["k_ps"], t + 1)
                V.tensor_reduce(mk0[:, :, :], k4, AX.X, ALU.max).then_inc(s["mk0_ready"], 1)
                dve.wait_ge(s["mk0_ready"], t + 1)
                V.tensor_scalar(mk[:, :, :], mk0[:, :, :], nk[:, :], None, ALU.max).then_inc(s["mk_ready"], 1)
                dve.wait_ge(s["mk_ready"], t + 1)
                reused(dve, s["en_ready"], t)
                V.tensor_scalar(dn[:, :, :], mk[:, :, :], -1.0, nk[:, :], ALU.mult, ALU.add).then_inc(s["dn_ready"], 1)
                reused(dve, s["ek_ready"], t)
                V.tensor_tensor(kc[:, :, :, :], k4, mk[:, :, :].unsqueeze(3).broadcast_to([P, J, 2, S]), ALU.subtract).then_inc(s["kc_ready"], 1)
                dve.wait_ge(s["q_ps"], t + 1)
                V.bn_stats(bn[:, :], ps_q[:, :]).then_inc(s["bn_ready"], 1)
                dve.wait_ge(s["shift_ready"], 1)
                dve.wait_ge(s["bn_ready"], t + 1)
                V.bn_aggr(mv[:, :], bn[:, :]).then_inc(s["mv_ready"], 1)
                dve.wait_ge(s["mv_ready"], t + 1)
                V.tensor_scalar(ve[:, :], mv[:, 1:2], LN_EPS, None, ALU.add).then_inc(s["ve_ready"], 1)
                dve.wait_ge(s["ek_ready"], t + 1)
                V.tensor_reduce(sk[:, :, :], ek[:, :, :, :], AX.X, ALU.add).then_inc(s["sk_ready"], 1)
                dve.wait_ge(s["rs_ready"], t + 1)
                V.tensor_scalar(qn[:, :], ps_q[:, :], mv[:, 0:1], rs[:, :], ALU.subtract, ALU.mult).then_inc(s["qn_ready"], 1)
                dve.wait_ge(s["sk_ready"], t + 1)
                dve.wait_ge(s["en_ready"], t + 1)
                V.tensor_tensor(sk2[:, :, :], sk[:, :, :], en[:, :, :], ALU.add).then_inc(s["sk2_ready"], 1)
                dve.wait_ge(s["sk2_ready"], t + 1)
                V.reciprocal(rk[:, :, :], sk2[:, :, :]).then_inc(s["rk_ready"], 1)
                if not is_last(t):
                    normalise(t + 1)
                dve.wait_ge(s["cm_ps"], t + 1)
                dve.wait_ge(s["nvt_ready"], t + 1)
                reused(dve, s["o_ps"], t)
                for b in range(2):
                    for h in range(2):
                        rows, cols = slice(64 * h, 64 * h + 64), slice(64 * h, 64 * h + 64)
                        last = V.tensor_tensor(cmb[rows, b, :, cols], ps_cm[b][rows, :, cols], nvt[rows, b, :, :], ALU.add)
                    last.then_inc(s["cmb_ready"], 1)
                dve.wait_ge(s["qb_ready"], t + 1)
                V.tensor_reduce(mq[:, :], qb[:, :, :], AX.X, ALU.max).then_inc(s["mq_ready"], 1)
                dve.wait_ge(s["mq_ready"], t + 1)
                V.tensor_tensor(qs[:, :, :], qb[:, :, :], mq[:, :].unsqueeze(2).broadcast_to([P, H, HD]), ALU.subtract).then_inc(s["qs_ready"], 1)
                dve.wait_ge(s["pq_ready"], t + 1)
                V.tensor_reduce(sq[:, :], pq[:, :, :], AX.X, ALU.add).then_inc(s["sq_ready"], 1)
                dve.wait_ge(s["qT_ps"], t + 1)
                dve.wait_ge(s["rk_ready"], t + 1)
                V.tensor_tensor(qT[:, :, :, :], ps_q[:, :].rearrange("p (j b k) -> p j b k", j=J, b=2),
                                rk[:, :, :].unsqueeze(3).broadcast_to([P, J, 2, S]), ALU.mult).then_inc(s["qT_ready"], 1)
                dve.wait_ge(s["sq_ready"], t + 1)
                V.reciprocal(rq[:, :], sq[:, :]).then_inc(s["rq_ready"], 1)
                dve.wait_ge(s["rq_ready"], t + 1)
                dve.wait_ge(s["o_ps"], t + 1)
                V.scalar_tensor_tensor(out=o1[:, :, :], in0=ps_o[:, :].rearrange("p (h d) -> p h d", h=H), scalar=8.0,
                                       in1=rq[:, :].unsqueeze(2).broadcast_to([P, H, HD]), op0=ALU.mult, op1=ALU.mult).then_inc(s["o1_ready"], 1)
                dve.wait_ge(s["o1_ready"], t + 1)
                V.bn_stats(bo[:, :], o1[:, :, :].rearrange("p h d -> p (h d)")).then_inc(s["bo_ready"], 1)
                dve.wait_ge(s["shift_ready"], 1)
                dve.wait_ge(s["bo_ready"], t + 1)
                V.bn_aggr(mo[:, :], bo[:, :]).then_inc(s["mo_ready"], 1)
                dve.wait_ge(s["mo_ready"], t + 1)
                V.tensor_scalar(vo[:, :], mo[:, 1:2], LN_EPS, None, ALU.add).then_inc(s["vo_ready"], 1)
                dve.wait_ge(s["ro_ready"], t + 1)
                reused(dve, s["oT_ps"], t)
                V.tensor_scalar(on[:, :], o1[:, :, :].rearrange("p h d -> p (h d)"), mo[:, 0:1], ro[:, :], ALU.subtract, ALU.mult
                                ).then_inc(s["on_ready"], 1)
                dve.wait_ge(s["y_ps"], t + 1)
                V.scalar_tensor_tensor(out=core.x[:, t, :], in0=ps_y[:, :], scalar=core.gates[:, gate:gate + 1],
                                       in1=core.x[:, t, :], op0=ALU.mult, op1=ALU.add).then_inc(s["x_ready"], 1)
                dve.wait_ge(s["x_ready"], t + 1)
                dve.wait_ge(s["shift_ready"], 1)
                V.bn_stats(core.bn[:, t, :], core.x[:, t, :]).then_inc(s["summed"], 1)
            normalise(0)
            tiles(dve, step)


def build_rest(nc, core, a, stop):
    with Phase(nc, "l0f") as ph:
        r = Routing(ph, 1, 16, T)
        route(nc, core, "l0r", r, 4, a["L0_ffn_Wg"], cap=T // 16)
        experts(nc, core, "l0e", r, 16, 1, a["L0_ffn_w1"], a["L0_ffn_w2"], ACT.Relu)
        combine(nc, core, "l0c", r)
    if stop <= 2:
        return

    def neg_of_side(ph, neg, ready):
        pad = ph.sb("pad", [P, NT, S], U8)
        side = ph.sb("side_mask", [P, S])
        neg_in = ph.sem("neg_in")
        halved = ph.sem("halved")

        def dma(sp):
            for b in range(2):
                rows = slice(64 * b, 64 * b + 64)
                src = a["mask_BxS2_bf0"].rearrange("(n b) k -> b n k", b=2)[b:b + 1, :, :]
                sp.dma_start(pad[rows, :, :], src.broadcast_to([64, NT, S])).then_inc(neg_in, 16)
                sp.dma_start(side[rows, :], a["fside_SxS2_0"]).then_inc(neg_in, 16)

        def vector(dve):
            dve.wait_ge(neg_in, 64)
            nc.vector.tensor_scalar(side[:, :], side[:, :], 0.5, None, ALU.mult).then_inc(halved, 1)
            dve.wait_ge(halved, 1)
            nc.vector.scalar_tensor_tensor(out=neg[:, :, :], in0=pad[:, :, :], scalar=MASKED / 2,
                                           in1=side[:, :].unsqueeze(1).broadcast_to([P, NT, S]),
                                           op0=ALU.mult, op1=ALU.add).then_inc(ready, 1)
            dve.wait_ge(ready, 1)
        return dma, vector

    attention16(nc, core, "l1a", 1, [a[f"L1_xattn_W{c}"] for c in "qkvo"], [a[f"L1_xattn_b{c}"] for c in "qkvo"],
                True, neg_of_side, side=a["fside_Bx16xSxS2_0"])


    if stop <= 3:
        return
    ternary_ffn(nc, core, "l1f", 5, a["L1_ffn_W_fc"], a["L1_ffn_W_proj"], a["L1_ffn_ln_w"], a["L1_ffn_ln_b"])
    if stop <= 4:
        return
    attention1(nc, core, "l2a", 2, a["L2_xattn_W"], a["L2_xattn_b"], a["ctx_1024"], a["mask_BxS2_bf0"])
    if stop <= 5:
        return
    with Phase(nc, "l2f") as ph:
        r = Routing(ph, 2, 8, MAX_SLOTS)
        route(nc, core, "l2r", r, None, a["L2_ffn_gate_w"], cap=None, bg_dram=a["L2_ffn_gate_b"], temp=0.9)
        experts(nc, core, "l2e", r, MAX_SLOTS // CHUNK, 1, a["L2_ffn_w1"], a["L2_ffn_w2"], ACT.Gelu,
                b1_dram=a["L2_ffn_b1"], b2_dram=a["L2_ffn_b2"], dynamic=True)
        combine(nc, core, "l2c", r, norm=(a["L2_ffn_ln_g"], a["L2_ffn_ln_b"]), gate=6)


    if stop <= 6:
        return
    linear_attention(nc, core, "l3a", 3, a["L3_xattn_Wq"], a["L3_xattn_Wkv"], a["L3_xattn_null_kv"], a["L3_xattn_ln_q_g"],
                     a["L3_xattn_ln_q_b"], a["L3_xattn_ln_out_g"], a["L3_xattn_ln_out_b"], a["L3_xattn_Wout"])
    if stop <= 7:
        return
    with Phase(nc, "l3f") as ph:
        r = Routing(ph, 2, 8, MAX_SLOTS)
        route(nc, core, "l3r", r, 7, a["L3_ffn_Wr"], cap=-(-T * 2 * 5 // (8 * 4)), sum_eps=1e-12, clamp=1e4)
        experts(nc, core, "l3e", r, 8, MAX_SLOTS // CHUNK // 8, a["L3_ffn_W1"], a["L3_ffn_W2"], ACT.Silu, w3_dram=a["L3_ffn_W3"])
        combine(nc, core, "l3c", r)


LAYOUT = {
    "L1_ffn_W_fc": lambda a: a.T,
    "L1_ffn_W_proj": lambda a: a.T,
    "L1_ffn_ln_w": lambda a: a.reshape(-1, P).T,
    "L1_ffn_ln_b": lambda a: a.reshape(-1, P).T,
    "L2_xattn_W": lambda a: a.T,
    "L3_xattn_ln_out_g": lambda a: a.reshape(-1, P).T,
    "L3_xattn_ln_out_b": lambda a: a.reshape(-1, P).T,
    "L2_ffn_b1": lambda a: a.reshape(a.shape[0], -1, P).transpose(0, 2, 1),
    "L2_ffn_b2": lambda a: a.reshape(a.shape[0], 1, -1),
}

STOP = 99


def kernel(**inputs):
    import numpy as _np
    import concourse.bacc as _bacc
    from concourse import mybir as _mybir
    from concourse.bass_utils import run_bass_kernel_spmd as _run

    nc = _bacc.Bacc("TRN2", target_bir_lowering=False, num_devices=1)
    arrays, aps = {}, {}
    for name, a in inputs.items():
        a = _np.asarray(a)
        if name in LAYOUT:
            a = LAYOUT[name](a)
        a = _np.ascontiguousarray(a)
        arrays[f"in_{name}"] = a
        aps[name] = nc.dram_tensor(f"in_{name}", a.shape, _mybir.dt.from_np(a.dtype), kind="ExternalInput").ap()
    out = nc.dram_tensor("out_x", (B, S, D), _mybir.dt.float32, kind="ExternalOutput").ap()
    build(nc, aps, out, STOP)
    r = _run(nc, [arrays], core_ids=[0])
    return r.results[0]["out_x"]
```

```python
from contextlib import ExitStack

import concourse.bass as bass
from concourse import mybir

F32 = mybir.dt.float32
BF16 = mybir.dt.bfloat16
I32 = mybir.dt.int32
U32 = mybir.dt.uint32
U8 = mybir.dt.uint8
ALU = mybir.AluOpType
ACT = mybir.ActivationFunctionType
AX = mybir.AxisListType

P = 128
B, S, D = 64, 64, 128
T = B * S
NT = T // P
H16, DH = 16, 8
HALF = H16 // 2
LN_EPS = 1e-5
UNROLL = 8
CHUNK = 256
MAX_SLOTS = 40 * CHUNK
ROW = D + 4
NOWHERE = 2.0 ** 20
MASKED = -(2.0 ** 100)


class Core:

    def __init__(self, nc, ctx):
        self.nc, self.ctx = nc, ctx
        sb = self.sb
        self.x = sb("x", [P, NT, D])
        self.bn = sb("bn", [P, NT, 6])
        self.mean = sb("mean", [P, NT])
        self.rstd = sb("rstd", [P, NT])
        self.ctxT = sb("ctxT", [P, T])
        self.ident = sb("ident", [P, P])
        self.ones = sb("ones", [1, P])
        self.gates = sb("gates", [P, 8])
        self.tables = {}
        for layer, slots, top in (("l0", T, 1), ("l2", MAX_SLOTS, 2), ("l3", MAX_SLOTS, 2)):
            self.tables[layer, "in"] = nc.dram_tensor(f"{layer}_rows_in", (slots, ROW), F32).ap()
            self.tables[layer, "out"] = nc.dram_tensor(f"{layer}_rows_out", (top * T, D), F32).ap()

    def sb(self, name, shape, dt=F32):
        return self.ctx.enter_context(self.nc.sbuf_tensor(name, shape, dt))


class Phase:

    def __init__(self, nc, name):
        self.nc, self.name, self.ctx, self.sems = nc, name, ExitStack(), []

    def __enter__(self):
        return self

    def __exit__(self, *e):
        self.ctx.__exit__(*e)
        if self.sems:
            self.nc.clear_and_free_semaphores(self.sems)
            self.nc.all_engine_barrier()

    def sb(self, name, shape, dt=F32):
        return self.ctx.enter_context(self.nc.sbuf_tensor(f"{self.name}_{name}", shape, dt))

    def ps(self, name, shape, dt=F32):
        return self.ctx.enter_context(self.nc.psum_tensor(f"{self.name}_{name}", shape, dt))

    def sem(self, name):
        self.sems.append(self.nc.alloc_semaphore(f"{self.name}_{name}"))
        return self.sems[-1]


def reused(eng, sem, value):
    if not isinstance(value, int) or value > 0:
        eng.wait_ge(sem, value)


def flat(ap):
    return ap.rearrange("b s d -> (b s) d")


def setup(nc, core, x_dram, ctx_dram, g_xattn, g_ffn):
    G = 4
    with Phase(nc, "setup") as ph:
        g_raw = ph.sb("g_raw", [P, 8])
        raw = ph.sb("raw", [P, 2, G, D])
        turned = [ph.ps(f"turned{k}", [P, G * P]) for k in range(2)]
        x_in, g_in, ctx_in = ph.sem("x_in"), ph.sem("g_in"), [ph.sem("ctx_in0"), ph.sem("ctx_in1")]
        filled, ident_done = ph.sem("filled"), ph.sem("ident_done")
        turned_ready, ctxT_done = ph.sem("turned_ready"), ph.sem("ctxT_done")
        summed, gates_done = ph.sem("summed"), ph.sem("gates_done")
        x_tiles = flat(x_dram).rearrange("(n p) d -> p n d", p=P)
        ctx_tiles = flat(ctx_dram).rearrange("(n p) d -> p n d", p=P)
        block = ph.ctx.enter_context(nc.Block())

        @block.sync
        def _(sp):
            sp.dma_start(raw[:, 0, :, :], ctx_tiles[:, 0:G, :]).then_inc(ctx_in[0], 16)
            sp.dma_start(core.x[:, :, :], x_tiles).then_inc(x_in, 16)
            sp.dma_start(g_raw[:, 0:4], g_xattn.rearrange("(a n) -> a n", a=1).broadcast_to([P, 4])).then_inc(g_in, 16)
            sp.dma_start(g_raw[:, 4:8], g_ffn.rearrange("(a n) -> a n", a=1).broadcast_to([P, 4])).then_inc(g_in, 16)
            for c in range(1, NT // G):
                if c >= 2:
                    sp.wait_ge(turned_ready, c - 1)
                sp.dma_start(raw[:, c % 2, :, :], ctx_tiles[:, c * G:(c + 1) * G, :]).then_inc(ctx_in[c % 2], 16)

        @block.gpsimd
        def _(pool):
            pool.memset(core.ident[:, :], 0.0).then_inc(filled, 1)
            pool.memset(core.ones[:, :], 1.0).then_inc(filled, 1)
            pool.wait_ge(filled, 2)
            pool.affine_select(out=core.ident[:, :], in_=core.ident[:, :], compare_op=ALU.not_equal, fill=1.0,
                               base=0, pattern=[[-1, P]], channel_multiplier=1).then_inc(ident_done, 1)

        @block.tensor
        def _(pe):
            pe.wait_ge(ident_done, 1)
            for c in range(NT // G):
                pe.wait_ge(ctx_in[c % 2], 16 * (c // 2 + 1))
                if c >= 2:
                    pe.wait_ge(ctxT_done, c - 1)
                for k in range(G):
                    last = nc.tensor.transpose(turned[c % 2][:, k * P:(k + 1) * P], raw[:, c % 2, k, :], core.ident[:, :])
                last.then_inc(turned_ready, 1)

        @block.scalar
        def _(act):
            act.wait_ge(g_in, 32)
            nc.scalar.activation(core.gates[:, :], g_raw[:, :], ACT.Tanh).then_inc(gates_done, 1)
            for c in range(NT // G):
                act.wait_ge(turned_ready, c + 1)
                nc.scalar.copy(core.ctxT[:, c * G * P:(c + 1) * G * P], turned[c % 2][:, :]).then_inc(ctxT_done, 1)

        @block.vector
        def _(dve):
            dve.wait_ge(x_in, 16)
            with dve.Fori(0, NT // UNROLL) as g:
                for j in range(UNROLL):
                    nc.vector.bn_stats(core.bn[:, g * UNROLL + j, :], core.x[:, g * UNROLL + j, :]).then_inc(summed, 1)


def row_statistics(nc, ph, core):
    root = ph.sb("root", [P, NT])
    y = ph.sb("y", [P, NT])
    yy = ph.sb("yy", [P, NT])
    veps = ph.sb("veps", [P, NT])
    ready, rooted, stepped = ph.sem("veps_ready"), ph.sem("rooted"), ph.sem("stepped")

    def on_scalar(act):
        act.wait_ge(ready, 1)
        nc.scalar.activation(root[:, :], veps[:, :], ACT.Sqrt).then_inc(rooted, 1)

    def on_vector(dve):
        def step(k, ins):
            ins.then_inc(stepped, 1)
            dve.wait_ge(stepped, k)
        even, odd = core.bn[:, :, 1], core.bn[:, :, 4]
        step(1, nc.vector.tensor_tensor(y[:, :], even, odd, ALU.subtract))
        step(2, nc.vector.tensor_tensor(yy[:, :], core.bn[:, :, 2], core.bn[:, :, 5], ALU.add))
        step(3, nc.vector.tensor_tensor(core.mean[:, :], even, odd, ALU.add))
        step(4, nc.vector.tensor_scalar(core.mean[:, :], core.mean[:, :], 0.5, None, ALU.mult))
        step(5, nc.vector.scalar_tensor_tensor(out=y[:, :], in0=y[:, :], scalar=0.25, in1=y[:, :], op0=ALU.mult, op1=ALU.mult))
        step(6, nc.vector.tensor_scalar(yy[:, :], yy[:, :], 1.0 / D, LN_EPS, ALU.mult, ALU.add))
        nc.vector.tensor_tensor(veps[:, :], yy[:, :], y[:, :], ALU.add).then_inc(ready, 1)
        dve.wait_ge(rooted, 1)
        step(7, nc.vector.reciprocal(y[:, :], root[:, :]))
        step(8, nc.vector.tensor_tensor(yy[:, :], y[:, :], y[:, :], ALU.mult))
        step(9, nc.vector.tensor_tensor(yy[:, :], yy[:, :], veps[:, :], ALU.mult))
        step(10, nc.vector.tensor_scalar(yy[:, :], yy[:, :], -0.5, 1.5, ALU.mult, ALU.add))
        step(11, nc.vector.tensor_tensor(core.rstd[:, :], y[:, :], yy[:, :], ALU.mult))

    return on_scalar, on_vector


def attention16(nc, core, name, gate, w_dram, b_dram, neg_steps, side=None, fills=()):
    with Phase(nc, name) as ph:
        w = ph.sb("w", [P, 4, D])
        bq = ph.sb("bq", [P, 2])
        bk = ph.sb("bk", [P, 2])
        bv = ph.sb("bv", [P, 1])
        bo = ph.sb("bo", [1, D])
        bvo = ph.sb("bvo", [1, D])
        own = ph.sb("own", [P, HALF])
        xn = ph.sb("xn", [P, D])
        xnT = ph.sb("xnT", [P, P])
        cdup = ph.sb("cdup", [P, 2, 2, S])
        qbd = ph.sb("qbd", [P, 2, 2, P])
        kT = ph.sb("kT", [P, 2, S])
        kbd = ph.sb("kbd", [P, 2, 2, HALF, S])
        vbd = ph.sb("vbd", [P, 2, 2, HALF, 2, DH + 1])
        s1 = ph.sb("s1", [P, H16, S])
        s2 = ph.sb("s2", [P, H16, S])
        p = ph.sb("p", [P, H16, S])
        pT = ph.sb("pT", [P, HALF, P])
        mx = ph.sb("mx", [P, H16])
        rden = ph.sb("rden", [P, H16])
        o = ph.sb("o", [P, D])
        oT = ph.sb("oT", [P, P])
        neg = ph.sb("neg", [P, NT, S])
        ps_qk = ph.ps("ps_qk", [P, 512])
        ps_v = ph.ps("ps_v", [P, 512])
        ps_s = ph.ps("ps_s", [P, H16, S])
        ps_t = ph.ps("ps_t", [P, HALF, P])
        ps_o = ph.ps("ps_o", [P, 512])
        ps_e = ph.ps("ps_e", [P, 512])
        ps_x, ps_oT, ps_y = ps_qk[:, 4 * S:4 * S + P], ps_e[:, 0:P], ps_e[:, P:P + D]
        side_in_buf = ph.sb("side", [P, 2, H16, S]) if side is not None else None

        names = ("w_in b_in bvo_ps neg_ready filled own_ready bvo_ready qk_scaled "
                 "xn_ready xnT_ps xnT_ready cdup_ready qk_ps v_ps q_ready k_ready kbd_ready vbd_ready "
                 "s_ps s1_ready max_ready s2_ready p_ready pT_ps pT_ready o_ps rden_ready o_ready oT_ps oT_ready "
                 "y_ps x_ready summed").split()
        if side is not None:
            names += ["side_in0", "side_in1", "side_ready"]
        FILL = 8
        fill_rows = ph.sb("fill_rows", [P, FILL, ROW])
        names += ["fill_ready", "tables_filled"]
        s = {n: ph.sem(n) for n in names}
        root_on_scalar, root_on_vector = row_statistics(nc, ph, core)
        neg_dma, neg_vector = neg_steps(ph, neg, s["neg_ready"])
        block = ph.ctx.enter_context(nc.Block())

        def is_tile(t):
            return not isinstance(t, int) or 0 <= t < NT

        def steps(eng, step):
            step(0, 0)
            step(1, 1)
            with eng.Fori(1, NT // 2 - 2) as u:
                step(u * 2, 0)
                step(u * 2 + 1, 1)
            for i in range(NT - 4, NT):
                step(i, i % 2)

        @block.sync
        def _(sp):
            for k in range(4):
                sp.dma_start(w[:, k, :], w_dram[k]).then_inc(s["w_in"], 16)
            for half in range(2):
                rows = slice(64 * half, 64 * half + 64)
                sp.dma_start(bq[rows, :], b_dram[0].rearrange("(h r) -> r h", h=2), allow_slow_non_contiguous=True).then_inc(s["b_in"], 16)
                sp.dma_start(bk[rows, :], b_dram[1].rearrange("(h r) -> r h", h=2), allow_slow_non_contiguous=True).then_inc(s["b_in"], 16)
            sp.dma_start(bv[:, :], b_dram[2].rearrange("(r a) -> r a", a=1)).then_inc(s["b_in"], 16)
            sp.dma_start(bo[:, :], b_dram[3].rearrange("(a r) -> a r", a=1)).then_inc(s["b_in"], 16)
            neg_dma(sp)
            if side is not None:
                side_tiles = side.rearrange("(n b) q h k -> n (b q) h k", b=2)

                def load_side(t, k):
                    sp.dma_start(side_in_buf[:, k, :, :], side_tiles[t, :, :, :]).then_inc(s[f"side_in{k}"], 16)
                load_side(0, 0)
                load_side(1, 1)
                with sp.Fori(1, NT // 2) as u:
                    for k in range(2):
                        sp.wait_ge(s["s1_ready"], u * 2 + (k - 1))
                        load_side(u * 2 + k, k)

        @block.gpsimd
        def _(pool):
            pool.memset(own[:, :], 1.0).then_inc(s["filled"], 1)
            pool.memset(qbd[:, :, :, :], 0.0).then_inc(s["filled"], 1)
            pool.memset(vbd[:, :, :, :, :, :], 0.0).then_inc(s["filled"], 1)
            pool.wait_ge(s["filled"], 3)
            for h in range(2):
                rows = slice(64 * h, 64 * h + 64)
                pool.memset(vbd[rows, :, :, :, h, DH:DH + 1], 1.0).then_inc(s["filled"], 1)
            for h in range(2):
                part = own[64 * h:64 * h + 64, :]
                pool.affine_select(out=part, in_=part, compare_op=ALU.is_ge, fill=0.0, base=0,
                                   pattern=[[-DH, HALF]], channel_multiplier=1).then_inc(s["own_ready"], 1)
            pool.wait_ge(s["own_ready"], 2)
            for h in range(2):
                part = own[64 * h:64 * h + 64, :]
                pool.affine_select(out=part, in_=part, compare_op=ALU.is_ge, fill=0.0, base=DH - 1,
                                   pattern=[[DH, HALF]], channel_multiplier=-1).then_inc(s["own_ready"], 1)
            pool.wait_ge(s["own_ready"], 4)

            def context(t):
                if not is_tile(t):
                    return
                reused(pool, s["v_ps"], t)
                src = core.ctxT[:, bass.ts(t, P)].rearrange("p (b k) -> p b k", b=2)
                pool.tensor_copy(cdup[:, :, :, :], src.unsqueeze(2).broadcast_to([P, 2, 2, S])).then_inc(s["cdup_ready"], 1)

            def spread(t, k):
                if not is_tile(t):
                    return
                pool.wait_ge(s["k_ready"], t + 1)
                reused(pool, s["s_ps"], t - 1)
                for hh in range(2):
                    pool.tensor_tensor(kbd[:, k, hh, :, :], kT[:, hh, :].unsqueeze(1).broadcast_to([P, HALF, S]),
                                       own[:, :].unsqueeze(2).broadcast_to([P, HALF, S]), ALU.mult
                                       ).then_inc(s["kbd_ready"], 1)

            def side_add(t, k, before):
                if side is None or not is_tile(t):
                    return
                pool.wait_ge(s[f"side_in{k}"], before * 16 + 16)
                buf = side_in_buf[:, k, :, :]
                pool.tensor_tensor(buf, buf, neg[:, t, :].unsqueeze(1).broadcast_to([P, H16, S]), ALU.add
                                   ).then_inc(s["side_ready"], 1)

            if side is not None:
                pool.wait_ge(s["neg_ready"], 1)
            context(0)
            side_add(0, 0, 0)
            spread(0, 0)
            context(1)
            spread(1, 1)
            context(2)
            side_add(1, 1, 0)

            def step(i, k, before):
                spread(i + 2, k)
                context(i + 3)
                side_add(i + 2, k, before)
            step(0, 0, 1)
            step(1, 1, 1)
            with pool.Fori(1, NT // 2 - 2) as u:
                step(u * 2, 0, u + 1)
                step(u * 2 + 1, 1, u + 1)
            for i in range(NT - 4, NT):
                step(i, i % 2, i // 2 + 1)

        @block.tensor
        def _(pe):
            pe.wait_ge(s["w_in"], 64)
            pe.wait_ge(s["b_in"], 96)
            nc.tensor.matmul(ps_o[0:1, 0:D], bv[:, :], w[:, 3, :], start=True, stop=True).then_inc(s["bvo_ps"], 1)
            pe.wait_ge(s["qk_scaled"], 2)
            pe.wait_ge(s["bvo_ready"], 1)

            def turn_x(t):
                if not is_tile(t):
                    return
                pe.wait_ge(s["xn_ready"], t + 1)
                reused(pe, s["k_ready"], t)
                nc.tensor.transpose(ps_x, xn[:, :], core.ident[:, :]).then_inc(s["xnT_ps"], 1)

            def project(t):
                if not is_tile(t):
                    return
                pe.wait_ge(s["xnT_ready"], t + 1)
                reused(pe, s["k_ready"], t)
                for hh in range(2):
                    for b in range(2):
                        nc.tensor.matmul(ps_qk[64 * b:64 * b + 64, hh * S:(hh + 1) * S], w[:, 0, 64 * hh:64 * hh + 64],
                                         xnT[:, 64 * b:64 * b + 64], start=True, stop=True)
                pe.wait_ge(s["cdup_ready"], t + 1)
                for hh in range(2):
                    for b in range(2):
                        last = nc.tensor.matmul(ps_qk[64 * b:64 * b + 64, (2 + hh) * S:(3 + hh) * S], w[:, 1, 64 * hh:64 * hh + 64],
                                                cdup[:, b, 0, :], start=True, stop=True)
                last.then_inc(s["qk_ps"], 1)

            def project_v(t):
                if not is_tile(t):
                    return
                pe.wait_ge(s["cdup_ready"], t + 1)
                reused(pe, s["vbd_ready"], 2 * t)
                for b in range(2):
                    last = nc.tensor.matmul(ps_v[:, b * D:(b + 1) * D], cdup[:, b, :, :].rearrange("p a k -> p (a k)"), w[:, 2, :],
                                            start=True, stop=True)
                last.then_inc(s["v_ps"], 1)

            def scores(t, k):
                if not is_tile(t):
                    return
                pe.wait_ge(s["q_ready"], 2 * t + 2)
                pe.wait_ge(s["kbd_ready"], 2 * t + 2)
                reused(pe, s["s1_ready"], t)
                for hh in range(2):
                    last = nc.tensor.matmul(ps_s[:, hh * HALF:(hh + 1) * HALF, :], qbd[:, k, hh, :], kbd[:, k, hh, :, :],
                                            start=True, stop=True)
                last.then_inc(s["s_ps"], 1)

            def turn_p(t):
                if not is_tile(t):
                    return
                pe.wait_ge(s["p_ready"], t + 1)
                for j in range(HALF):
                    if j % 4 == 0:
                        reused(pe, s["pT_ready"], 2 * t - (1 - j // 4))
                    last = nc.tensor.transpose(ps_t[:, j, :], p[:, 2 * j:2 * j + 2, :].rearrange("q a k -> q (a k)"), core.ident[:, :])
                    if j % 4 == 3:
                        last.then_inc(s["pT_ps"], 1)

            def values(t, k):
                if not is_tile(t):
                    return
                pe.wait_ge(s["vbd_ready"], 2 * t + 2)
                reused(pe, s["o_ready"], t)
                for j in range(HALF):
                    if j % 4 == 0:
                        pe.wait_ge(s["pT_ready"], 2 * t + j // 4 + 1)
                    for b in range(2):
                        last = nc.tensor.matmul(ps_o[64 * b:64 * b + 64, 18 * j:18 * j + 18], pT[:, j, 64 * b:64 * b + 64],
                                                vbd[:, k, b, j, :, :], start=True, stop=True)
                last.then_inc(s["o_ps"], 1)

            def turn_o(t):
                if not is_tile(t):
                    return
                pe.wait_ge(s["o_ready"], t + 1)
                reused(pe, s["x_ready"], t)
                nc.tensor.transpose(ps_oT, o[:, :], core.ident[:, :]).then_inc(s["oT_ps"], 1)

            def output(t):
                if not is_tile(t):
                    return
                pe.wait_ge(s["oT_ready"], t + 1)
                nc.tensor.matmul(ps_y, oT[:, :], w[:, 3, :], start=True, stop=False)
                nc.tensor.matmul(ps_y, core.ones[:, :], bvo[:, :], start=False, stop=True).then_inc(s["y_ps"], 1)

            turn_x(0)
            project(0)
            project_v(0)
            turn_x(1)
            project(1)
            project_v(1)
            scores(0, 0)
            turn_x(2)

            def step(i, k):
                project(i + 2)
                scores(i + 1, 1 - k)
                turn_o(i - 1)
                project_v(i + 2)
                turn_p(i)
                output(i - 1)
                turn_x(i + 3)
                values(i, k)
            steps(pe, step)
            turn_o(NT - 1)
            output(NT - 1)

        @block.scalar
        def _(act):
            root_on_scalar(act)

            def normalised(t):
                if not is_tile(t):
                    return
                act.wait_ge(s["xnT_ps"], t + 1)
                reused(act, s["qk_ps"], t)
                nc.scalar.copy(xnT[:, :], ps_x).then_inc(s["xnT_ready"], 1)

            def values(t, k):
                if not is_tile(t):
                    return
                act.wait_ge(s["v_ps"], t + 1)
                reused(act, s["o_ps"], t - 1)
                for h in range(2):
                    rows = slice(64 * h, 64 * h + 64)
                    src = ps_v[rows, 0:2 * D].rearrange("p (b j a d) -> p b j a d", b=2, a=2, d=DH)[:, :, :, h, :]
                    nc.scalar.copy(vbd[rows, k, :, :, h, 0:DH], src).then_inc(s["vbd_ready"], 1)

            def exponent(t):
                if not is_tile(t):
                    return
                act.wait_ge(s["s2_ready"], t + 1)
                reused(act, s["pT_ps"], 2 * t)
                nc.scalar.activation(p[:, :, :], s2[:, :, :], ACT.Exp).then_inc(s["p_ready"], 1)

            def turned(t):
                if not is_tile(t):
                    return
                for k in range(2):
                    act.wait_ge(s["pT_ps"], 2 * t + k + 1)
                    if k == 0:
                        reused(act, s["o_ps"], t)
                    nc.scalar.copy(pT[:, 4 * k:4 * k + 4, :], ps_t[:, 4 * k:4 * k + 4, :]).then_inc(s["pT_ready"], 1)

            def outputs(t):
                if not is_tile(t):
                    return
                act.wait_ge(s["oT_ps"], t + 1)
                reused(act, s["y_ps"], t)
                nc.scalar.copy(oT[:, :], ps_oT).then_inc(s["oT_ready"], 1)

            act.wait_ge(s["fill_ready"], 2)
            fill_dmas = 0
            for table in fills:
                width = table.shape[1]
                blocks = table.rearrange("(n p a) d -> n p a d", p=P, a=FILL)
                for n in range(table.shape[0] // P // FILL):
                    act.dma_start(blocks[n, :, :, :], fill_rows[:, :, 0:width]).then_inc(s["tables_filled"], 16)
                    fill_dmas += 1
            act.wait_ge(s["filled"], 5)
            normalised(0)
            values(0, 0)
            normalised(1)
            values(1, 1)
            normalised(2)
            nc.scalar.preload_act_table(ACT.Exp)

            def step(i, k):
                exponent(i)
                outputs(i - 1)
                turned(i)
                normalised(i + 3)
                values(i + 2, k)
            steps(act, step)
            outputs(NT - 1)
            act.wait_ge(s["tables_filled"], 16 * fill_dmas)

        @block.vector
        def _(dve):
            nc.vector.memset(fill_rows[:, :, 0:D], 0.0).then_inc(s["fill_ready"], 1)
            nc.vector.memset(fill_rows[:, :, D:ROW], NOWHERE).then_inc(s["fill_ready"], 1)
            dve.wait_ge(s["w_in"], 64)
            dve.wait_ge(s["b_in"], 96)
            dve.wait_ge(s["bvo_ps"], 1)
            nc.vector.tensor_tensor(bvo[:, :], ps_o[0:1, 0:D], bo[:, :], ALU.add).then_inc(s["bvo_ready"], 1)
            nc.vector.tensor_scalar(w[:, 0, :], w[:, 0, :], DH ** -0.5, None, ALU.mult).then_inc(s["qk_scaled"], 1)
            nc.vector.tensor_scalar(bq[:, :], bq[:, :], DH ** -0.5, None, ALU.mult).then_inc(s["qk_scaled"], 1)
            dve.wait_ge(s["filled"], 5)
            dve.wait_ge(s["qk_scaled"], 2)
            dve.wait_ge(s["bvo_ready"], 1)
            root_on_vector(dve)
            neg_vector(dve)

            def normalise(t):
                if not is_tile(t):
                    return
                reused(dve, s["xnT_ps"], t)
                nc.vector.tensor_scalar(xn[:, :], core.x[:, t, :], core.mean[:, bass.ts(t, 1)], core.rstd[:, bass.ts(t, 1)],
                                        ALU.subtract, ALU.mult).then_inc(s["xn_ready"], 1)

            def queries_keys(t, k):
                if not is_tile(t):
                    return
                dve.wait_ge(s["qk_ps"], t + 1)
                reused(dve, s["s_ps"], t - 1)
                for b in range(2):
                    rows = slice(64 * b, 64 * b + 64)
                    nc.vector.tensor_tensor(qbd[rows, k, :, 64 * b:64 * b + 64], ps_qk[rows, 0:2 * S].rearrange("p (h q) -> p h q", h=2),
                                            bq[rows, :].unsqueeze(2).broadcast_to([64, 2, S]), ALU.add).then_inc(s["q_ready"], 1)
                reused(dve, s["kbd_ready"], 2 * t)
                nc.vector.tensor_tensor(kT[:, :, :], ps_qk[:, 2 * S:4 * S].rearrange("p (h q) -> p h q", h=2),
                                        bk[:, :].unsqueeze(2).broadcast_to([P, 2, S]), ALU.add).then_inc(s["k_ready"], 1)

            def masked(t, k):
                if not is_tile(t):
                    return
                dve.wait_ge(s["s_ps"], t + 1)
                reused(dve, s["s2_ready"], t)
                if side is None:
                    nc.vector.tensor_tensor(s1[:, :, :], ps_s[:, :, :], neg[:, t, :].unsqueeze(1).broadcast_to([P, H16, S]),
                                            ALU.add).then_inc(s["s1_ready"], 1)
                else:
                    dve.wait_ge(s["side_ready"], t + 1)
                    nc.vector.scalar_tensor_tensor(out=s1[:, :, :], in0=side_in_buf[:, k, :, :], scalar=2.0, in1=ps_s[:, :, :],
                                                   op0=ALU.mult, op1=ALU.add).then_inc(s["s1_ready"], 1)

            def maximum(t):
                if not is_tile(t):
                    return
                dve.wait_ge(s["s1_ready"], t + 1)
                nc.vector.tensor_reduce(mx[:, :], s1[:, :, :], AX.X, ALU.max).then_inc(s["max_ready"], 1)

            def centred(t):
                if not is_tile(t):
                    return
                dve.wait_ge(s["max_ready"], t + 1)
                reused(dve, s["p_ready"], t)
                nc.vector.tensor_tensor(s2[:, :, :], s1[:, :, :], mx[:, :].unsqueeze(2).broadcast_to([P, H16, S]),
                                        ALU.subtract).then_inc(s["s2_ready"], 1)

            def outputs(t):
                if not is_tile(t):
                    return
                dve.wait_ge(s["o_ps"], t + 1)
                o_ps = ps_o[:, 0:18 * HALF].rearrange("p (h d) -> p h d", d=DH + 1)
                nc.vector.reciprocal(rden[:, :], o_ps[:, :, DH]).then_inc(s["rden_ready"], 1)
                dve.wait_ge(s["rden_ready"], t + 1)
                reused(dve, s["oT_ps"], t)
                nc.vector.tensor_tensor(o[:, :].rearrange("p (h d) -> p h d", d=DH), o_ps[:, :, 0:DH],
                                        rden[:, :].unsqueeze(2).broadcast_to([P, H16, DH]), ALU.mult).then_inc(s["o_ready"], 1)

            def residual(t):
                if not is_tile(t):
                    return
                dve.wait_ge(s["y_ps"], t + 1)
                nc.vector.scalar_tensor_tensor(out=core.x[:, t, :], in0=ps_y, scalar=core.gates[:, gate:gate + 1],
                                               in1=core.x[:, t, :], op0=ALU.mult, op1=ALU.add).then_inc(s["x_ready"], 1)

            def summed(t):
                if not is_tile(t):
                    return
                dve.wait_ge(s["bvo_ready"], 1)
                dve.wait_ge(s["x_ready"], t + 1)
                nc.vector.bn_stats(core.bn[:, t, :], core.x[:, t, :]).then_inc(s["summed"], 1)

            normalise(0)
            normalise(1)
            queries_keys(0, 0)
            normalise(2)
            queries_keys(1, 1)
            masked(0, 0)
            maximum(0)
            centred(0)

            def step(i, k):
                outputs(i - 1)
                queries_keys(i + 2, k)
                normalise(i + 3)
                masked(i + 1, 1 - k)
                maximum(i + 1)
                residual(i - 1)
                centred(i + 1)
                summed(i - 1)
            steps(dve, step)
            outputs(NT - 1)
            residual(NT - 1)
            summed(NT - 1)


def store_x(nc, core, out):
    with Phase(nc, "store") as ph:
        stored = ph.sem("stored")
        block = ph.ctx.enter_context(nc.Block())

        @block.sync
        def _(sp):
            sp.dma_start(flat(out).rearrange("(n p) d -> p n d", p=P), core.x[:, :, :]).then_inc(stored, 16)
            sp.wait_ge(stored, 16)


def build(nc, a, out):
    with ExitStack() as ctx:
        core = Core(nc, ctx)
        setup(nc, core, a["x"], a["ctx_1024"], a["g_xattn"], a["g_ffn"])

        def neg_of_mask(ph, neg, ready):
            raw = ph.sb("mask_raw", [P, NT, S], I32)
            mask_in = ph.sem("mask_in")

            def dma(sp):
                sp.dma_start(raw[:, :, :], a["mask_Bx1xSxS2_ik1"].rearrange("b a q k -> (b a q) k").rearrange(
                    "(n p) k -> p n k", p=P)).then_inc(mask_in, 16)

            def vector(dve):
                dve.wait_ge(mask_in, 16)
                nc.vector.tensor_scalar(neg[:, :, :], raw[:, :, :], 0.0, MASKED, ALU.is_equal, ALU.mult).then_inc(ready, 1)
                dve.wait_ge(ready, 1)
            return dma, vector

        attention16(nc, core, "l0a", 0, [a[f"L0_xattn_W{c}"] for c in "qkvo"], [a[f"L0_xattn_b{c}"] for c in "qkvo"],
                    neg_of_mask, fills=[core.tables[k] for k in (("l0", "in"), ("l0", "out"), ("l3", "in"), ("l3", "out"))])
        later_layers(nc, core, a)
        store_x(nc, core, out)


class Routing:

    def __init__(self, ph, core, layer, top, experts):
        self.top, self.experts = top, experts
        self.rows_in, self.rows_out = core.tables[layer, "in"], core.tables[layer, "out"]
        self.slot = ph.sb("slot", [P, top, NT], U32)
        self.weight = ph.sb("weight", [P, top, NT])
        self.chunk_expert = ph.sb("chunk_expert", [1, MAX_SLOTS // CHUNK], I32)


def route(nc, core, name, r, gate, wg_dram, cap, bg_dram=None, temp=1.0, sum_eps=0.0, clamp=None):
    E, top = r.experts, r.top
    G = 4
    with Phase(nc, name) as ph:
        wg = ph.sb("wg", [P, E])
        bg = ph.sb("bg", [P, E])
        xT = ph.sb("xT", [P, 2, G * P])
        xn_all = ph.sb("xn_all", [P, NT, ROW])
        token_i = ph.sb("token_i", [P, NT], I32)
        lg = ph.sb("lg", [P, NT, E])
        tmp = ph.sb("tmp", [P, NT, E])
        picks = [ph.sb(f"pick{k}", [P, NT, E]) for k in range(top)]
        member = ph.sb("member", [P, NT, E])
        pos = ph.sb("pos", [P, NT, E])
        scan = [ph.sb(f"scan{k}", [P, NT, E]) for k in range(2)]
        best = ph.sb("best", [P, top, NT])
        index = ph.sb("index", [P, NT])
        choice_pos = ph.sb("choice_pos", [P, NT])
        choice_slot = ph.sb("choice_slot", [P, NT])
        iota_i = ph.sb("iota_i", [P, E], I32)
        iota = ph.sb("iota", [P, E])
        before = ph.sb("before", [P, P])
        ones = ph.sb("ones", [P, P])
        total = ph.sb("total", [P, NT])
        ps_x = [ph.ps(f"ps_x{k}", [P, G * P]) for k in range(2)]
        ps_l = ph.ps("ps_l", [P, 512])
        ps_before = ph.ps("ps_before", [P, 512])
        ps_total = ph.ps("ps_total", [P, 512])
        NC = MAX_SLOTS // CHUNK
        if cap is None:
            starts_i = ph.sb("starts_i", [P, NC], I32)
            starts = ph.sb("starts", [P, NC])
            more = ph.sb("more", [P, E, NC])
            ends = [ph.sb(f"ends{k}", [P, E]) for k in range(2)]
            chunks = ph.sb("chunks", [P, E])
            ce = ph.sb("ce", [P, NC])
        sems = {n: ph.sem(n) for n in "wg_in xn_ready xT_ps xT_ready l_ps lg_ready member_ready filled consts prefix_ps exp_in exp_out slots_ready scattered targets".split()}
        step_sem = ph.sem("step")
        root_on_scalar, root_on_vector = row_statistics(nc, ph, core)
        block = ph.ctx.enter_context(nc.Block())

        @block.sync
        def _(sp):
            sp.dma_start(wg[:, :], wg_dram).then_inc(sems["wg_in"], 16)
            if bg_dram is not None:
                sp.dma_start(bg[:, :], bg_dram.rearrange("(a n) -> a n", a=1).broadcast_to([P, E])).then_inc(sems["wg_in"], 16)

        @block.gpsimd
        def _(pool):
            pool.memset(ones[:, :], 1.0).then_inc(sems["filled"], 1)
            pool.iota(iota_i[:, :], [[1, E]], base=0, channel_multiplier=0).then_inc(sems["filled"], 1)
            if cap is None:
                pool.iota(starts_i[:, :], [[CHUNK, NC]], base=0, channel_multiplier=0).then_inc(sems["filled"], 1)
            pool.iota(token_i[:, :], [[P, NT]], base=0, channel_multiplier=1).then_inc(sems["filled"], 1)
            pool.memset(xn_all[:, :, D + 1:ROW], 0.0).then_inc(sems["filled"], 1)
            pool.wait_ge(sems["filled"], 5 if cap is None else 4)
            pool.tensor_copy(xn_all[:, :, D], token_i[:, :]).then_inc(sems["targets"], 1)
            pool.affine_select(out=before[:, :], in_=ones[:, :], compare_op=ALU.is_ge, fill=0.0, base=-1,
                               pattern=[[1, P]], channel_multiplier=-1).then_inc(sems["consts"], 1)
            pool.tensor_copy(iota[:, :], iota_i[:, :]).then_inc(sems["consts"], 1)
            if cap is None:
                pool.tensor_copy(starts[:, :], starts_i[:, :]).then_inc(sems["consts"], 1)
            for k in range(top):
                if k > 0:
                    pool.wait_ge(sems["scattered"], 16 * NT * k)
                    pool.wait_ge(sems["targets"], k)
                    pool.tensor_scalar(xn_all[:, :, D], xn_all[:, :, D], float(T), None, ALU.add).then_inc(sems["targets"], 1)
                pool.wait_ge(sems["targets"], k + 1)
                pool.wait_ge(sems["slots_ready"], k + 1)
                for t in range(NT):
                    pool.indirect_dma_start(
                        out=r.rows_in, out_offset=bass.IndirectOffsetOnAxis(ap=r.slot[:, k, t:t + 1], axis=0),
                        in_=xn_all[:, t, :], in_offset=None, bounds_check=r.rows_in.shape[0] - 1, oob_is_err=False
                    ).then_inc(sems["scattered"], 16)
            pool.wait_ge(sems["scattered"], 16 * NT * top)

        @block.tensor
        def _(pe):
            def turn(c):
                pe.wait_ge(sems["xn_ready"], G * (c + 1))
                reused(pe, sems["xT_ready"], c - 1)
                for g in range(G):
                    last = nc.tensor.transpose(ps_x[c % 2][:, g * P:(g + 1) * P], xn_all[:, c * G + g, 0:D], core.ident[:, :])
                last.then_inc(sems["xT_ps"], 1)

            def logits(c):
                pe.wait_ge(sems["xT_ready"], c + 1)
                for g in range(G):
                    t = c * G + g
                    last = nc.tensor.matmul(ps_l[:, t * E:(t + 1) * E], xT[:, c % 2, g * P:(g + 1) * P], wg[:, :], start=True, stop=True)
                last.then_inc(sems["l_ps"], 1)
            pe.wait_ge(sems["wg_in"], 16 if bg_dram is None else 32)
            turn(0)
            for c in range(NT // G):
                if c + 1 < NT // G:
                    turn(c + 1)
                logits(c)
            pe.wait_ge(sems["consts"], 2)
            pe.wait_ge(sems["member_ready"], 1)
            flat_member = member[:, :, :].rearrange("p t e -> p (t e)")
            nc.tensor.matmul(ps_before[:, 0:NT * E], before[:, :], flat_member, start=True, stop=True).then_inc(sems["prefix_ps"], 1)
            nc.tensor.matmul(ps_total[:, 0:NT * E], ones[:, :], flat_member, start=True, stop=True).then_inc(sems["prefix_ps"], 1)

        @block.scalar
        def _(act):
            root_on_scalar(act)

            for c in range(NT // G):
                act.wait_ge(sems["xT_ps"], c + 1)
                reused(act, sems["l_ps"], c - 1)
                nc.scalar.copy(xT[:, c % 2, :], ps_x[c % 2][:, :]).then_inc(sems["xT_ready"], 1)
            act.wait_ge(sems["exp_in"], 1)
            if top == 1:
                nc.scalar.activation(tmp[:, :, :], tmp[:, :, :], ACT.Exp).then_inc(sems["exp_out"], 1)
            else:
                nc.scalar.activation(total[:, :], total[:, :], ACT.Exp, scale=1.0 / temp).then_inc(sems["exp_out"], 1)

        @block.vector
        def _(dve):
            root_on_vector(dve)
            dve.wait_ge(sems["wg_in"], 16 if bg_dram is None else 32)

            with dve.Fori(0, NT // UNROLL) as g:
                for j in range(UNROLL):
                    t = g * UNROLL + j
                    nc.vector.tensor_scalar(xn_all[:, t, 0:D], core.x[:, t, :], core.mean[:, bass.ts(t, 1)],
                                            core.rstd[:, bass.ts(t, 1)], ALU.subtract, ALU.mult).then_inc(sems["xn_ready"], 1)
            dve.wait_ge(sems["l_ps"], NT // G)
            src = ps_l[:, 0:NT * E].rearrange("p (t e) -> p t e", e=E)
            if bg_dram is not None:
                nc.vector.tensor_tensor(lg[:, :, :], src, bg[:, :].unsqueeze(1).broadcast_to([P, NT, E]), ALU.add).then_inc(sems["lg_ready"], 1)
            elif clamp is not None:
                nc.vector.tensor_scalar(lg[:, :, :], src, clamp, -clamp, ALU.min, ALU.max).then_inc(sems["lg_ready"], 1)
            else:
                nc.vector.tensor_copy(lg[:, :, :], src).then_inc(sems["lg_ready"], 1)
            dve.wait_ge(sems["lg_ready"], 1)
            dve.wait_ge(sems["consts"], 3 if cap is None else 2)

            steps = [0]

            def step(ins):
                steps[0] += 1
                ins.then_inc(step_sem, 1)
                dve.wait_ge(step_sem, steps[0])

            def over_experts(ap):
                return ap.unsqueeze(2).broadcast_to([P, NT, E])

            def over_tokens(ap):
                return ap.unsqueeze(1).broadcast_to([P, NT, E])
            V = nc.vector
            for k in range(top):
                step(V.tensor_reduce(best[:, k, :], lg[:, :, :], AX.X, ALU.max))
                if k == 0 and top == 1:
                    step(V.tensor_tensor(tmp[:, :, :], lg[:, :, :], over_experts(best[:, 0, :]), ALU.subtract))
                    nc.vector.memset(total[:, 0:1], 0.0).then_inc(sems["exp_in"], 1)
                    dve.wait_ge(sems["exp_out"], 1)
                    step(V.tensor_reduce(total[:, :], tmp[:, :, :], AX.X, ALU.add))
                    step(V.reciprocal(total[:, :], total[:, :]))
                step(V.tensor_tensor(tmp[:, :, :], lg[:, :, :], over_experts(best[:, k, :]), ALU.is_equal))
                step(V.scalar_tensor_tensor(out=tmp[:, :, :], in0=tmp[:, :, :], scalar=-float(E), in1=over_tokens(iota[:, :]),
                                            op0=ALU.mult, op1=ALU.add))
                step(V.tensor_reduce(index[:, :], tmp[:, :, :], AX.X, ALU.min))
                step(V.tensor_scalar(index[:, :], index[:, :], float(E), None, ALU.add))
                step(V.tensor_tensor(picks[k][:, :, :], over_tokens(iota[:, :]), over_experts(index[:, :]), ALU.is_equal))
                if k + 1 < top:
                    step(V.scalar_tensor_tensor(out=lg[:, :, :], in0=picks[k][:, :, :], scalar=MASKED, in1=lg[:, :, :],
                                                op0=ALU.mult, op1=ALU.add))
            if top == 1:
                V.tensor_copy(member[:, :, :], picks[0][:, :, :]).then_inc(sems["member_ready"], 1)
                step(V.tensor_scalar(r.weight[:, 0, :], total[:, :], core.gates[:, gate:gate + 1], None, ALU.mult))
            else:
                V.tensor_tensor(member[:, :, :], picks[0][:, :, :], picks[1][:, :, :], ALU.add).then_inc(sems["member_ready"], 1)
                V.tensor_tensor(total[:, :], best[:, 1, :], best[:, 0, :], ALU.subtract).then_inc(sems["exp_in"], 1)
                dve.wait_ge(sems["exp_out"], 1)
                step(V.tensor_scalar(index[:, :], total[:, :], 1.0, sum_eps, ALU.add, ALU.add))
                step(V.reciprocal(index[:, :], index[:, :]))
                if gate is not None:
                    step(V.tensor_scalar(index[:, :], index[:, :], core.gates[:, gate:gate + 1], None, ALU.mult))
                step(V.tensor_copy(r.weight[:, 0, :], index[:, :]))
                step(V.tensor_tensor(r.weight[:, 1, :], total[:, :], index[:, :], ALU.mult))
            dve.wait_ge(sems["prefix_ps"], 2)
            tot = ps_total[:, 0:NT * E].rearrange("p (t e) -> p t e", e=E)
            step(V.tensor_copy(tmp[:, :, :], tot))
            src, k, width = tmp, 0, 1
            while width < NT:
                dst = scan[k]
                step(V.tensor_copy(dst[:, 0:width, :], src[:, 0:width, :]))
                step(V.tensor_tensor(dst[:, width:NT, :], src[:, width:NT, :], src[:, 0:NT - width, :], ALU.add))
                src, k, width = dst, 1 - k, 2 * width
            counts = src
            step(V.tensor_tensor(pos[:, :, :], counts[:, :, :], tmp[:, :, :], ALU.subtract))
            step(V.tensor_tensor(pos[:, :, :], pos[:, :, :], ps_before[:, 0:NT * E].rearrange("p (t e) -> p t e", e=E), ALU.add))
            slot_of = scan[k]
            if cap is not None:
                step(V.tensor_scalar(iota[:, :], iota[:, :], float(cap), None, ALU.mult))
                base = iota
            else:
                n = counts[:, NT - 1, :]
                step(V.tensor_tensor(more[:, :, :], n.unsqueeze(2).broadcast_to([P, E, NC]),
                                     starts[:, :].unsqueeze(1).broadcast_to([P, E, NC]), ALU.is_gt))
                step(V.tensor_reduce(chunks[:, :], more[:, :, :], AX.X, ALU.add))
                step(V.tensor_scalar(chunks[:, :], chunks[:, :], float(CHUNK), None, ALU.mult))
                e_src, ke, width = chunks, 0, 1
                while width < E:
                    step(V.tensor_copy(ends[ke][:, 0:width], e_src[:, 0:width]))
                    step(V.tensor_tensor(ends[ke][:, width:E], e_src[:, width:E], e_src[:, 0:E - width], ALU.add))
                    e_src, ke, width = ends[ke], 1 - ke, 2 * width
                step(V.tensor_tensor(more[:, :, :], starts[:, :].unsqueeze(1).broadcast_to([P, E, NC]),
                                     e_src[:, :].unsqueeze(2).broadcast_to([P, E, NC]), ALU.is_ge))
                step(V.tensor_reduce(ce[:, :], more[:, :, :].rearrange("p e c -> p c e"), AX.X, ALU.add))
                step(V.tensor_scalar(ce[:, :], ce[:, :], float(E - 1), None, ALU.min))
                step(V.tensor_copy(r.chunk_expert[:, :], ce[0:1, :]))
                step(V.tensor_tensor(chunks[:, :], e_src[:, :], chunks[:, :], ALU.subtract))
                base = chunks
            step(V.tensor_tensor(slot_of[:, :, :], pos[:, :, :], over_tokens(base[:, :]), ALU.add))
            for k in range(top):
                step(V.tensor_tensor(tmp[:, :, :], slot_of[:, :, :], picks[k][:, :, :], ALU.mult))
                step(V.tensor_reduce(choice_slot[:, :], tmp[:, :, :], AX.X, ALU.add))
                if cap is not None:
                    step(V.tensor_tensor(tmp[:, :, :], pos[:, :, :], picks[k][:, :, :], ALU.mult))
                    step(V.tensor_reduce(choice_pos[:, :], tmp[:, :, :], AX.X, ALU.add))
                    step(V.tensor_scalar(choice_pos[:, :], choice_pos[:, :], float(cap), None, ALU.is_ge))
                    step(V.scalar_tensor_tensor(out=choice_slot[:, :], in0=choice_pos[:, :], scalar=NOWHERE, in1=choice_slot[:, :],
                                                op0=ALU.mult, op1=ALU.add))
                    step(V.tensor_scalar(choice_pos[:, :], choice_pos[:, :], -1.0, 1.0, ALU.mult, ALU.add))
                    step(V.tensor_tensor(r.weight[:, k, :], r.weight[:, k, :], choice_pos[:, :], ALU.mult))
                V.tensor_copy(r.slot[:, k, :], choice_slot[:, :]).then_inc(sems["slots_ready"], 1)
                dve.wait_ge(sems["slots_ready"], k + 1)

def experts(nc, core, name, r, sets, inner, w1_dram, w2_dram, act_func, w3_dram=None, b1_dram=None, b2_dram=None, dynamic=False):
    F = w1_dram.shape[2]
    FC = F // P
    A = CHUNK // P
    BUFS = 4 if inner == 1 else 2
    STEP = BUFS * inner
    ROWS = 4 if STEP % 4 == 0 else 5
    with Phase(nc, name) as ph:
        w1 = ph.sb("w1", [P, BUFS, F])
        w3 = ph.sb("w3", [P, BUFS, F]) if w3_dram is not None else None
        w2 = ph.sb("w2", [P, BUFS, FC, D])
        b1 = ph.sb("b1", [P, BUFS, FC]) if b1_dram is not None else None
        b2 = ph.sb("b2", [P, BUFS, D]) if b2_dram is not None else None
        rows = ph.sb("rows", [P, ROWS, A, ROW])
        target = ph.sb("target", [P, 2, A], U32)
        xT = ph.sb("xT", [P, 2, CHUNK])
        hT = ph.sb("hT", [P, 2, FC, CHUNK])
        sT = ph.sb("sT", [P, 2, CHUNK]) if w3_dram is not None else None
        y = ph.sb("y", [P, 2, A, D])
        ps_x = ph.ps("ps_x", [P, CHUNK])
        ps_h = [ph.ps(f"ps_h{k}", [P, 512]) for k in range(4)]
        ps_y = [ph.ps(f"ps_y{k}", [P, 512]) for k in range(A)]
        w_in = [ph.sem(f"w_in{k}") for k in range(BUFS)]
        rows_in = [ph.sem(f"rows_in{k}") for k in range(ROWS)]
        stored = [ph.sem("stored0"), ph.sem("stored1")]
        xT_ps, xT_ready, h_ps, h_ready = ph.sem("xT_ps"), ph.sem("xT_ready"), ph.sem("h_ps"), ph.sem("h_ready")
        paced = ph.sem("paced")
        s_ready, y_ps, y_ready, target_ready = ph.sem("s_ready"), ph.sem("y_ps"), ph.sem("y_ready"), ph.sem("target_ready")
        set_dmas = 2 + (w3 is not None) + (b1 is not None) + (b2 is not None)
        in_tiles = r.rows_in.rearrange("(n a p) d -> n p a d", p=P, a=A)
        w2_tiles = w2_dram.rearrange("e (f p) d -> e p f d", p=P)
        block = ph.ctx.enter_context(nc.Block())

        def run(eng, one):
            for c in range(STEP):
                one(0, c)
            with eng.Fori(1, sets // BUFS - 1) as u:
                for c in range(STEP):
                    one(u, c)
            for c in range(STEP):
                one(sets // BUFS - 1, c)

        def set_arrived(eng, u, c):
            if c % inner == 0:
                eng.wait_ge(w_in[c // inner], (u + 1) * (16 * set_dmas))

        def is_last(u, c):
            return isinstance(u, int) and u == sets // BUFS - 1 and c == STEP - 1

        @block.sync
        def _(sp):
            def load_set(u, k):
                if not isinstance(u, int) or u > 0:
                    sp.wait_ge(y_ready, u * STEP + (k + 1 - BUFS) * inner)
                e = u * BUFS + k
                if dynamic:
                    at = r.chunk_expert[0:1, e:e + 1] if isinstance(e, int) else r.chunk_expert[0:1, bass.ts(e, 1)]
                    e = sp.value_load(at, min_val=0, max_val=r.experts - 1)
                sp.dma_start(w1[:, k, :], w1_dram[e, :, :]).then_inc(w_in[k], 16)
                if w3 is not None:
                    sp.dma_start(w3[:, k, :], w3_dram[e, :, :]).then_inc(w_in[k], 16)
                if b1 is not None:
                    sp.dma_start(b1[:, k, :], b1_dram[e, :, :]).then_inc(w_in[k], 16)
                if b2 is not None:
                    sp.dma_start(b2[:, k, :], b2_dram[e, :, :].broadcast_to([P, D])).then_inc(w_in[k], 16)
                sp.dma_start(w2[:, k, :, :], w2_tiles[e, :, :, :]).then_inc(w_in[k], 16)

            def one(u, c):
                if c % inner == 0:
                    load_set(u, c // inner)
                q = u * STEP + c
                reused(sp, target_ready, q - ROWS + 1)
                sp.dma_start(rows[:, c % ROWS, :, :], in_tiles[q, :, :, :]).then_inc(rows_in[c % ROWS], 16)
            run(sp, one)

        @block.tensor
        def _(pe):
            def turn(u, c):
                pe.wait_ge(rows_in[c % ROWS], u * (16 * (STEP // ROWS)) + 16 * (c // ROWS + 1))
                reused(pe, xT_ready, u * STEP + c)
                for a in range(A):
                    last = nc.tensor.transpose(ps_x[:, a * P:(a + 1) * P], rows[:, c % ROWS, a, 0:D], core.ident[:, :])
                last.then_inc(xT_ps, 1)

            def one(u, c):
                q, k, b = u * STEP + c, c // inner, c % 2
                set_arrived(pe, u, c)
                pe.wait_ge(xT_ready, q + 1)
                for f in range(FC):
                    if w3 is None:
                        reused(pe, h_ready, (q - 1) * FC + (f + 1))
                        nc.tensor.matmul(ps_h[f][:, 0:CHUNK], w1[:, k, f * P:(f + 1) * P], xT[:, b, :], start=True, stop=True
                                         ).then_inc(h_ps, 1)
                    else:
                        reused(pe, h_ready, q * FC + (f - 1))
                        nc.tensor.matmul(ps_h[f % 2][:, 0:CHUNK], w1[:, k, f * P:(f + 1) * P], xT[:, b, :], start=True, stop=True)
                        nc.tensor.matmul(ps_h[2 + f % 2][:, 0:CHUNK], w3[:, k, f * P:(f + 1) * P], xT[:, b, :], start=True, stop=True
                                         ).then_inc(h_ps, 1)
                if not is_last(u, c):
                    turn(*((u, c + 1) if c + 1 < STEP else (u + 1, 0)))
                for f in range(FC):
                    pe.wait_ge(h_ready, q * FC + (f + 1))
                    if f == 0:
                        reused(pe, y_ready, q)
                    for a in range(A):
                        last = nc.tensor.matmul(ps_y[a][:, 0:D], hT[:, b, f, a * P:(a + 1) * P], w2[:, k, f, :],
                                                start=(f == 0), stop=(f == FC - 1))
                last.then_inc(y_ps, 1)
            turn(0, 0)
            run(pe, one)

        @block.scalar
        def _(act):
            def one(u, c):
                q, k, b = u * STEP + c, c // inner, c % 2
                if b1 is not None:
                    set_arrived(act, u, c)
                for f in range(FC):
                    act.wait_ge(h_ps, q * FC + (f + 1))
                    if w3 is None:
                        if f == 0:
                            reused(act, y_ps, q - 1)
                        bias = {"bias": b1[:, k, f:f + 1]} if b1 is not None else {}
                        nc.scalar.activation(hT[:, b, f, :], ps_h[f][:, 0:CHUNK], act_func, **bias).then_inc(h_ready, 1)
                    else:
                        reused(act, h_ready, q * FC + (f - 1))
                        nc.scalar.activation(sT[:, f % 2, :], ps_h[f % 2][:, 0:CHUNK], act_func).then_inc(s_ready, 1)
            nc.scalar.preload_act_table(act_func)
            run(act, one)

        @block.vector
        def _(dve):
            def copy_x(u, c):
                q = u * STEP + c
                dve.wait_ge(xT_ps, q + 1)
                reused(dve, h_ps, (q - 1) * FC)
                nc.vector.tensor_copy(xT[:, c % 2, :], ps_x[:, :]).then_inc(xT_ready, 1)

            def one(u, c):
                q, k, b = u * STEP + c, c // inner, c % 2
                if w3 is not None:
                    for f in range(FC):
                        dve.wait_ge(s_ready, q * FC + (f + 1))
                        if f == 0:
                            reused(dve, y_ps, q - 1)
                        nc.vector.tensor_tensor(hT[:, b, f, :], sT[:, f % 2, :], ps_h[2 + f % 2][:, 0:CHUNK], ALU.mult
                                                ).then_inc(h_ready, 1)
                if not is_last(u, c):
                    copy_x(*((u, c + 1) if c + 1 < STEP else (u + 1, 0)))
                if b2 is not None:
                    set_arrived(dve, u, c)
                dve.wait_ge(y_ps, q + 1)
                reused(dve, stored[b], u * (8 * A * STEP) + 16 * A * (c // 2))
                nc.vector.tensor_copy(target[:, b, :], rows[:, c % ROWS, :, D]).then_inc(target_ready, 1)
                for a in range(A):
                    if b2 is not None:
                        last = nc.vector.tensor_tensor(y[:, b, a, :], ps_y[a][:, 0:D], b2[:, k, :], ALU.add)
                    else:
                        last = nc.vector.tensor_copy(y[:, b, a, :], ps_y[a][:, 0:D])
                last.then_inc(y_ready, 1)
            copy_x(0, 0)
            run(dve, one)

        @block.gpsimd
        def _(pool):
            def one(u, c):
                q = u * STEP + c
                pool.wait_ge(target_ready, q + 1)
                pool.wait_ge(y_ready, q + 1)
                pool.sem_inc(paced, 1)
                for a in range(A):
                    pool.indirect_dma_start(
                        out=r.rows_out, out_offset=bass.IndirectOffsetOnAxis(ap=target[:, c % 2, a:a + 1], axis=0),
                        in_=y[:, c % 2, a, :], in_offset=None, bounds_check=r.rows_out.shape[0] - 1, oob_is_err=False
                    ).then_inc(stored[c % 2], 16)
            run(pool, one)
            for b in range(2):
                pool.wait_ge(stored[b], 16 * A * (sets * inner // 2))


def combine(nc, core, name, r, norm=None, gate=None):
    top = r.top
    GROUP = 8
    NG = NT // GROUP
    with Phase(nc, name) as ph:
        got = ph.sb("got", [P, top, NT, D])
        lnp = ph.sb("lnp", [P, 2, D])
        lnp_in, scaled, normed = ph.sem("lnp_in"), ph.sem("scaled"), ph.sem("normed")
        rows_arrived = [ph.sem(f"rows_arrived{g}") for g in range(NG)]
        added, summed = ph.sem("added"), ph.sem("summed")
        root_on_scalar, root_on_vector = row_statistics(nc, ph, core)
        block = ph.ctx.enter_context(nc.Block())

        @block.sync
        def _(sp):
            if norm is not None:
                for k in range(2):
                    sp.dma_start(lnp[:, k, :], norm[k].rearrange("(a n) -> a n", a=1).broadcast_to([P, D])).then_inc(lnp_in, 16)
            tiles = r.rows_out.rearrange("(k n p) d -> k p n d", k=top, p=P)
            for g in range(NG):
                for k in range(top):
                    part = slice(g * GROUP, (g + 1) * GROUP)
                    sp.dma_start(got[:, k, part, :], tiles[k, :, part, :]).then_inc(rows_arrived[g], 16)

        @block.scalar
        def _(act):
            if norm is not None:
                root_on_scalar(act)

        @block.vector
        def _(dve):
            V = nc.vector
            if norm is not None:
                dve.wait_ge(lnp_in, 32)
                for k in range(2):
                    V.tensor_scalar(lnp[:, k, :], lnp[:, k, :], core.gates[:, gate:gate + 1], None, ALU.mult).then_inc(scaled, 1)
            if norm is not None:
                dve.wait_ge(scaled, 2)
                V.tensor_tensor(core.x[:, :, :], core.x[:, :, :], lnp[:, 1, :].unsqueeze(1).broadcast_to([P, NT, D]), ALU.add
                                ).then_inc(scaled, 1)
                dve.wait_ge(scaled, 3)
            for g in range(NG):
                dve.wait_ge(rows_arrived[g], 16 * top)
                tiles = range(g * GROUP, (g + 1) * GROUP)

                def sums(t):
                    return core.x[:, t, :] if norm is None else got[:, 0, t, :]
                for t in tiles:
                    if norm is None:
                        V.scalar_tensor_tensor(out=core.x[:, t, :], in0=got[:, 0, t, :], scalar=r.weight[:, 0, t:t + 1],
                                               in1=core.x[:, t, :], op0=ALU.mult, op1=ALU.add).then_inc(added, 1)
                    else:
                        V.tensor_scalar(got[:, 0, t, :], got[:, 0, t, :], r.weight[:, 0, t:t + 1], None, ALU.mult).then_inc(added, 1)
                n = (g + 1) * GROUP + g * GROUP * (top - 1)
                if top == 2:
                    for j, t in enumerate(tiles):
                        dve.wait_ge(added, n - GROUP + j + 1)
                        V.scalar_tensor_tensor(out=sums(t), in0=got[:, 1, t, :], scalar=r.weight[:, 1, t:t + 1],
                                               in1=sums(t), op0=ALU.mult, op1=ALU.add).then_inc(added, 1)
                    n += GROUP
                for j, t in enumerate(tiles):
                    dve.wait_ge(added, n - GROUP + j + 1)
                    V.bn_stats(core.bn[:, t, :], sums(t)).then_inc(summed, 1)
            if norm is not None:
                dve.wait_ge(summed, NT)
                root_on_vector(dve)
                with dve.Fori(0, NT // UNROLL) as g:
                    for j in range(UNROLL):
                        t = g * UNROLL + j
                        V.scalar_tensor_tensor(out=got[:, 0, t, :], in0=got[:, 0, t, :], scalar=core.mean[:, bass.ts(t, 1)],
                                               in1=lnp[:, 0, :], op0=ALU.subtract, op1=ALU.mult).then_inc(normed, 1)
                dve.wait_ge(normed, NT)
                with dve.Fori(0, NT // UNROLL) as g:
                    for j in range(UNROLL):
                        t = g * UNROLL + j
                        V.scalar_tensor_tensor(out=core.x[:, t, :], in0=got[:, 0, t, :], scalar=core.rstd[:, bass.ts(t, 1)],
                                               in1=core.x[:, t, :], op0=ALU.mult, op1=ALU.add).then_inc(normed, 1)
                dve.wait_ge(normed, 2 * NT)
                with dve.Fori(0, NT // UNROLL) as g:
                    for j in range(UNROLL):
                        V.bn_stats(core.bn[:, g * UNROLL + j, :], core.x[:, g * UNROLL + j, :]).then_inc(summed, 1)


def ternary_ffn(nc, core, name, gate, wfcT_dram, wprojT_dram, ln_w, ln_b):
    F = wfcT_dram.shape[1]
    FC = F // P
    with Phase(nc, name) as ph:
        wfc = ph.sb("wfc", [P, F])
        wproj = ph.sb("wproj", [P, FC, D])
        pos = ph.sb("pos", [P, F])
        neg = ph.sb("neg", [P, F])
        q_fc = ph.sb("q_fc", [P, F])
        q_proj = ph.sb("q_proj", [P, FC, D])
        w_out = ph.sb("w_out", [P, FC, D])
        lnw = ph.sb("lnw", [P, FC])
        lnb = ph.sb("lnb", [P, FC])
        shift = ph.sb("shift", [1, D])
        sums = ph.sb("sums", [P, 2])
        thr = ph.sb("thr", [P, 4])
        ones = ph.sb("ones", [P, P])
        half = ph.sb("half", [P, 1])
        xn = ph.sb("xn", [P, 2, D])
        xnT = ph.sb("xnT", [P, 2, P])
        h = ph.sb("h", [P, 2, F])
        hn = ph.sb("hn", [P, 2, F])
        hT = ph.sb("hT", [P, 2, F])
        bn = ph.sb("bn", [P, 2, 6])
        mv = ph.sb("mv", [P, 2, 2])
        ve = ph.sb("ve", [P, 2, 1])
        rs = ph.sb("rs", [P, 2, 1])
        ps_x = [ph.ps(f"ps_x{k}", [P, P]) for k in range(2)]
        ps_h = [ph.ps(f"ps_h{k}", [P, F]) for k in range(2)]
        ps_t = [ph.ps(f"ps_t{k}", [P, F]) for k in range(2)]
        ps_y = [ph.ps(f"ps_y{k}", [P, D]) for k in range(2)]
        s = {n: ph.sem(n) for n in ("w_in filled summed0 sums_ps signs quantised shift_ps shift_ready xn_ready xnT_ps xnT_ready h_ps "
                                    "h_ready bn_ready mv_ready ve_ready rs_ready hn_ready hT_ps hT_ready y_ps x_ready summed").split()}
        root_on_scalar, root_on_vector = row_statistics(nc, ph, core)
        block = ph.ctx.enter_context(nc.Block())

        def for_tile(part):
            def run(t, k):
                if not isinstance(t, int) or 0 <= t < NT:
                    part(t, k)
            return run

        def steps(eng, step):
            for t in range(-3, 4):
                step(t, t % 2)
            with eng.Fori(2, NT // 2 - 2) as u:
                step(u * 2, 0)
                step(u * 2 + 1, 1)
            for t in range(NT - 4, NT + 1):
                step(t, t % 2)

        @block.sync
        def _(sp):
            sp.dma_start(wfc[:, :], wfcT_dram).then_inc(s["w_in"], 16)
            sp.dma_start(wproj[:, :, :], wprojT_dram.rearrange("(f p) d -> p f d", p=P)).then_inc(s["w_in"], 16)
            sp.dma_start(lnw[:, :], ln_w).then_inc(s["w_in"], 16)
            sp.dma_start(lnb[:, :], ln_b).then_inc(s["w_in"], 16)

        @block.gpsimd
        def _(pool):
            pool.memset(ones[:, :], 1.0).then_inc(s["filled"], 1)
            pool.memset(half[:, :], -0.5).then_inc(s["filled"], 1)
            pool.wait_ge(s["filled"], 2)

            @for_tile
            def root(t, k):
                pool.wait_ge(s["ve_ready"], t + 1)
                reused(pool, s["hn_ready"], t - 1)
                pool.tensor_tensor(rs[:, k, :], ve[:, k, :], half[:, :], ALU.pow).then_inc(s["rs_ready"], 1)

            def step(t, k):
                root(t + 2, k)
            steps(pool, step)

        @block.tensor
        def _(pe):
            pe.wait_ge(s["filled"], 2)
            pe.wait_ge(s["summed0"], 2)
            nc.tensor.matmul(ps_y[0][:, 0:2], ones[:, :], sums[:, :], start=True, stop=True).then_inc(s["sums_ps"], 1)
            pe.wait_ge(s["quantised"], 3)
            for f in range(FC):
                last = nc.tensor.matmul(ps_y[0][0:1, 0:D], lnb[:, f:f + 1], q_proj[:, f, :], start=(f == 0), stop=(f == FC - 1))
            last.then_inc(s["shift_ps"], 1)
            pe.wait_ge(s["shift_ready"], 1)

            @for_tile
            def turn_x(t, k):
                pe.wait_ge(s["xn_ready"], t + 1)
                reused(pe, s["xnT_ready"], t - 1)
                nc.tensor.transpose(ps_x[k][:, :], xn[:, k, :], core.ident[:, :]).then_inc(s["xnT_ps"], 1)

            @for_tile
            def hidden(t, k):
                pe.wait_ge(s["xnT_ready"], t + 1)
                reused(pe, s["h_ready"], t - 1)
                nc.tensor.matmul(ps_h[k][:, :], xnT[:, k, :], q_fc[:, :], start=True, stop=True).then_inc(s["h_ps"], 1)

            @for_tile
            def turn_h(t, k):
                pe.wait_ge(s["hn_ready"], t + 1)
                reused(pe, s["hT_ready"], t - 1)
                for f in range(FC):
                    last = nc.tensor.transpose(ps_t[k][:, f * P:(f + 1) * P], hn[:, k, f * P:(f + 1) * P], core.ident[:, :])
                last.then_inc(s["hT_ps"], 1)

            @for_tile
            def project(t, k):
                pe.wait_ge(s["hT_ready"], t + 1)
                reused(pe, s["x_ready"], t - 1)
                for f in range(FC):
                    nc.tensor.matmul(ps_y[k][:, :], hT[:, k, f * P:(f + 1) * P], w_out[:, f, :], start=(f == 0), stop=False)
                nc.tensor.matmul(ps_y[k][:, :], core.ones[:, :], shift[:, :], start=False, stop=True).then_inc(s["y_ps"], 1)

            def step(t, k):
                turn_x(t + 2, k)
                turn_h(t, k)
                hidden(t + 2, k)
                project(t, k)
            steps(pe, step)

        @block.scalar
        def _(act):
            root_on_scalar(act)

            @for_tile
            def turned_x(t, k):
                act.wait_ge(s["xnT_ps"], t + 1)
                reused(act, s["h_ps"], t - 1)
                nc.scalar.copy(xnT[:, k, :], ps_x[k][:, :]).then_inc(s["xnT_ready"], 1)

            @for_tile
            def hidden(t, k):
                act.wait_ge(s["h_ps"], t + 1)
                reused(act, s["hn_ready"], t - 1)
                nc.scalar.activation(h[:, k, :], ps_h[k][:, :], ACT.Gelu).then_inc(s["h_ready"], 1)

            @for_tile
            def turned_h(t, k):
                act.wait_ge(s["hT_ps"], t + 1)
                reused(act, s["y_ps"], t - 1)
                nc.scalar.copy(hT[:, k, :], ps_t[k][:, :]).then_inc(s["hT_ready"], 1)

            def step(t, k):
                turned_x(t + 2, k)
                turned_h(t, k)
                hidden(t + 2, k)
            nc.scalar.preload_act_table(ACT.Gelu)
            steps(act, step)

        @block.vector
        def _(dve):
            V = nc.vector
            root_on_vector(dve)
            dve.wait_ge(s["w_in"], 64)
            for k, w in enumerate((wfc[:, :], wproj[:, :, :].rearrange("p f d -> p (f d)"))):
                V.tensor_reduce(sums[:, k:k + 1], w, AX.X, ALU.add, apply_absolute_value=True).then_inc(s["summed0"], 1)
            dve.wait_ge(s["sums_ps"], 1)
            V.tensor_scalar(thr[:, 0:2], ps_y[0][:, 0:2], 1.0 / (P * F), 1e-6, ALU.mult, ALU.add).then_inc(s["signs"], 1)
            dve.wait_ge(s["signs"], 1)
            V.tensor_scalar(thr[:, 2:4], thr[:, 0:2], -0.5, None, ALU.mult).then_inc(s["signs"], 1)
            dve.wait_ge(s["signs"], 2)
            V.tensor_scalar(thr[:, 0:2], thr[:, 0:2], 0.5, None, ALU.mult).then_inc(s["signs"], 1)
            dve.wait_ge(s["signs"], 3)
            for k, (w, q) in enumerate(((wfc[:, :], q_fc[:, :]), (wproj[:, :, :].rearrange("p f d -> p (f d)"), q_proj[:, :, :].rearrange("p f d -> p (f d)")))):
                n = 3 + 2 * k
                reused(dve, s["quantised"], k)
                V.tensor_scalar(pos[:, :], w, thr[:, k:k + 1], None, ALU.is_gt).then_inc(s["signs"], 1)
                V.tensor_scalar(neg[:, :], w, thr[:, 2 + k:3 + k], None, ALU.is_lt).then_inc(s["signs"], 1)
                dve.wait_ge(s["signs"], n + 2)
                V.tensor_tensor(q, pos[:, :], neg[:, :], ALU.subtract).then_inc(s["quantised"], 1)
            dve.wait_ge(s["quantised"], 2)
            V.tensor_tensor(w_out[:, :, :], q_proj[:, :, :], lnw[:, :].unsqueeze(2).broadcast_to([P, FC, D]), ALU.mult).then_inc(s["quantised"], 1)
            dve.wait_ge(s["shift_ps"], 1)
            V.tensor_copy(shift[:, :], ps_y[0][0:1, 0:D]).then_inc(s["shift_ready"], 1)

            @for_tile
            def normalise(t, k):
                reused(dve, s["xnT_ps"], t - 1)
                V.tensor_scalar(xn[:, k, :], core.x[:, t, :], core.mean[:, bass.ts(t, 1)], core.rstd[:, bass.ts(t, 1)],
                                ALU.subtract, ALU.mult).then_inc(s["xn_ready"], 1)

            @for_tile
            def variance(t, k):
                dve.wait_ge(s["h_ready"], t + 1)
                V.bn_stats(bn[:, k, :], h[:, k, :]).then_inc(s["bn_ready"], 1)
                dve.wait_ge(s["w_in"], 64)
                dve.wait_ge(s["bn_ready"], t + 1)
                V.bn_aggr(mv[:, k, :], bn[:, k, :]).then_inc(s["mv_ready"], 1)
                dve.wait_ge(s["mv_ready"], t + 1)
                V.tensor_scalar(ve[:, k, :], mv[:, k, 1:2], LN_EPS, None, ALU.add).then_inc(s["ve_ready"], 1)

            @for_tile
            def inner(t, k):
                dve.wait_ge(s["rs_ready"], t + 1)
                reused(dve, s["hT_ps"], t - 1)
                V.tensor_scalar(hn[:, k, :], h[:, k, :], mv[:, k, 0:1], rs[:, k, :], ALU.subtract, ALU.mult).then_inc(s["hn_ready"], 1)

            @for_tile
            def residual(t, k):
                dve.wait_ge(s["y_ps"], t + 1)
                V.scalar_tensor_tensor(out=core.x[:, t, :], in0=ps_y[k][:, :], scalar=core.gates[:, gate:gate + 1],
                                       in1=core.x[:, t, :], op0=ALU.mult, op1=ALU.add).then_inc(s["x_ready"], 1)
                dve.wait_ge(s["x_ready"], t + 1)
                dve.wait_ge(s["w_in"], 64)
                V.bn_stats(core.bn[:, t, :], core.x[:, t, :]).then_inc(s["summed"], 1)

            def step(t, k):
                inner(t + 1, 1 - k)
                normalise(t + 3, 1 - k)
                residual(t - 1, 1 - k)
                variance(t + 2, k)
            steps(dve, step)


def attention1(nc, core, name, gate, wT_dram, b_dram, ctx_dram, pad_dram):
    G = 4
    NSTEP = NT // G
    with Phase(nc, name) as ph:
        wT = ph.sb("wT", [P, D])
        b = ph.sb("b", [P, 1])
        pad = ph.sb("pad", [P, 2, NT, S], U8)
        neg = ph.sb("neg", [P, NT, P])
        across = ph.sb("across", [P, P])
        yp = ph.sb("yp", [P, T])
        cx = ph.sb("cx", [P, NT, D])
        xn = ph.sb("xn", [P, G, D])
        xnT = ph.sb("xnT", [P, G * P])
        xp = ph.sb("xp", [P, G * P])
        s1 = ph.sb("s1", [P, G, P])
        nmx = ph.sb("nmx", [P, G])
        p = ph.sb("p", [P, G, P])
        den = ph.sb("den", [P, G])
        rg = ph.sb("rg", [P, G])
        rgate = ph.sb("rgate", [P, G])
        pT = ph.sb("pT", [P, G * P])
        ps_x, ps_p, ps_s, ps_t, ps_o = (ph.ps(n, [P, G * P]) for n in ("ps_x", "ps_p", "ps_s", "ps_t", "ps_o"))
        ps_c = [ph.ps(f"ps_c{k}", [P, 512]) for k in range(2)]
        s = {n: ph.sem(n) for n in ("w_in pad_in cx_in filled across_ready neg_ready c_ps yp_ready xn_ready xnT_ps xnT_ready p_ps "
                                    "xp_ready s_ps s1_ready max_ready p_ready pT_ps pT_ready o_ps den_ready rg_ready x_ready summed").split()}
        root_on_scalar, root_on_vector = row_statistics(nc, ph, core)
        block = ph.ctx.enter_context(nc.Block())

        @block.sync
        def _(sp):
            sp.dma_start(wT[:, :], wT_dram).then_inc(s["w_in"], 16)
            sp.dma_start(b[:, :], b_dram.rearrange("(r a) -> r a", a=1)).then_inc(s["w_in"], 16)
            src = pad_dram.rearrange("(a b) k -> a (b k)", a=1)
            sp.dma_start(pad[:, :, :, :].rearrange("p b n k -> p (b n k)"), src.broadcast_to([P, NT * P])).then_inc(s["pad_in"], 16)
            sp.dma_start(cx[:, :, :], flat(ctx_dram).rearrange("(n p) d -> p n d", p=P)).then_inc(s["cx_in"], 16)

        @block.gpsimd
        def _(pool):
            pool.memset(across[:, :], 0.0).then_inc(s["filled"], 1)
            pool.wait_ge(s["filled"], 1)
            for k in range(2):
                pool.memset(across[64 * k:64 * k + 64, 64 * (1 - k):64 * (1 - k) + 64], MASKED).then_inc(s["across_ready"], 1)

        @block.tensor
        def _(pe):
            pe.wait_ge(s["w_in"], 32)
            for c in range(T // 512):
                reused(pe, s["yp_ready"], c - 1)
                nc.tensor.matmul(ps_c[c % 2][:, :], wT[:, :], core.ctxT[:, c * 512:(c + 1) * 512], start=True, stop=True).then_inc(s["c_ps"], 1)

            def front(t):
                pe.wait_ge(s["xn_ready"], t * G + G)
                reused(pe, s["xnT_ready"], t)
                for g in range(G):
                    last = nc.tensor.transpose(ps_x[:, g * P:(g + 1) * P], xn[:, g, :], core.ident[:, :])
                last.then_inc(s["xnT_ps"], 1)
                pe.wait_ge(s["xnT_ready"], t + 1)
                reused(pe, s["xp_ready"], t)
                nc.tensor.matmul(ps_p[:, :], wT[:, :], xnT[:, :], start=True, stop=True).then_inc(s["p_ps"], 1)

            def scores(t):
                pe.wait_ge(s["xp_ready"], t + 1)
                reused(pe, s["s1_ready"], t)
                for g in range(G):
                    last = nc.tensor.matmul(ps_s[:, g * P:(g + 1) * P], xp[:, g * P:(g + 1) * P], yp[:, bass.ts(t * G + g, P)], start=True, stop=True)
                last.then_inc(s["s_ps"], 1)

            def values(t):
                pe.wait_ge(s["p_ready"], t * G + G)
                reused(pe, s["pT_ready"], t)
                for g in range(G):
                    last = nc.tensor.transpose(ps_t[:, g * P:(g + 1) * P], p[:, g, :], core.ident[:, :])
                last.then_inc(s["pT_ps"], 1)
                pe.wait_ge(s["pT_ready"], t + 1)
                reused(pe, s["x_ready"], t * G)
                for g in range(G):
                    last = nc.tensor.matmul(ps_o[:, g * P:(g + 1) * P], pT[:, g * P:(g + 1) * P], cx[:, t * G + g, :], start=True, stop=True)
                last.then_inc(s["o_ps"], 1)
            pe.wait_ge(s["yp_ready"], T // 512)
            pe.wait_ge(s["cx_in"], 16)
            front(0)
            scores(0)
            front(1)
            values(0)
            with pe.Fori(1, NSTEP - 1) as t:
                scores(t)
                front(t + 1)
                values(t)
            scores(NSTEP - 1)
            values(NSTEP - 1)

        @block.scalar
        def _(act):
            root_on_scalar(act)
            act.wait_ge(s["w_in"], 32)
            for c in range(T // 512):
                act.wait_ge(s["c_ps"], c + 1)
                nc.scalar.activation(yp[:, c * 512:(c + 1) * 512], ps_c[c % 2][:, :], ACT.Relu, bias=b[:, :]).then_inc(s["yp_ready"], 1)
            nc.scalar.preload_act_table(ACT.Exp)

            def front(t):
                act.wait_ge(s["xnT_ps"], t + 1)
                reused(act, s["p_ps"], t)
                nc.scalar.copy(xnT[:, :], ps_x[:, :]).then_inc(s["xnT_ready"], 1)
                act.wait_ge(s["p_ps"], t + 1)
                reused(act, s["s_ps"], t)
                nc.scalar.activation(xp[:, :], ps_p[:, :], ACT.Relu, bias=b[:, :]).then_inc(s["xp_ready"], 1)

            def exponent(t):
                act.wait_ge(s["max_ready"], t + 1)
                reused(act, s["pT_ps"], t)
                reused(act, s["rg_ready"], t)
                for g in range(G):
                    nc.scalar.activation(p[:, g, :], s1[:, g, :], ACT.Exp, bias=nmx[:, g:g + 1], accum_out=den[:, g:g + 1]).then_inc(s["p_ready"], 1)

            def turned(t):
                act.wait_ge(s["pT_ps"], t + 1)
                reused(act, s["o_ps"], t)
                nc.scalar.copy(pT[:, :], ps_t[:, :]).then_inc(s["pT_ready"], 1)
            front(0)
            exponent(0)
            front(1)
            turned(0)
            with act.Fori(1, NSTEP - 1) as t:
                exponent(t)
                front(t + 1)
                turned(t)
            exponent(NSTEP - 1)
            turned(NSTEP - 1)

        @block.vector
        def _(dve):
            V = nc.vector
            root_on_vector(dve)
            dve.wait_ge(s["pad_in"], 16)
            dve.wait_ge(s["across_ready"], 2)
            for b in range(2):
                V.scalar_tensor_tensor(out=neg[:, :, b * S:(b + 1) * S], in0=pad[:, b, :, :], scalar=MASKED,
                                       in1=across[:, b * S:(b + 1) * S].unsqueeze(1).broadcast_to([P, NT, S]),
                                       op0=ALU.mult, op1=ALU.add).then_inc(s["neg_ready"], 1)
            dve.wait_ge(s["neg_ready"], 2)

            def normalise(t):
                reused(dve, s["xnT_ps"], t)
                for g in range(G):
                    at = bass.ts(t * G + g, 1)
                    V.tensor_scalar(xn[:, g, :], core.x[:, t * G + g, :], core.mean[:, at], core.rstd[:, at],
                                    ALU.subtract, ALU.mult).then_inc(s["xn_ready"], 1)

            def softmax(t):
                dve.wait_ge(s["s_ps"], t + 1)
                reused(dve, s["p_ready"], t * G)
                V.tensor_tensor(s1[:, :, :], ps_s[:, :].rearrange("p (g k) -> p g k", g=G), neg[:, bass.ts(t, G), :], ALU.add).then_inc(s["s1_ready"], 1)
                dve.wait_ge(s["s1_ready"], t + 1)
                V.tensor_reduce(nmx[:, :], s1[:, :, :], AX.X, ALU.max, negate=True).then_inc(s["max_ready"], 1)

            def residual(t):
                dve.wait_ge(s["p_ready"], t * G + G)
                reused(dve, s["rg_ready"], t)
                V.reciprocal(rg[:, :], den[:, :]).then_inc(s["den_ready"], 1)
                dve.wait_ge(s["den_ready"], t + 1)
                reused(dve, s["x_ready"], t * G)
                V.tensor_scalar(rgate[:, :], rg[:, :], core.gates[:, gate:gate + 1], None, ALU.mult).then_inc(s["rg_ready"], 1)
                dve.wait_ge(s["rg_ready"], t + 1)
                dve.wait_ge(s["o_ps"], t + 1)
                for g in range(G):
                    V.scalar_tensor_tensor(out=core.x[:, t * G + g, :], in0=ps_o[:, g * P:(g + 1) * P], scalar=rgate[:, g:g + 1],
                                           in1=core.x[:, t * G + g, :], op0=ALU.mult, op1=ALU.add).then_inc(s["x_ready"], 1)
                dve.wait_ge(s["x_ready"], t * G + G)
                for g in range(G):
                    dve.wait_ge(s["pad_in"], 16)
                    V.bn_stats(core.bn[:, t * G + g, :], core.x[:, t * G + g, :]).then_inc(s["summed"], 1)
            normalise(0)
            softmax(0)
            normalise(1)
            residual(0)
            with dve.Fori(1, NSTEP - 1) as t:
                softmax(t)
                normalise(t + 1)
                residual(t)
            softmax(NSTEP - 1)
            residual(NSTEP - 1)


def linear_attention(nc, core, name, gate, wq_dram, wkv_dram, null_kv, lnq_g, lnq_b, lno_g, lno_b, wout_dram):
    HD = 64
    H = 8
    I = H * HD
    J = I // P
    with Phase(nc, name) as ph:
        wq = ph.sb("wq", [P, I])
        wkv = ph.sb("wkv", [P, 2 * I])
        wout = ph.sb("wout", [P, J, D])
        w_out = ph.sb("w_out", [P, J, D])
        lq = ph.sb("lq", [P, 2, I])
        log = ph.sb("log", [P, J])
        lob = ph.sb("lob", [P, J])
        shift = ph.sb("shift", [1, D])
        nk = ph.sb("nk", [P, 1])
        nnk = ph.sb("nnk", [P, 1])
        nv = ph.sb("nv", [P, HD])
        half = ph.sb("half", [P, 1])
        xn = ph.sb("xn", [P, D])
        xnT = ph.sb("xnT", [P, P])
        cT = ph.sb("cT", [P, P])
        bn = ph.sb("bn", [P, 6])
        mv = ph.sb("mv", [P, 2])
        ve = ph.sb("ve", [P, 1])
        rs = ph.sb("rs", [P, 1])
        nmr = ph.sb("nmr", [P, 1])
        qn = ph.sb("qn", [P, I])
        qg = ph.sb("qg", [P, I])
        qb = ph.sb("qb", [P, H, HD])
        nmq = ph.sb("nmq", [P, H])
        pq = ph.sb("pq", [P, H, HD])
        sq = ph.sb("sq", [P, H])
        rq = ph.sb("rq", [P, H])
        nmk0 = ph.sb("nmk0", [P, J, 2])
        nmk = ph.sb("nmk", [P, J, 2])
        dn = ph.sb("dn", [P, J, 2])
        en = ph.sb("en", [P, J, 2])
        ek = ph.sb("ek", [P, J, 2, S])
        sk = ph.sb("sk", [P, J, 2])
        sk2 = ph.sb("sk2", [P, J, 2])
        rk = ph.sb("rk", [P, J, 2])
        kS = ph.sb("kS", [P, I])
        v = ph.sb("v", [P, I])
        nvt = ph.sb("nvt", [P, 2, J, HD])
        cmb = ph.sb("cmb", [P, 2, J, P])
        qT = ph.sb("qT", [P, J, 2, S])
        o1 = ph.sb("o1", [P, H, HD])
        bo = ph.sb("bo", [P, 6])
        mo = ph.sb("mo", [P, 2])
        vo = ph.sb("vo", [P, 1])
        ro = ph.sb("ro", [P, 1])
        on = ph.sb("on", [P, I])
        oT = ph.sb("oT", [P, I])
        ps_q, ps_k, ps_v, ps_o, ps_t = (ph.ps(n, [P, I]) for n in ("ps_q", "ps_k", "ps_v", "ps_o", "ps_t"))
        ps_cm = [ph.ps(f"ps_cm{b}", [P, J, P]) for b in range(2)]
        ps_y = ph.ps("ps_y", [P, D])[:, :]
        ps_x = ps_q[:, 0:P]
        s = {n: ph.sem(n) for n in (
            "w_in filled folded shift_ps shift_ready xn_ready xnT_ps xnT_ready cT_ready q_ps k_ps v_ps bn_ready mv_ready ve_ready "
            "rs_ready nmr_ready qn_ready qg_ready qb_ready mq_ready pq_ready rq_ready qT_ps qT_ready mk0_ready mk_ready nnk_ready "
            "dn_ready en_ready ek_ready sk_ready sk2_ready rk_ready kS_ps kS_ready v_ready nvt_ready cm_ps cmb_ready "
            "o_ps o1_ready bo_ready mo_ready vo_ready ro_ready on_ready oT_ps oT_ready y_ps x_ready summed").split()}
        root_on_scalar, root_on_vector = row_statistics(nc, ph, core)
        block = ph.ctx.enter_context(nc.Block())
        W_DMAS = 11

        def for_tile(part):
            def run(t):
                if not isinstance(t, int) or 0 <= t < NT:
                    part(t)
            return run

        def steps(eng, step):
            for i in range(-3, 4):
                step(i)
            with eng.Fori(2, NT // 2 - 2) as u:
                for k in range(2):
                    step(u * 2 + k)
            for i in range(NT - 4, NT + 1):
                step(i)

        @block.sync
        def _(sp):
            def load(dst, src):
                sp.dma_start(dst, src).then_inc(s["w_in"], 16)
            load(wq[:, :], wq_dram)
            load(wkv[:, :], wkv_dram)
            load(wout[:, :, :], wout_dram.rearrange("(j p) d -> p j d", p=P))
            load(lq[:, 0, :], lnq_g.rearrange("(a n) -> a n", a=1).broadcast_to([P, I]))
            load(lq[:, 1, :], lnq_b.rearrange("(a n) -> a n", a=1).broadcast_to([P, I]))
            load(log[:, :], lno_g)
            load(lob[:, :], lno_b)
            for b in range(2):
                load(nk[64 * b:64 * b + 64, :], null_kv[0:1, :].rearrange("a d -> d a"))
                load(nv[64 * b:64 * b + 64, :], null_kv[1:2, :].broadcast_to([64, HD]))

        @block.gpsimd
        def _(pool):
            pool.memset(half[:, :], -0.5).then_inc(s["filled"], 1)
            pool.memset(cmb[:, :, :, :], 0.0).then_inc(s["filled"], 1)
            pool.wait_ge(s["filled"], 2)
            pool.wait_ge(s["w_in"], 16 * W_DMAS)

            @for_tile
            def output_root(t):
                pool.wait_ge(s["vo_ready"], t + 1)
                reused(pool, s["on_ready"], t)
                pool.tensor_tensor(ro[:, :], vo[:, :], half[:, :], ALU.pow).then_inc(s["ro_ready"], 1)

            @for_tile
            def query_root(t):
                pool.wait_ge(s["ve_ready"], t + 1)
                reused(pool, s["qn_ready"], t)
                pool.tensor_tensor(rs[:, :], ve[:, :], half[:, :], ALU.pow).then_inc(s["rs_ready"], 1)

            @for_tile
            def query_norm(t):
                pool.wait_ge(s["qn_ready"], t + 1)
                pool.tensor_tensor(qg[:, :], qn[:, :], lq[:, 0, :], ALU.mult).then_inc(s["qg_ready"], 1)
                pool.wait_ge(s["qg_ready"], t + 1)
                reused(pool, s["pq_ready"], t)
                pool.tensor_tensor(qb[:, :, :].rearrange("p h d -> p (h d)"), qg[:, :], lq[:, 1, :], ALU.add).then_inc(s["qb_ready"], 1)

            @for_tile
            def null_values(t):
                pool.wait_ge(s["en_ready"], t + 1)
                reused(pool, s["cmb_ready"], 2 * t)
                pool.tensor_tensor(nvt[:, :, :, :], en[:, :, :].rearrange("p j b -> p b j").unsqueeze(3).broadcast_to([P, 2, J, HD]),
                                   nv[:, :].unsqueeze(1).unsqueeze(1).broadcast_to([P, 2, J, HD]), ALU.mult).then_inc(s["nvt_ready"], 1)

            @for_tile
            def context(t):
                reused(pool, s["v_ps"], t)
                pool.tensor_copy(cT[:, :], core.ctxT[:, bass.ts(t, P)]).then_inc(s["cT_ready"], 1)

            def step(i):
                query_root(i + 2)
                output_root(i)
                query_norm(i + 2)
                null_values(i + 2)
                context(i + 3)
            steps(pool, step)

        @block.tensor
        def _(pe):
            pe.wait_ge(s["w_in"], 16 * W_DMAS)
            for j in range(J):
                last = nc.tensor.matmul(ps_y[0:1, :], lob[:, j:j + 1], wout[:, j, :], start=(j == 0), stop=(j == J - 1))
            last.then_inc(s["shift_ps"], 1)
            pe.wait_ge(s["shift_ready"], 1)
            pe.wait_ge(s["folded"], 1)

            @for_tile
            def turn_x(t):
                pe.wait_ge(s["xn_ready"], t + 1)
                reused(pe, s["qn_ready"], t)
                nc.tensor.transpose(ps_x, xn[:, :], core.ident[:, :]).then_inc(s["xnT_ps"], 1)

            @for_tile
            def keys(t):
                pe.wait_ge(s["cT_ready"], t + 1)
                reused(pe, s["ek_ready"], t)
                for j in range(J):
                    last = nc.tensor.matmul(ps_k[:, j * P:(j + 1) * P], wkv[:, j * P:(j + 1) * P], cT[:, :], start=True, stop=True)
                last.then_inc(s["k_ps"], 1)

            @for_tile
            def queries(t):
                pe.wait_ge(s["xnT_ready"], t + 1)
                nc.tensor.matmul(ps_q[:, :], xnT[:, :], wq[:, :], start=True, stop=True).then_inc(s["q_ps"], 1)

            @for_tile
            def values(t):
                reused(pe, s["v_ready"], t)
                nc.tensor.matmul(ps_v[:, :], cT[:, :], wkv[:, I:2 * I], start=True, stop=True).then_inc(s["v_ps"], 1)

            @for_tile
            def turn_keys(t):
                pe.wait_ge(s["ek_ready"], t + 1)
                reused(pe, s["qT_ready"], t)
                for j in range(J):
                    last = nc.tensor.transpose(ps_t[:, j * P:(j + 1) * P], ek[:, j, :, :].rearrange("p b k -> p (b k)"), core.ident[:, :])
                last.then_inc(s["kS_ps"], 1)

            @for_tile
            def turn_outputs(t):
                pe.wait_ge(s["on_ready"], t + 1)
                reused(pe, s["kS_ready"], min(t + 3, NT) if isinstance(t, int) else t + 3)
                if isinstance(t, int):
                    reused(pe, s["qT_ready"], min(t + 2, NT))
                for j in range(J):
                    last = nc.tensor.transpose(ps_t[:, j * P:(j + 1) * P], on[:, j * P:(j + 1) * P], core.ident[:, :])
                last.then_inc(s["oT_ps"], 1)

            @for_tile
            def turn_queries(t):
                pe.wait_ge(s["pq_ready"], t + 1)
                pe.wait_ge(s["kS_ready"], t + 1)
                reused(pe, s["oT_ready"], t - 1)
                for j in range(J):
                    last = nc.tensor.transpose(ps_t[:, j * P:(j + 1) * P], pq[:, 2 * j:2 * j + 2, :].rearrange("p h d -> p (h d)"), core.ident[:, :])
                last.then_inc(s["qT_ps"], 1)

            @for_tile
            def keys_values(t):
                pe.wait_ge(s["kS_ready"], t + 1)
                pe.wait_ge(s["v_ready"], t + 1)
                reused(pe, s["cmb_ready"], 2 * t)
                for b in range(2):
                    rows = slice(64 * b, 64 * b + 64)
                    for j in range(J):
                        last = nc.tensor.matmul(ps_cm[b][:, j, :], kS[rows, j * P:(j + 1) * P], v[rows, j * P:(j + 1) * P], start=True, stop=True)
                last.then_inc(s["cm_ps"], 1)

            @for_tile
            def outputs(t):
                pe.wait_ge(s["qT_ready"], t + 1)
                pe.wait_ge(s["cmb_ready"], 2 * t + 2)
                reused(pe, s["o1_ready"], t)
                for j in range(J):
                    for b in range(2):
                        last = nc.tensor.matmul(ps_o[64 * b:64 * b + 64, j * P:(j + 1) * P], qT[:, j, b, :], cmb[:, b, j, :], start=True, stop=True)
                last.then_inc(s["o_ps"], 1)

            @for_tile
            def project_out(t):
                pe.wait_ge(s["oT_ready"], t + 1)
                reused(pe, s["x_ready"], t)
                for j in range(J):
                    nc.tensor.matmul(ps_y, oT[:, j * P:(j + 1) * P], w_out[:, j, :], start=(j == 0), stop=False)
                nc.tensor.matmul(ps_y, core.ones[:, :], shift[:, :], start=False, stop=True).then_inc(s["y_ps"], 1)

            def step(i):
                turn_x(i + 2)
                turn_keys(i + 1)
                queries(i + 2)
                turn_outputs(i - 1)
                outputs(i)
                keys(i + 2)
                keys_values(i + 1)
                values(i + 2)
                project_out(i - 1)
                turn_queries(i + 1)
            steps(pe, step)

        @block.scalar
        def _(act):
            root_on_scalar(act)
            nc.scalar.preload_act_table(ACT.Exp)

            @for_tile
            def turned_x(t):
                act.wait_ge(s["xnT_ps"], t + 1)
                reused(act, s["q_ps"], t)
                nc.scalar.copy(xnT[:, :], ps_x).then_inc(s["xnT_ready"], 1)

            @for_tile
            def turned_keys(t):
                act.wait_ge(s["kS_ps"], t + 1)
                reused(act, s["cm_ps"], t)
                nc.scalar.copy(kS[:, :], ps_t[:, :]).then_inc(s["kS_ready"], 1)

            @for_tile
            def turned_outputs(t):
                act.wait_ge(s["oT_ps"], t + 1)
                reused(act, s["y_ps"], t)
                nc.scalar.copy(oT[:, :], ps_t[:, :]).then_inc(s["oT_ready"], 1)

            @for_tile
            def values(t):
                act.wait_ge(s["v_ps"], t + 1)
                reused(act, s["cm_ps"], t)
                nc.scalar.copy(v[:, :], ps_v[:, :]).then_inc(s["v_ready"], 1)

            @for_tile
            def query_exponents(t):
                act.wait_ge(s["mq_ready"], t + 1)
                reused(act, s["qT_ps"], t)
                reused(act, s["rq_ready"], t)
                for h in range(H):
                    last = nc.scalar.activation(pq[:, h, :], qb[:, h, :], ACT.Exp, bias=nmq[:, h:h + 1], accum_out=sq[:, h:h + 1])
                last.then_inc(s["pq_ready"], 1)

            @for_tile
            def key_exponents(t):
                act.wait_ge(s["mk_ready"], t + 1)
                reused(act, s["kS_ps"], t)
                for j in range(J):
                    for b in range(2):
                        at = (2 * j + b) * S
                        last = nc.scalar.activation(ek[:, j, b, :], ps_k[:, at:at + S], ACT.Exp, bias=nmk[:, j, b:b + 1])
                last.then_inc(s["ek_ready"], 1)

            @for_tile
            def null_exponent(t):
                act.wait_ge(s["dn_ready"], t + 1)
                reused(act, s["nvt_ready"], t)
                nc.scalar.activation(en[:, :, :], dn[:, :, :], ACT.Exp).then_inc(s["en_ready"], 1)

            @for_tile
            def query_norm(t):
                act.wait_ge(s["nmr_ready"], t + 1)
                reused(act, s["qg_ready"], t)
                nc.scalar.activation(qn[:, :], ps_q[:, :], ACT.Identity, scale=rs[:, :], bias=nmr[:, :]).then_inc(s["qn_ready"], 1)

            def step(i):
                turned_x(i + 2)
                turned_keys(i + 1)
                turned_outputs(i - 1)
                query_exponents(i + 1)
                query_norm(i + 2)
                key_exponents(i + 2)
                null_exponent(i + 2)
                values(i + 2)
            steps(act, step)

        @block.vector
        def _(dve):
            V = nc.vector
            root_on_vector(dve)
            dve.wait_ge(s["w_in"], 16 * W_DMAS)
            V.tensor_tensor(w_out[:, :, :], wout[:, :, :], log[:, :].unsqueeze(2).broadcast_to([P, J, D]), ALU.mult).then_inc(s["folded"], 1)
            V.tensor_scalar(nnk[:, :], nk[:, :], -1.0, None, ALU.mult).then_inc(s["nnk_ready"], 1)
            dve.wait_ge(s["shift_ps"], 1)
            V.tensor_copy(shift[:, :], ps_y[0:1, :]).then_inc(s["shift_ready"], 1)
            dve.wait_ge(s["filled"], 2)
            dve.wait_ge(s["nnk_ready"], 1)

            @for_tile
            def normalise(t):
                reused(dve, s["xnT_ps"], t)
                V.tensor_scalar(xn[:, :], core.x[:, t, :], core.mean[:, bass.ts(t, 1)], core.rstd[:, bass.ts(t, 1)],
                                ALU.subtract, ALU.mult).then_inc(s["xn_ready"], 1)

            @for_tile
            def key_maximum(t):
                dve.wait_ge(s["k_ps"], t + 1)
                V.tensor_reduce(nmk0[:, :, :], ps_k[:, :].rearrange("p (j b k) -> p j b k", j=J, b=2), AX.X, ALU.max,
                                negate=True).then_inc(s["mk0_ready"], 1)

            @for_tile
            def null_maximum(t):
                dve.wait_ge(s["mk0_ready"], t + 1)
                reused(dve, s["ek_ready"], t)
                V.tensor_scalar(nmk[:, :, :], nmk0[:, :, :], nnk[:, :], None, ALU.min).then_inc(s["mk_ready"], 1)

            @for_tile
            def null_centred(t):
                dve.wait_ge(s["mk_ready"], t + 1)
                reused(dve, s["en_ready"], t)
                V.tensor_scalar(dn[:, :, :], nmk[:, :, :], nk[:, :], None, ALU.add).then_inc(s["dn_ready"], 1)

            @for_tile
            def query_moments(t):
                dve.wait_ge(s["q_ps"], t + 1)
                V.bn_stats(bn[:, :], ps_q[:, :]).then_inc(s["bn_ready"], 1)

            @for_tile
            def query_mean(t):
                dve.wait_ge(s["shift_ready"], 1)
                dve.wait_ge(s["bn_ready"], t + 1)
                V.bn_aggr(mv[:, :], bn[:, :]).then_inc(s["mv_ready"], 1)

            @for_tile
            def query_variance(t):
                dve.wait_ge(s["mv_ready"], t + 1)
                reused(dve, s["rs_ready"], t)
                V.tensor_scalar(ve[:, :], mv[:, 1:2], LN_EPS, None, ALU.add).then_inc(s["ve_ready"], 1)

            @for_tile
            def query_offset(t):
                dve.wait_ge(s["rs_ready"], t + 1)
                reused(dve, s["qn_ready"], t)
                V.scalar_tensor_tensor(out=nmr[:, :], in0=mv[:, 0:1], scalar=-1.0, in1=rs[:, :], op0=ALU.mult, op1=ALU.mult
                                       ).then_inc(s["nmr_ready"], 1)

            @for_tile
            def key_sums(t):
                dve.wait_ge(s["ek_ready"], t + 1)
                V.tensor_reduce(sk[:, :, :], ek[:, :, :, :], AX.X, ALU.add).then_inc(s["sk_ready"], 1)

            @for_tile
            def key_null_sums(t):
                dve.wait_ge(s["sk_ready"], t + 1)
                dve.wait_ge(s["en_ready"], t + 1)
                V.tensor_tensor(sk2[:, :, :], sk[:, :, :], en[:, :, :], ALU.add).then_inc(s["sk2_ready"], 1)

            @for_tile
            def key_denominators(t):
                dve.wait_ge(s["sk2_ready"], t + 1)
                V.reciprocal(rk[:, :, :], sk2[:, :, :]).then_inc(s["rk_ready"], 1)

            @for_tile
            def combined(t):
                dve.wait_ge(s["cm_ps"], t + 1)
                dve.wait_ge(s["nvt_ready"], t + 1)
                reused(dve, s["o_ps"], t)
                for b in range(2):
                    for h in range(2):
                        rows, cols = slice(64 * h, 64 * h + 64), slice(64 * h, 64 * h + 64)
                        last = V.tensor_tensor(cmb[rows, b, :, cols], ps_cm[b][rows, :, cols], nvt[rows, b, :, :], ALU.add)
                    last.then_inc(s["cmb_ready"], 1)

            @for_tile
            def query_maximum(t):
                dve.wait_ge(s["qb_ready"], t + 1)
                reused(dve, s["pq_ready"], t)
                V.tensor_reduce(nmq[:, :], qb[:, :, :], AX.X, ALU.max, negate=True).then_inc(s["mq_ready"], 1)

            @for_tile
            def turned_queries(t):
                dve.wait_ge(s["qT_ps"], t + 1)
                dve.wait_ge(s["rk_ready"], t + 1)
                reused(dve, s["o_ps"], t)
                V.tensor_tensor(qT[:, :, :, :], ps_t[:, :].rearrange("p (j b k) -> p j b k", j=J, b=2),
                                rk[:, :, :].unsqueeze(3).broadcast_to([P, J, 2, S]), ALU.mult).then_inc(s["qT_ready"], 1)

            @for_tile
            def query_denominators(t):
                dve.wait_ge(s["pq_ready"], t + 1)
                reused(dve, s["o1_ready"], t)
                V.reciprocal(rq[:, :], sq[:, :]).then_inc(s["rq_ready"], 1)

            @for_tile
            def outputs(t):
                dve.wait_ge(s["o_ps"], t + 1)
                dve.wait_ge(s["rq_ready"], t + 1)
                reused(dve, s["on_ready"], t)
                V.scalar_tensor_tensor(out=o1[:, :, :], in0=ps_o[:, :].rearrange("p (h d) -> p h d", h=H), scalar=8.0,
                                       in1=rq[:, :].unsqueeze(2).broadcast_to([P, H, HD]), op0=ALU.mult, op1=ALU.mult).then_inc(s["o1_ready"], 1)

            @for_tile
            def output_moments(t):
                dve.wait_ge(s["o1_ready"], t + 1)
                V.bn_stats(bo[:, :], o1[:, :, :].rearrange("p h d -> p (h d)")).then_inc(s["bo_ready"], 1)

            @for_tile
            def output_mean(t):
                dve.wait_ge(s["shift_ready"], 1)
                dve.wait_ge(s["bo_ready"], t + 1)
                V.bn_aggr(mo[:, :], bo[:, :]).then_inc(s["mo_ready"], 1)

            @for_tile
            def output_variance(t):
                dve.wait_ge(s["mo_ready"], t + 1)
                V.tensor_scalar(vo[:, :], mo[:, 1:2], LN_EPS, None, ALU.add).then_inc(s["vo_ready"], 1)

            @for_tile
            def output_norm(t):
                dve.wait_ge(s["ro_ready"], t + 1)
                reused(dve, s["oT_ps"], t)
                V.tensor_scalar(on[:, :], o1[:, :, :].rearrange("p h d -> p (h d)"), mo[:, 0:1], ro[:, :], ALU.subtract, ALU.mult
                                ).then_inc(s["on_ready"], 1)

            @for_tile
            def residual(t):
                dve.wait_ge(s["y_ps"], t + 1)
                V.scalar_tensor_tensor(out=core.x[:, t, :], in0=ps_y, scalar=core.gates[:, gate:gate + 1],
                                       in1=core.x[:, t, :], op0=ALU.mult, op1=ALU.add).then_inc(s["x_ready"], 1)

            @for_tile
            def summed(t):
                dve.wait_ge(s["shift_ready"], 1)
                dve.wait_ge(s["x_ready"], t + 1)
                V.bn_stats(core.bn[:, t, :], core.x[:, t, :]).then_inc(s["summed"], 1)

            def step(i):
                query_maximum(i + 1)
                query_moments(i + 2)
                normalise(i + 3)
                query_mean(i + 2)
                outputs(i)
                query_variance(i + 2)
                output_moments(i)
                key_maximum(i + 2)
                output_mean(i)
                null_maximum(i + 2)
                output_variance(i)
                query_offset(i + 2)
                null_centred(i + 2)
                combined(i + 1)
                output_norm(i)
                turned_queries(i + 1)
                query_denominators(i + 1)
                key_sums(i + 2)
                residual(i - 1)
                key_null_sums(i + 2)
                summed(i - 1)
                key_denominators(i + 2)
            steps(dve, step)


def later_layers(nc, core, a):
    with Phase(nc, "l0f") as ph:
        r = Routing(ph, core, "l0", 1, 16)
        route(nc, core, "l0r", r, 4, a["L0_ffn_Wg"], cap=T // 16)
        experts(nc, core, "l0e", r, 16, 1, a["L0_ffn_w1"], a["L0_ffn_w2"], ACT.Relu)
        combine(nc, core, "l0c", r)

    def neg_of_side(ph, neg, ready):
        pad = ph.sb("pad", [P, NT, S], U8)
        side = ph.sb("side_mask", [P, S])
        neg_in = ph.sem("neg_in")
        halved = ph.sem("halved")

        def dma(sp):
            for b in range(2):
                rows = slice(64 * b, 64 * b + 64)
                sp.dma_start(pad[rows, :, :].rearrange("p n k -> p (n k)"), a["mask_BxS2_bf0"][b:b + 1, :].broadcast_to([64, NT * S])
                             ).then_inc(neg_in, 16)
                sp.dma_start(side[rows, :], a["fside_SxS2_0"]).then_inc(neg_in, 16)

        def vector(dve):
            dve.wait_ge(neg_in, 64)
            nc.vector.tensor_scalar(side[:, :], side[:, :], 0.5, None, ALU.mult).then_inc(halved, 1)
            dve.wait_ge(halved, 1)
            nc.vector.scalar_tensor_tensor(out=neg[:, :, :], in0=pad[:, :, :], scalar=MASKED / 2,
                                           in1=side[:, :].unsqueeze(1).broadcast_to([P, NT, S]),
                                           op0=ALU.mult, op1=ALU.add).then_inc(ready, 1)
            dve.wait_ge(ready, 1)
        return dma, vector

    attention16(nc, core, "l1a", 1, [a[f"L1_xattn_W{c}"] for c in "qkvo"], [a[f"L1_xattn_b{c}"] for c in "qkvo"],
                neg_of_side, side=a["fside_Bx16xSxS2_0"], fills=[core.tables["l2", "in"]])

    ternary_ffn(nc, core, "l1f", 5, a["L1_ffn_W_fc"], a["L1_ffn_W_proj"], a["L1_ffn_ln_w"], a["L1_ffn_ln_b"])
    attention1(nc, core, "l2a", 2, a["L2_xattn_W"], a["L2_xattn_b"], a["ctx_1024"], a["mask_BxS2_bf0"])
    with Phase(nc, "l2f") as ph:
        r = Routing(ph, core, "l2", 2, 8)
        route(nc, core, "l2r", r, None, a["L2_ffn_gate_w"], cap=None, bg_dram=a["L2_ffn_gate_b"], temp=0.9)
        experts(nc, core, "l2e", r, MAX_SLOTS // CHUNK, 1, a["L2_ffn_w1"], a["L2_ffn_w2"], ACT.Gelu,
                b1_dram=a["L2_ffn_b1"], b2_dram=a["L2_ffn_b2"], dynamic=True)
        combine(nc, core, "l2c", r, norm=(a["L2_ffn_ln_g"], a["L2_ffn_ln_b"]), gate=6)

    linear_attention(nc, core, "l3a", 3, a["L3_xattn_Wq"], a["L3_xattn_Wkv"], a["L3_xattn_null_kv"], a["L3_xattn_ln_q_g"],
                     a["L3_xattn_ln_q_b"], a["L3_xattn_ln_out_g"], a["L3_xattn_ln_out_b"], a["L3_xattn_Wout"])
    with Phase(nc, "l3f") as ph:
        r = Routing(ph, core, "l3", 2, 8)
        route(nc, core, "l3r", r, 7, a["L3_ffn_Wr"], cap=-(-T * 2 * 5 // (8 * 4)), sum_eps=1e-12, clamp=1e4)
        experts(nc, core, "l3e", r, 8, MAX_SLOTS // CHUNK // 8, a["L3_ffn_W1"], a["L3_ffn_W2"], ACT.Silu, w3_dram=a["L3_ffn_W3"])
        combine(nc, core, "l3c", r)


LAYOUT = {
    "fside_Bx16xSxS2_0": lambda a: a.transpose(0, 2, 1, 3),
    "mask_BxS2_bf0": lambda a: a.reshape(-1, 2, a.shape[1]).transpose(1, 0, 2).reshape(2, -1),
    "L1_xattn_Wq": lambda a: a.T,
    "L1_xattn_Wk": lambda a: a.T,
    "L1_xattn_Wv": lambda a: a.T,
    "L1_xattn_Wo": lambda a: a.T,
    "L1_ffn_W_fc": lambda a: a.T,
    "L1_ffn_W_proj": lambda a: a.T,
    "L1_ffn_ln_w": lambda a: a.reshape(-1, P).T,
    "L1_ffn_ln_b": lambda a: a.reshape(-1, P).T,
    "L2_xattn_W": lambda a: a.T,
    "L3_xattn_ln_out_g": lambda a: a.reshape(-1, P).T,
    "L3_xattn_ln_out_b": lambda a: a.reshape(-1, P).T,
    "L2_ffn_b1": lambda a: a.reshape(a.shape[0], -1, P).transpose(0, 2, 1),
    "L2_ffn_b2": lambda a: a.reshape(a.shape[0], 1, -1),
}


def kernel(**inputs):
    import numpy as _np
    import concourse.bacc as _bacc
    from concourse import mybir as _mybir
    from concourse.bass_utils import run_bass_kernel_spmd as _run

    nc = _bacc.Bacc("TRN2", target_bir_lowering=False, num_devices=1)
    arrays, aps = {}, {}
    for name, a in inputs.items():
        a = _np.asarray(a)
        if name in LAYOUT:
            a = LAYOUT[name](a)
        a = _np.ascontiguousarray(a)
        arrays[f"in_{name}"] = a
        aps[name] = nc.dram_tensor(f"in_{name}", a.shape, _mybir.dt.from_np(a.dtype), kind="ExternalInput").ap()
    out = nc.dram_tensor("out_x", (B, S, D), _mybir.dt.float32, kind="ExternalOutput").ap()
    build(nc, aps, out)
    r = _run(nc, [arrays], core_ids=[0])
    return r.results[0]["out_x"]
```
